# Optimizing a Trainium2 kernel written in Bass

```python
import numpy as np
import jax
import jax.numpy as jnp

def _softmax(x, axis=-1):
    return jax.nn.softmax(x, axis=axis)

def _gelu(x):
    return jax.nn.gelu(x, approximate=True)

def _silu(x):
    return jax.nn.silu(x)

def _sigmoid(x):
    return jax.nn.sigmoid(x)

def _layernorm(x, axis=-1, eps=1e-05):
    m = jnp.mean(x, axis=axis, keepdims=True)
    v = jnp.var(x, axis=axis, keepdims=True)
    return (x - m) / jnp.sqrt(v + eps)

def _scatter_add(tgt, idx, src, axis=0):
    return tgt.at[idx].add(src)

def _segment_sum(src, seg, n):
    return jax.ops.segment_sum(src, seg, n)
kernel_name = 'mk_adaln_ffn_d1_seqx_r2_c69563'

def setup_inputs(seed: int=0):
    np.random.seed(seed)
    _w = jnp.asarray

    def _rec_inputs():
        import jax
        import jax.numpy as jnp
        _rk = jax.random.key(seed)
        x = -8.015e-05 + 0.9999 * jax.random.normal(jax.random.fold_in(_rk, 1), (8, 512, 1024), jnp.float32)
        _lenS = 512 - jax.random.randint(jax.random.fold_in(_rk, 7), (8,), 0, max(1, 512 // 4) + 1, jnp.int32)
        _lenS2 = 512 - jax.random.randint(jax.random.fold_in(_rk, 8), (8,), 0, max(1, 512 // 4) + 1, jnp.int32)
        cond_1024 = 0.00191187 + 0.999416 * jax.random.normal(jax.random.fold_in(_rk, 11), (8, 512), jnp.float32)
        return (x, cond_1024)
    x, cond_1024 = _rec_inputs()

    def _L0_cond_setup():
        import jax, jax.numpy as jnp
        import numpy as np
        B, N, V_DIM, Q_DIM = (128, 100, 1024, 512)
        key = jax.random.key(seed)
        k1, k2, k3, k4 = jax.random.split(key, 4)
        v = jax.random.normal(k1, (B, N, V_DIM), dtype=jnp.float32)
        q = jax.random.normal(k2, (B, Q_DIM), dtype=jnp.float32)
        W3 = jax.random.normal(k3, (Q_DIM, V_DIM), dtype=jnp.float32) * (1.0 / np.sqrt(Q_DIM))
        b3 = jnp.zeros((V_DIM,), dtype=jnp.float32)
        W2 = jax.random.normal(k4, (V_DIM, V_DIM), dtype=jnp.float32) * (1.0 / np.sqrt(V_DIM))
        b2 = jnp.zeros((V_DIM,), dtype=jnp.float32)
        return {'v': v, 'q': q, 'W3': W3, 'b3': b3, 'W2': W2, 'b2': b2}
    _L0_cond_all = _L0_cond_setup()
    _L0_cond_in = {k: v for k, v in _L0_cond_all.items() if k in ('W3', 'b3', 'W2', 'b2')}
    del _L0_cond_all

    def _L0_ffn_setup():
        import jax, jax.numpy as jnp
        import numpy as np
        CAPACITY = 0.125
        HEAD_DIM = 128
        N_HEADS = 16
        N_KV_HEADS = 8
        ROPE_THETA = 10000.0
        EPS = 1e-06

        def _rms_norm(x, w):
            return x * jax.lax.rsqrt(jnp.mean(x * x, axis=-1, keepdims=True) + EPS) * w

        def _rotate_half(t):
            h = t.shape[-1] // 2
            return jnp.concatenate([-t[..., h:], t[..., :h]], axis=-1)
        key = jax.random.key(seed)
        ks = jax.random.split(key, 12)
        B, T, D = (4, 2048, 1024)
        I = 4096
        s = 0.02
        return {'hidden_states': jax.random.normal(ks[0], (B, T, D), jnp.float32), 'w_router': jax.random.normal(ks[1], (D,), jnp.float32) * s, 'wq': jax.random.normal(ks[2], (D, N_HEADS * HEAD_DIM), jnp.float32) * s, 'bq': jnp.zeros((N_HEADS * HEAD_DIM,), jnp.float32), 'wk': jax.random.normal(ks[3], (D, N_KV_HEADS * HEAD_DIM), jnp.float32) * s, 'bk': jnp.zeros((N_KV_HEADS * HEAD_DIM,), jnp.float32), 'wv': jax.random.normal(ks[4], (D, N_KV_HEADS * HEAD_DIM), jnp.float32) * s, 'bv': jnp.zeros((N_KV_HEADS * HEAD_DIM,), jnp.float32), 'wo': jax.random.normal(ks[5], (N_HEADS * HEAD_DIM, D), jnp.float32) * s, 'w_gate': jax.random.normal(ks[6], (D, I), jnp.float32) * s, 'w_up': jax.random.normal(ks[7], (D, I), jnp.float32) * s, 'w_down': jax.random.normal(ks[8], (I, D), jnp.float32) * s, 'ln1_w': jnp.ones((D,), jnp.float32), 'ln2_w': jnp.ones((D,), jnp.float32)}
    _L0_ffn_all = _L0_ffn_setup()
    _L0_ffn_in = {k: v for k, v in _L0_ffn_all.items() if k in ('w_router', 'wq', 'bq', 'wk', 'bk', 'wv', 'bv', 'wo', 'w_gate', 'w_up', 'w_down', 'ln1_w', 'ln2_w')}
    del _L0_ffn_all
    return {'x': x, 'cond_1024': cond_1024, 'L0_cond_W3': _L0_cond_in['W3'], 'L0_cond_b3': _L0_cond_in['b3'], 'L0_cond_W2': _L0_cond_in['W2'], 'L0_cond_b2': _L0_cond_in['b2'], 'L0_ffn_w_router': _L0_ffn_in['w_router'], 'L0_ffn_wq': _L0_ffn_in['wq'], 'L0_ffn_bq': _L0_ffn_in['bq'], 'L0_ffn_wk': _L0_ffn_in['wk'], 'L0_ffn_bk': _L0_ffn_in['bk'], 'L0_ffn_wv': _L0_ffn_in['wv'], 'L0_ffn_bv': _L0_ffn_in['bv'], 'L0_ffn_wo': _L0_ffn_in['wo'], 'L0_ffn_w_gate': _L0_ffn_in['w_gate'], 'L0_ffn_w_up': _L0_ffn_in['w_up'], 'L0_ffn_w_down': _L0_ffn_in['w_down'], 'L0_ffn_ln1_w': _L0_ffn_in['ln1_w'], 'L0_ffn_ln2_w': _L0_ffn_in['ln2_w']}

def reference(x, cond_1024, L0_cond_W3, L0_cond_b3, L0_cond_W2, L0_cond_b2, L0_ffn_w_router, L0_ffn_wq, L0_ffn_bq, L0_ffn_wk, L0_ffn_bk, L0_ffn_wv, L0_ffn_bv, L0_ffn_wo, L0_ffn_w_gate, L0_ffn_w_up, L0_ffn_w_down, L0_ffn_ln1_w, L0_ffn_ln2_w):
    import jax
    import jax.numpy as jnp

    def _L0_cond_ref(v, q, W3, b3, W2, b2):
        import jax, jax.numpy as jnp
        import numpy as np
        B, N, V_DIM, Q_DIM = (128, 100, 1024, 512)
        q_emb = jax.nn.relu(q @ W3 + b3)
        n = v.shape[1]
        v_sum = jnp.sum(v, axis=1, keepdims=True)
        x = (n * v + v_sum) * q_emb[:, None, :]
        return jax.nn.relu(x @ W2 + b2)

    def _L0_ffn_ref(hidden_states, w_router, wq, bq, wk, bk, wv, bv, wo, w_gate, w_up, w_down, ln1_w, ln2_w):
        import jax, jax.numpy as jnp
        import numpy as np
        CAPACITY = 0.125
        HEAD_DIM = 128
        N_HEADS = 16
        N_KV_HEADS = 8
        ROPE_THETA = 10000.0
        EPS = 1e-06

        def _rms_norm(x, w):
            return x * jax.lax.rsqrt(jnp.mean(x * x, axis=-1, keepdims=True) + EPS) * w

        def _rotate_half(t):
            h = t.shape[-1] // 2
            return jnp.concatenate([-t[..., h:], t[..., :h]], axis=-1)
        B, T, D = hidden_states.shape
        k = max(1, int(T * CAPACITY))
        scores = jnp.einsum('btd,d->bt', hidden_states, w_router)
        _, idx = jax.lax.top_k(scores, k)
        idx = jnp.sort(idx, axis=-1)
        b = jnp.arange(B)[:, None]
        sel = hidden_states[b, idx]
        sel_scores = scores[b, idx]
        S = B * k
        x = sel.reshape(S, D)
        pos = idx.reshape(S)
        inv_freq = 1.0 / ROPE_THETA ** (jnp.arange(0, HEAD_DIM, 2, dtype=jnp.float32) / HEAD_DIM)
        ang = pos.astype(jnp.float32)[:, None] * inv_freq
        cos = jnp.concatenate([jnp.cos(ang), jnp.cos(ang)], axis=-1)[:, None, :]
        sin = jnp.concatenate([jnp.sin(ang), jnp.sin(ang)], axis=-1)[:, None, :]
        h = _rms_norm(x, ln1_w)
        q = (h @ wq + bq).reshape(S, N_HEADS, HEAD_DIM)
        kk = (h @ wk + bk).reshape(S, N_KV_HEADS, HEAD_DIM)
        v = (h @ wv + bv).reshape(S, N_KV_HEADS, HEAD_DIM)
        q = q * cos + _rotate_half(q) * sin
        kk = kk * cos + _rotate_half(kk) * sin
        rep = N_HEADS // N_KV_HEADS
        kk = jnp.repeat(kk, rep, axis=1)
        v = jnp.repeat(v, rep, axis=1)
        att = jnp.einsum('shd,thd->hst', q, kk) / np.sqrt(HEAD_DIM)
        causal = jnp.tril(jnp.ones((S, S), bool))
        att = jnp.where(causal[None], att, jnp.finfo(att.dtype).min)
        att = jax.nn.softmax(att, axis=-1)
        attn_out = jnp.einsum('hst,thd->shd', att, v).reshape(S, N_HEADS * HEAD_DIM) @ wo
        x1 = x + attn_out
        h2 = _rms_norm(x1, ln2_w)
        mlp = jax.nn.silu(h2 @ w_gate) * (h2 @ w_up) @ w_down
        processed = x1 + mlp
        gate = jax.nn.sigmoid(sel_scores).reshape(S, 1)
        gated = gate * processed + (1.0 - gate) * x
        output = hidden_states.at[b, idx].set(gated.reshape(B, k, D))
        return output
    x = x + _L0_ffn_ref(_L0_cond_ref(x, cond_1024, L0_cond_W3, L0_cond_b3, L0_cond_W2, L0_cond_b2), L0_ffn_w_router, L0_ffn_wq, L0_ffn_bq, L0_ffn_wk, L0_ffn_bk, L0_ffn_wv, L0_ffn_bv, L0_ffn_wo, L0_ffn_w_gate, L0_ffn_w_up, L0_ffn_w_down, L0_ffn_ln1_w, L0_ffn_ln2_w)
    return x

_drawn_inputs = setup_inputs


def setup_inputs(seed=0):
    import zlib

    import numpy as np

    out = dict(_drawn_inputs(seed))
    spreads = {'L0_cond_b3': (0.0, 0.1),
     'L0_cond_b2': (0.0, 2.0),
     'L0_ffn_bq': (0.0, 0.8),
     'L0_ffn_bk': (0.0, 0.8),
     'L0_ffn_bv': (0.0, 2.0),
     'L0_ffn_ln1_w': (1.0, 0.6),
     'L0_ffn_ln2_w': (1.0, 0.6)}
    factors = {'L0_ffn_w_router': 8.0,
     'L0_ffn_wq': 8.0,
     'L0_ffn_wk': 8.0,
     'L0_ffn_wv': 8.0,
     'L0_ffn_wo': 8.0,
     'L0_ffn_w_gate': 8.0,
     'L0_ffn_w_up': 8.0,
     'L0_ffn_w_down': 8.0}
    for name, (base, spread) in spreads.items():
        noise = np.random.default_rng([zlib.crc32(name.encode()), seed]).standard_normal(out[name].shape)
        drawn = base * np.exp(spread * noise) if base else spread * noise
        out[name] = jnp.asarray(drawn.astype(out[name].dtype))
    for name, factor in factors.items():
        out[name] = (out[name] * factor).astype(out[name].dtype)
    return out
```

```python
from contextlib import ExitStack

import numpy as np

import concourse.bass as bass
from concourse import mybir

P = 128
BATCH, SEQ, D = 8, 512, 1024
COND = 512
HEADS, KV_HEADS, HD = 16, 8, 128
FF = 4096
PICK = 64
S = BATCH * PICK
KC = D // P
TT = SEQ // P
ST = S // P
FT = FF // P
EPS = 1e-6
SCALE = 1.0 / float(np.sqrt(np.float32(HD)))
LOWEST = -3.0e38

W_V = KC
W_QK = W_V + KC
W_O = W_QK + HEADS + KV_HEADS
W_GU = W_O + HEADS
W_DOWN = W_GU + 2 * FT
W_END = W_DOWN + FT

C_B3, C_LN1, C_LN2 = 0, KC, 2 * KC
C_BQK = 3 * KC
C_BQKS = C_BQK + HEADS + KV_HEADS
N_COLS = C_BQKS + HEADS + KV_HEADS
Z_IDENT, Z_MASK, Z_PAIR, Z_RANK, Z_BASE = 0, P, 2 * P, 3 * P, 3 * P + 1
Z_YBASE = Z_BASE + ST
N_CONSTS = Z_YBASE + ST


def after(engine, sem, n):
    if isinstance(n, int) and n <= 0:
        return
    engine.wait_ge(sem, n)


def apart(engine, sem, n, passed):
    engine.wait_ge(sem, n)
    engine.sem_inc(passed, 1)


def build(nc, x_t, x_rows, cond_t, w3, wstream, cols, rows, shape_consts, angles, out):
    f32, f32r, bf16, u32 = mybir.dt.float32, mybir.dt.float32r, mybir.dt.bfloat16, mybir.dt.uint32
    ALU, ACT, AX = mybir.AluOpType, mybir.ActivationFunctionType, mybir.AxisListType.X

    PAIR = 2 * SEQ
    y_first = nc.dram_tensor("y_first", [PAIR, D], f32).ap()
    y_middle = nc.dram_tensor("y_middle", [2 * PAIR, D], f32).ap()
    y_last = nc.dram_tensor("y_last", [PAIR, D], f32).ap()
    y_of = [y_first, y_middle, y_middle, y_last]
    base_rows = nc.dram_tensor("base_rows", [S, D], f32).ap()

    ctx = ExitStack()
    with ctx:
        K = 256
        plain = ctx.enter_context(nc.sbuf_tensor("plain", [P, 76 * K], f32))
        split = ctx.enter_context(nc.sbuf_tensor("split", [P, 128 * K], f32r))
        ident_r = ctx.enter_context(nc.sbuf_tensor("ident_r", [P, P], f32r))
        mask_r = ctx.enter_context(nc.sbuf_tensor("mask_r", [P, P], f32r))
        consts = ctx.enter_context(nc.sbuf_tensor("consts", [P, N_CONSTS], f32))
        col = ctx.enter_context(nc.sbuf_tensor("col", [P, N_COLS], f32))
        small = ctx.enter_context(nc.sbuf_tensor("small", [P, 208], f32))
        idx = ctx.enter_context(nc.sbuf_tensor("idx", [P, 3 * ST], u32))
        psum = ctx.enter_context(nc.psum_tensor("psum", [P, 8, 512], f32))

        def kib(a, b):
            return plain[:, a * K:b * K]

        def skib(a, b):
            return split[:, int(a * K):int(b * K)]

        xT = kib(0, 8).rearrange("p (s n) -> p s n", s=4)
        xrow = kib(8, 24).rearrange("p (s n) -> p s n", s=TT)
        y = kib(24, 32).rearrange("p (s n) -> p s n", s=2)
        w3_sb = kib(32, 48).rearrange("p (k n) -> p k n", k=COND // P)
        ysel = kib(32, 40).rearrange("p (s n) -> p s n", s=2)
        hs = kib(40, 44)
        rank_a, rank_b = plain[:, 40 * K:42 * K], plain[:, 42 * K:44 * K]
        hfull = kib(44, 48).rearrange("p (k n) -> p k n", k=KC)
        bias_row = kib(48, 52)
        wr_row = kib(52, 56)
        cosT, sinT = kib(56, 58), kib(58, 60)
        junk = kib(60, 62).bitcast(bf16)
        junk_sum = kib(62, 63).bitcast(bf16)
        ang = kib(63, 64)
        raw = kib(64, 76).rearrange("p (s n) -> p s n", s=3)
        prob = kib(0, 8).rearrange("p (i n) -> p i n", i=ST)
        V = kib(8, 24).rearrange("p (i n) -> p i n", i=ST)
        attn = kib(24, 56).rearrange("p (h n) -> p h n", h=HEADS)
        rope = kib(60, 64).rearrange("p (s n) -> p s n", s=2)
        ysel4 = [kib(0, 4), kib(4, 8), kib(48, 52), kib(52, 56)]
        x1 = kib(8, 24).rearrange("p (i n) -> p i n", i=ST)
        h2s = kib(24, 28)
        h2full = kib(28, 32).rearrange("p (k n) -> p k n", k=KC)
        xsel = kib(32, 48).rearrange("p (i n) -> p i n", i=ST)
        m = kib(0, 64).rearrange("p (f n) -> p f n", f=FT)
        silu_g = kib(72, 76).rearrange("p (s n) -> p s n", s=2)
        base = kib(0, 16).rearrange("p (i n) -> p i n", i=ST)

        w8 = skib(0, 64).rearrange("p (s q n) -> p s q n", s=KC, q=2)
        xx = skib(64, 128).rearrange("p (b k q n) -> p b k q n", b=2, k=KC, q=2)
        hT = skib(64, 96).rearrange("p (k q n) -> p k q n", k=KC, q=2)
        w4 = skib(96, 128).rearrange("p (s q n) -> p s q n", s=4, q=2)
        k_hl = skib(0, 4).rearrange("p (q n) -> p q n", q=2)
        q_hl = skib(4, 8).rearrange("p (q n) -> p q n", q=2)
        v_hl = skib(8, 12).rearrange("p (q i n) -> p q i n", q=2, i=ST)
        pT = skib(12, 28).rearrange("p (j q n) -> p j q n", j=ST, q=2)
        attn_hl = skib(56, 64).rearrange("p (s q n) -> p s q n", s=2, q=2)
        m_hl = skib(0, 8).rearrange("p (s q n) -> p s q n", s=2, q=2)

        ident = consts[:, Z_IDENT:Z_IDENT + P]
        qe = small[:, 0:KC * BATCH].rearrange("p (k b) -> p k b", b=BATCH)
        vs = small[:, 64:80].rearrange("p (b k) -> p b k", b=2)
        sc = small[:, 80:88].rearrange("p (j b) -> p j b", b=2)
        top8 = small[:, 112:120]
        idxf = small[:, 120:124]
        ssq, rt, rs, na = small[:, 124:128], small[:, 128:132], small[:, 132:136], small[:, 136:140]
        sels = small[:, 140:144]
        mx, nmx = small[:, 144:148], small[:, 148:152]
        lsum, rl = small[:, 152:156], small[:, 156:160]
        gate, ungate = small[:, 160:164], small[:, 164:168]
        ms = small[:, 168:172]
        condT = small[:, 176:208].rearrange("p (k b) -> p k b", b=BATCH)

        def sem(name):
            return ctx.enter_context(nc.semaphore(name))

        d_consts, d_cols, d_cond, d_w3, d_b2, d_wr, d_bv = (sem(n) for n in (
            "d_consts", "d_cols", "d_cond", "d_w3", "d_b2", "d_wr", "d_bv"))
        d_xT = [sem(f"d_xT{s}") for s in range(4)]
        d_x = [sem(f"d_x{s}") for s in range(TT)]
        d_y = [sem(f"d_y{s}") for s in range(2)]
        d_out = [sem(f"d_out{s}") for s in range(TT)]
        d_raw2 = [sem(f"d_raw2_{s}") for s in range(2)]
        d_raw3 = [sem(f"d_raw3_{s}") for s in range(3)]
        d_raw = [sem(f"d_raw{s}") for s in range(2)]
        d_ysel = [sem(f"d_ysel{s}") for s in range(ST)]
        d_ang = [sem(f"d_ang{s}") for s in range(ST)]
        d_ysel4 = [sem(f"d_ysel4_{s}") for s in range(ST)]
        d_xsel = [sem(f"d_xsel{s}") for s in range(ST)]
        d_base = sem("d_base")
        d_baseld = [sem(f"d_baseld{s}") for s in range(ST)]
        d_fin = sem("d_fin")
        dve_passed, pool_passed = sem("dve_passed"), sem("pool_passed")
        qe_mm, qe_b, qe_done = sem("qe_mm"), sem("qe_b"), sem("qe_done")
        const_r = sem("const_r")
        x_sum, x_mod, x_hi, x_lo = sem("x_sum"), sem("x_mod"), sem("x_hi"), sem("x_lo")
        w_hi, w_lo = sem("w_hi"), sem("w_lo")
        w2_used, wv_used, w_used = sem("w2_used"), sem("wv_used"), sem("w_used")
        y_mm, y_biased, y_relu, y_score, out_row = (sem(n) for n in (
            "y_mm", "y_biased", "y_relu", "y_score", "out_row"))
        score_T, top_max, top_cut, top_mask, top_rank, rank_bc = (sem(n) for n in (
            "score_T", "top_max", "top_cut", "top_mask", "top_rank", "rank_bc"))
        idx_f, idx_u = sem("idx_f"), sem("idx_u")
        h_sq, h_ms, h_rt, h_chain, h_rs, h_sel, h_norm = (sem(n) for n in (
            "h_sq", "h_ms", "h_rt", "h_chain", "h_rs", "h_sel", "h_norm"))
        h_T, h_full, h_hi, h_lo, ang_T, ang_sb = (sem(n) for n in (
            "h_T", "h_full", "h_hi", "h_lo", "ang_T", "ang_sb"))
        v_mm, v_sb, v_hi, v_lo = sem("v_mm"), sem("v_sb"), sem("v_hi"), sem("v_lo")
        qk_mm, rope_c, rope_s, rope_sum, qk_hi, qk_lo = (sem(n) for n in (
            "qk_mm", "rope_c", "rope_s", "rope_sum", "qk_hi", "qk_lo"))
        s_mm, s_max, s_nmax, s_exp, s_rl, s_prob = (sem(n) for n in (
            "s_mm", "s_max", "s_nmax", "s_exp", "s_rl", "s_prob"))
        p_T, p_hi, p_lo, pv_mm, o_sb = sem("p_T"), sem("p_hi"), sem("p_lo"), sem("pv_mm"), sem("o_sb")
        a_hi, a_lo, wo_mm, x1_sb = sem("a_hi"), sem("a_lo"), sem("wo_mm"), sem("x1_sb")
        g_sig, g_un, g_mix, g_base = sem("g_sig"), sem("g_un"), sem("g_mix"), sem("g_base")
        n_sq, n_ms, n_rt, n_chain, n_rs, n_norm = (sem(n) for n in (
            "n_sq", "n_ms", "n_rt", "n_chain", "n_rs", "n_norm"))
        n_T, n_full, n_hi, n_lo = sem("n_T"), sem("n_full"), sem("n_hi"), sem("n_lo")
        g_silu, m_sb, m_hi, m_lo, dn_mm, fin = (sem(n) for n in (
            "g_silu", "m_sb", "m_hi", "m_lo", "dn_mm", "fin"))

        def bank(b, n=512):
            return psum[:, b, 0:n]

        def pair(b):
            return psum[:, b:b + 2, :].rearrange("p b n -> p (b n)")

        def as_f32(ap):
            return ap.bitcast(f32)

        block = ctx.enter_context(nc.Block())

        @block.sync
        def _(sp):
            def load_w(n, slot, slot_sem):
                sp.dma_start(raw[:, slot, :], wstream[n]).then_inc(slot_sem, 16)

            def load_xT(b, kc):
                c = b * KC + kc
                after(sp, x_lo, c - 3)
                sp.dma_start(xT[:, kc % 4, :], x_t[c]).then_inc(d_xT[kc % 4], 16)

            def load_x(b, j):
                sp.dma_start(xrow[:, j, :], x_rows[bass.ds((b * TT + j) * P, P), :]).then_inc(d_x[j], 16)

            sp.dma_start(condT, cond_t).then_inc(d_cond, 16)
            sp.dma_start(col[:], cols).then_inc(d_cols, 16)
            sp.dma_start(w3_sb, w3.rearrange("(k p) n -> p k n", p=P)).then_inc(d_w3, 16)
            for kc in range(4):
                load_xT(0, kc)
            load_w(0, 0, d_raw2[0])
            load_w(1, 1, d_raw2[1])
            sp.dma_start(consts[:], shape_consts).then_inc(d_consts, 16)
            for n in range(2, KC):
                if n < 6:
                    load_xT(0, n + 2)
                sp.wait_ge(w_hi, n - 1)
                sp.wait_ge(w_lo, n - 1)
                load_w(n, n % 2, d_raw2[n % 2])
            sp.dma_start(bias_row, rows[0:1, :].broadcast_to([P, D])).then_inc(d_b2, 16)
            sp.dma_start(wr_row, rows[1:2, :].broadcast_to([P, D])).then_inc(d_wr, 16)
            for j in range(TT):
                load_x(0, j)

            def window(b, last=False):
                if not last:
                    for kc in range(KC):
                        load_xT(b + 1, kc)
                for j in range(TT):
                    t = b * TT + j
                    sp.wait_ge(out_row, t + 1)
                    sp.dma_start(out[bass.ds(t * P, P), :], xrow[:, j, :]).then_inc(d_out[j], 16)
                    if not last and j >= 1:
                        sp.wait_ge(d_out[j - 1], 16 * b + 16)
                        load_x(b + 1, j - 1)
                if not last:
                    sp.wait_ge(d_out[TT - 1], 16 * b + 16)
                    load_x(b + 1, TT - 1)

            window(0)
            with sp.Fori(1, BATCH - 1) as b:
                window(b)
            for n in range(W_V, W_V + 2):
                sp.wait_ge(w_hi, n - 1)
                sp.wait_ge(w_lo, n - 1)
                load_w(n, n % 2, d_raw2[n % 2])
            window(BATCH - 1, last=True)
            sp.wait_ge(y_biased, BATCH * TT)
            sp.dma_start(bias_row, rows[2:3, :].broadcast_to([P, D])).then_inc(d_bv, 16)
            for n in range(W_V + 2, W_QK):
                sp.wait_ge(w_hi, n - 1)
                sp.wait_ge(w_lo, n - 1)
                load_w(n, n % 2, d_raw2[n % 2])
            for u, need in ((0, W_QK - 1), (1, W_QK), (2, 0)):
                after(sp, w_hi, need)
                after(sp, w_lo, need)
                load_w(W_QK + u, u, d_raw3[u])
            with sp.Fori(1, KV_HEADS) as g:
                for u in range(3):
                    sp.wait_ge(w_hi, W_QK + 3 * (g - 1) + u + 1)
                    sp.wait_ge(w_lo, W_QK + 3 * (g - 1) + u + 1)
                    load_w(W_QK + 3 * g + u, u, d_raw3[u])
            for s in range(2):
                sp.wait_ge(w_hi, W_O - 2 + s)
                sp.wait_ge(w_lo, W_O - 2 + s)
                load_w(W_O + s, s, d_raw[s])
            with sp.Fori(1, (W_END - W_O) // 2) as k:
                for s in range(2):
                    sp.wait_ge(w_hi, W_O + 2 * k + s - 1)
                    sp.wait_ge(w_lo, W_O + 2 * k + s - 1)
                    load_w(W_O + 2 * k + s, s, d_raw[s])
            for j in range(TT):
                sp.wait_ge(d_out[j], 16 * BATCH)
            sp.wait_ge(d_fin, 16 * ST)

        @block.tensor
        def _(pe):
            def three(out_ap, w_hl, x_hl, start, stop):
                nc.tensor.matmul(out_ap, w_hl[0], x_hl[0], start=start, stop=False, skip_group_check=True)
                nc.tensor.matmul(out_ap, w_hl[0], x_hl[1], start=False, stop=False, skip_group_check=True)
                return nc.tensor.matmul(out_ap, w_hl[1], x_hl[0], start=False, stop=stop, skip_group_check=True)

            pe.wait_ge(d_cond, 16)
            pe.wait_ge(d_w3, 16)
            for mo in range(KC):
                for kc in range(COND // P):
                    last = nc.tensor.matmul(psum[:, 7, mo * BATCH:(mo + 1) * BATCH],
                                            w3_sb[:, kc, mo * P:(mo + 1) * P], condT[:, kc, :],
                                            start=(kc == 0), stop=(kc == COND // P - 1),
                                            skip_group_check=True)
            last.then_inc(qe_mm, 1)

            def y_tile(t, p, j, chunks, final=False):
                after(pe, y_biased, t - 1)
                for kc in range(KC):
                    if j == 0:
                        pe.wait_ge(x_lo, chunks + kc + 1)
                    if isinstance(t, int) and t == 0:
                        pe.wait_ge(w_lo, kc + 1)
                    xa = xx[:, p, kc, 0, j * P:(j + 1) * P]
                    xb = xx[:, p, kc, 1, j * P:(j + 1) * P]
                    for half in range(2):
                        o = bank(2 * (j % 2) + half)
                        cut = slice(half * 512, half * 512 + 512)
                        last = three(o, (xa, xb), (w8[:, kc, 0, cut], w8[:, kc, 1, cut]),
                                     kc == 0, kc == KC - 1)
                    if final:
                        last.then_inc(w2_used, 1)
                if not final:
                    last.then_inc(y_mm, 1)

            def score_rows(k):
                pe.wait_ge(y_score, 2 * TT * (k + 1))
                after(pe, top_mask, k)
                for j in range(TT):
                    last = nc.tensor.transpose(psum[0:2, 4, j * P:(j + 1) * P],
                                               sc[:, j, :], ident)
                last.then_inc(score_T, 1)

            def spread_ranks(k):
                pe.wait_ge(top_rank, k + 1)
                nc.tensor.matmul(bank(5), consts[0:2, Z_PAIR:Z_PAIR + P], rank_b[0:2, :],
                                 start=True, stop=True, skip_group_check=True).then_inc(rank_bc, 1)

            def routed_T(k, ang_bank):
                pe.wait_ge(d_ang[k], 16)
                after(pe, ang_sb, k)
                for q in range(2):
                    last = nc.tensor.transpose(psum[:, ang_bank, q * P:(q + 1) * P],
                                               ang[:, q * P:(q + 1) * P], ident)
                last.then_inc(ang_T, 1)
                pe.wait_ge(h_norm, k + 1)
                after(pe, h_full, k)
                for kc in range(KC):
                    last = nc.tensor.transpose(psum[:, 4 + kc // 4, (kc % 4) * P:(kc % 4 + 1) * P],
                                               hs[:, kc * P:(kc + 1) * P], ident)
                last.then_inc(h_T, 1)

            def windows(i):
                first, end = isinstance(i, int) and i == 0, isinstance(i, int) and i == ST - 1
                for p in range(2):
                    for j in range(TT):
                        t = i * 2 * TT + p * TT + j
                        y_tile(t, p, j, (i * 2 + p) * KC, final=end and p == 1 and j == TT - 1)
                        if not first and p == 0 and j == 0:
                            score_rows(i - 1)
                        if not first and p == 0 and j == TT - 1:
                            spread_ranks(i - 1)
                        if end and p == 1 and j > 0:
                            routed_T(j - 1, 6)

            pe.wait_ge(d_consts, 16)
            windows(0)
            with pe.Fori(1, ST - 1) as i:
                windows(i)
            windows(ST - 1)

            def v_part(i, kc, banks):
                for half in range(2):
                    cut = slice(half * 512, half * 512 + 512)
                    last = three(bank(banks + half),
                                 (hT[:, kc, 0, i * P:(i + 1) * P], hT[:, kc, 1, i * P:(i + 1) * P]),
                                 (w8[:, kc, 0, cut], w8[:, kc, 1, cut]), kc == 0, kc == KC - 1)
                return last

            for kc in range(KC):
                pe.wait_ge(w_lo, W_V + kc + 1)
                if kc == 0:
                    pe.wait_ge(y_biased, BATCH * TT)
                    pe.wait_ge(h_lo, 2)
                for i in range(2):
                    last = v_part(i, kc, 2 * i)
                    if kc == KC - 1:
                        last.then_inc(v_mm, 1)
                if kc == 0:
                    pe.wait_ge(h_full, ST - 1)
                    score_rows(ST - 1)
                if kc == 5:
                    spread_ranks(ST - 1)
            pe.wait_ge(h_lo, 3)
            pe.wait_ge(ang_sb, 3)
            for kc in range(KC):
                last = v_part(2, kc, 6)
            last.then_inc(v_mm, 1)
            pe.wait_ge(v_sb, 2)
            routed_T(ST - 1, 3)
            pe.wait_ge(h_lo, ST)
            for kc in range(KC):
                last = v_part(3, kc, 0)
                last.then_inc(wv_used, 1)

            def project(u, slot, b):
                pe.wait_ge(w_lo, W_QK + u + 1)
                for kc in range(KC):
                    wt = [w4[:, slot, q, kc * P:(kc + 1) * P] for q in range(2)]
                    last = three(bank(b), wt, (hT[:, kc, 0, :], hT[:, kc, 1, :]), kc == 0, kc == KC - 1)
                last.then_inc(qk_mm, 1)

            def scores(h, u):
                pe.wait_ge(qk_lo, u + 1)
                for i in range(ST):
                    after(pe, s_exp, (h - 1) * ST + i + 1)
                    n = (i + 1) * P
                    qt = [q_hl[:, q, i * P:(i + 1) * P] for q in range(2)]
                    three(bank(i, n), qt, (k_hl[:, 0, 0:n], k_hl[:, 1, 0:n]), True, False)
                    nc.tensor.matmul(psum[:, i, n - P:n], ident_r[:], mask_r[:], start=False, stop=True,
                                     skip_group_check=True).then_inc(s_mm, 1)

            def flip(h, j):
                if j == 0:
                    pe.wait_ge(s_prob, (h + 1) * ST)
                after(pe, p_lo, h * ST + j - 1)
                for i in range(j, ST):
                    last = nc.tensor.transpose(psum[:, 4 + j % 2, i * P:(i + 1) * P],
                                               prob[:, i, j * P:(j + 1) * P], ident)
                last.then_inc(p_T, 1)

            def head(g, side, last_group=False):
                h = g * 2 + side
                u = g * 3
                if side == 0:
                    after(pe, qk_lo, u + 2)
                    project(u + 2, 2, 7)
                elif not last_group:
                    pe.wait_ge(p_lo, h * ST)
                    project(u + 3, 0, 5)
                    project(u + 4, 1, 7)
                if side == 1 and not last_group:
                    pe.wait_ge(rope_s, 2 * (u + 3) + 2)
                flip(h, 0)
                flip(h, 1)
                if side == 0:
                    pe.wait_ge(v_lo, g + 1)
                after(pe, o_sb, h)
                for j in range(ST):
                    pe.wait_ge(p_lo, h * ST + j + 1)
                    vt = [v_hl[:, q, j, :] for q in range(2)]
                    last = three(psum[:, 6, j * P:], vt, (pT[:, j, 0, j * P:], pT[:, j, 1, j * P:]),
                                 j == 0, j == ST - 1)
                    last.then_inc(pv_mm, 1)
                    if j + 2 < ST:
                        flip(h, j + 2)
                if side == 0:
                    scores(h + 1, u + 2)
                elif not last_group:
                    scores(h + 1, u + 4)

            pe.wait_ge(v_sb, 3)
            pe.wait_ge(h_full, ST)
            project(0, 0, 5)
            project(1, 1, 7)
            pe.wait_ge(ang_sb, ST)
            pe.wait_ge(v_sb, ST)
            pe.wait_ge(const_r, 2)
            scores(0, 1)
            head(0, 0)
            head(0, 1)
            with pe.Fori(1, KV_HEADS - 1) as g:
                head(g, 0)
                head(g, 1)
            head(KV_HEADS - 1, 0, last_group=True)
            head(KV_HEADS - 1, 1, last_group=True)

            def wo_tile(h, s, final=False):
                pe.wait_ge(w_lo, W_O + h + 1)
                pe.wait_ge(a_lo, h + 1)
                for i in range(ST):
                    at = [attn_hl[:, s % 2, q, i * P:(i + 1) * P] for q in range(2)]
                    for half in range(2):
                        if isinstance(h, int) and h == 0 and (i, half) == (3, 0):
                            pe.wait_ge(o_sb, HEADS)
                        cut = slice(half * 512, half * 512 + 512)
                        last = three(bank(2 * i + half), at, (w4[:, s, 0, cut], w4[:, s, 1, cut]),
                                     isinstance(h, int) and h == 0, final)
                    if final and i < ST - 1:
                        last.then_inc(wo_mm, 1)
                last.then_inc(w_used, 1)

            for s in range(4):
                wo_tile(s, s)
            with pe.Fori(1, HEADS // 4 - 1) as k:
                for s in range(4):
                    wo_tile(k * 4 + s, s)
            for s in range(4):
                wo_tile(HEADS - 4 + s, s, final=(s == 3))

            for i in range(ST):
                pe.wait_ge(n_norm, i + 1)
                for kc in range(KC):
                    last = nc.tensor.transpose(psum[:, 2 * i + kc // 4, (kc % 4) * P:(kc % 4 + 1) * P],
                                               h2s[:, kc * P:(kc + 1) * P], ident)
                last.then_inc(n_T, 1)

            def ffn_tile(f, odd):
                if odd is not None:
                    for gu in range(2):
                        b = 2 * odd + gu
                        n = f * 2 + gu
                        pe.wait_ge(w_lo, W_GU + n + 1)
                        after(pe, m_sb, f - 1)
                        for kc in range(KC):
                            wt = [w4[:, 2 * odd + gu, q, kc * P:(kc + 1) * P] for q in range(2)]
                            last = three(bank(b), wt, (hT[:, kc, 0, :], hT[:, kc, 1, :]),
                                         kc == 0, kc == KC - 1)
                        last.then_inc(w_used, 1)

            pe.wait_ge(n_full, ST)
            pe.wait_ge(n_lo, ST)
            ffn_tile(0, 0)
            ffn_tile(1, 1)
            with pe.Fori(1, FT // 2) as k:
                ffn_tile(k * 2, 0)
                ffn_tile(k * 2 + 1, 1)

            def down_tile(f, s, first=False, final=False):
                pe.wait_ge(w_lo, W_DOWN + f + 1)
                pe.wait_ge(m_lo, f + 1)
                order = (2, 3, 0, 1) if first else range(ST)
                for i in order:
                    if first and i == 0:
                        pe.wait_ge(m_sb, FT)
                    mt = [m_hl[:, s % 2, q, i * P:(i + 1) * P] for q in range(2)]
                    for half in range(2):
                        cut = slice(half * 512, half * 512 + 512)
                        last = three(bank(2 * i + half), mt, (w4[:, s, 0, cut], w4[:, s, 1, cut]),
                                     first, final)
                    if final and i < ST - 1:
                        last.then_inc(dn_mm, 1)
                last.then_inc(w_used, 1)

            for s in range(4):
                down_tile(s, s, first=(s == 0))
            with pe.Fori(1, FT // 4 - 1) as k:
                for s in range(4):
                    down_tile(k * 4 + s, s)
            for s in range(4):
                down_tile(FT - 4 + s, s, final=(s == 3))

        @block.scalar
        def _(act):
            act.preload_act_table(ACT.Sqrt)

            def w_part(n, raw_slot, landed, count, dst, free=None, used=0):
                act.wait_ge(landed, count)
                if free is not None:
                    act.wait_ge(free, used)
                nc.scalar.activation(dst, raw[:, raw_slot, :], ACT.Copy).then_inc(w_hi, 1)

            def x_chunks(b, p, kcs, gemm_done):
                for kc in kcs:
                    c = b * KC + kc
                    act.wait_ge(d_xT[kc % 4], 16 * (2 * b + kc // 4) + 16)
                    after(act, x_sum, c)
                    nc.scalar.activation(junk_sum[:, 0:SEQ], xT[:, kc % 4, :], ACT.Identity,
                                         scale=1.0 / SEQ, accum_out=vs[:, p, kc:kc + 1]).then_inc(x_sum, 1)
                for kc in kcs:
                    c = b * KC + kc
                    act.wait_ge(x_mod, c + 1)
                    after(act, y_mm, gemm_done)
                    nc.scalar.activation(xx[:, p, kc, 0, :], xT[:, kc % 4, :], ACT.Copy).then_inc(x_hi, 1)

            def y_out(t, j, dst, row):
                act.wait_ge(y_biased, t + 1)
                nc.scalar.activation(y[:, j % 2, :], y[:, j % 2, :], ACT.Relu).then_inc(y_relu, 1)
                act.wait_ge(y_relu, t + 1)
                act.dma_start(dst[bass.ds(row, P), :], y[:, j % 2, :]).then_inc(d_y[j % 2], 16)

            def routed(k):
                act.wait_ge(d_ysel[k], 16)
                if k == 0:
                    act.wait_ge(rank_bc, ST - 1)
                after(act, h_T, k)
                nc.scalar.activation(hs, ysel[:, k % 2, :], ACT.Square, accum_out=ssq[:, k:k + 1]).then_inc(h_sq, 1)
                act.wait_ge(h_ms, k + 1)
                nc.scalar.activation(rt[:, k:k + 1], ms[:, k:k + 1], ACT.Sqrt).then_inc(h_rt, 1)

            def routed_split(k):
                act.wait_ge(ang_T, k + 1)
                b = 3 if k == ST - 1 else 6
                nc.scalar.activation(cosT[:, k * P:(k + 1) * P], psum[:, b, 0:P], ACT.Copy)
                nc.scalar.activation(sinT[:, k * P:(k + 1) * P], psum[:, b, P:2 * P], ACT.Copy).then_inc(ang_sb, 1)
                act.wait_ge(h_full, k + 1)
                nc.scalar.activation(hT[:, :, 0, k * P:(k + 1) * P], hfull, ACT.Copy).then_inc(h_hi, 1)

            for kc in range(0, KC, 2):
                x_chunks(0, 0, (kc, kc + 1), 0)
                for n in (kc, kc + 1):
                    w_part(n, n % 2, d_raw2[n % 2], 16 * (n // 2) + 16, w8[:, n, 0, :])
            act.wait_ge(d_consts, 16)
            nc.scalar.activation(ident_r[:], ident, ACT.Copy).then_inc(const_r, 1)
            nc.scalar.activation(mask_r[:], consts[:, Z_MASK:Z_MASK + P], ACT.Copy).then_inc(const_r, 1)

            def windows(i):
                end = isinstance(i, int) and i == ST - 1
                for p in range(2):
                    b = i * 2 + p
                    for j in range(TT):
                        if not (end and p == 1):
                            x_chunks(b + 1, 1 - p, (2 * j, 2 * j + 1), b * TT)
                        elif j == 0:
                            act.wait_ge(y_mm, b * TT)
                        row = (p * TT + j) * P
                        if end:
                            y_out(b * TT + j, j, y_last, row)
                        elif isinstance(i, int):
                            y_out(b * TT + j, j, y_first, row)
                        else:
                            y_out(b * TT + j, j, y_middle, (i - 1) * PAIR + row)
                        if end and p == 1:
                            if j > 0:
                                routed_split(j - 1)
                            if j < TT - 1:
                                routed(j)

            windows(0)
            with act.Fori(1, ST - 1) as i:
                windows(i)
            windows(ST - 1)

            for kc in range(KC):
                n = W_V + kc
                w_part(n, n % 2, d_raw2[n % 2], 16 * (n // 2) + 16, w8[:, kc, 0, :], w2_used, kc + 1)
            for u in range(3):
                w_part(W_QK + u, u, d_raw3[u], 16, w4[:, u, 0, :], w2_used, KC)
            routed(3)
            routed_split(3)

            act.preload_act_table(ACT.Exp)

            def qk_part(u, dst):
                act.wait_ge(rope_sum, u + 1)
                nc.scalar.activation(dst, rope[:, 0, :], ACT.Copy).then_inc(qk_hi, 1)

            def head(g, side, last_group=False):
                h = g * 2 + side
                for i in range(ST):
                    n = (i + 1) * P
                    act.wait_ge(s_nmax, h + 1)
                    after(act, p_T, h * ST)
                    nc.scalar.activation(prob[:, i, 0:n], bank(i, n), ACT.Exp, bias=nmx[:, i:i + 1],
                                         scale=SCALE, accum_out=lsum[:, i:i + 1]).then_inc(s_exp, 1)
                if side == 0:
                    after(act, pv_mm, h * ST)
                    nc.scalar.activation(v_hl[:, 0, :, :], V[:, :, bass.ds(g * HD, HD)], ACT.Copy).then_inc(v_hi, 1)
                if not last_group:
                    for u in ((0, 1) if side == 0 else (2,)):
                        w_part(W_QK + 3 * g + 3 + u, u, d_raw3[u], 16 * g + 32, w4[:, u, 0, :],
                               qk_mm, 3 * g + u + 1)
                if side == 1 and not last_group:
                    act.wait_ge(s_mm, (h + 1) * ST)
                    qk_part(3 * g + 3, k_hl[:, 0, :])
                for j in range(ST):
                    act.wait_ge(p_T, h * ST + j + 1)
                    after(act, pv_mm, h * ST)
                    nc.scalar.activation(pT[:, j, 0, j * P:], psum[:, 4 + j % 2, j * P:], ACT.Copy).then_inc(p_hi, 1)
                if side == 0:
                    qk_part(3 * g + 2, q_hl[:, 0, :])
                elif not last_group:
                    qk_part(3 * g + 4, q_hl[:, 0, :])
                act.wait_ge(pv_mm, (h + 1) * ST)
                nc.scalar.activation(attn[:, bass.ds(h, 1), :].rearrange("p a n -> p (a n)"), bank(6), ACT.Copy).then_inc(o_sb, 1)

            act.wait_ge(wv_used, KC)
            qk_part(0, k_hl[:, 0, :])
            qk_part(1, q_hl[:, 0, :])
            head(0, 0)
            head(0, 1)
            with act.Fori(1, KV_HEADS - 1) as g:
                head(g, 0)
                head(g, 1)
            head(KV_HEADS - 1, 0, last_group=True)
            head(KV_HEADS - 1, 1, last_group=True)

            def rest_part(n, s, first=False):
                k = n - W_O
                act.wait_ge(d_raw[s % 2], 8 * (k - s % 2) + 16)
                if first:
                    act.wait_ge(qk_mm, W_O - W_QK)
                else:
                    act.wait_ge(w_used, k - 3)
                nc.scalar.activation(w4[:, s, 0, :], raw[:, s % 2, :], ACT.Copy).then_inc(w_hi, 1)

            def attn_part(h, s):
                act.wait_ge(o_sb, HEADS) if isinstance(h, int) and h == 0 else None
                after(act, w_used, h - 1)
                nc.scalar.activation(attn_hl[:, s % 2, 0, :], attn[:, bass.ds(h, 1), :].rearrange("p a n -> p (a n)"),
                                     ACT.Copy).then_inc(a_hi, 1)

            for s in range(4):
                rest_part(W_O + s, s, first=True)
                attn_part(s, s)
            with act.Fori(1, HEADS // 4) as k:
                for s in range(4):
                    rest_part(W_O + k * 4 + s, s)
                    attn_part(k * 4 + s, s)
            act.preload_act_table(ACT.Sigmoid)
            nc.scalar.activation(gate, sels, ACT.Sigmoid).then_inc(g_sig, 1)
            act.preload_act_table(ACT.Sqrt)
            for n in range(4):
                rest_part(W_GU + n, n)
            for i in range(ST):
                act.wait_ge(x1_sb, i + 1)
                after(act, n_T, i)
                nc.scalar.activation(h2s, x1[:, i, :], ACT.Square, accum_out=ssq[:, i:i + 1]).then_inc(n_sq, 1)
                act.wait_ge(n_ms, i + 1)
                nc.scalar.activation(rt[:, i:i + 1], ms[:, i:i + 1], ACT.Sqrt).then_inc(n_rt, 1)
                act.wait_ge(n_full, i + 1)
                nc.scalar.activation(hT[:, :, 0, i * P:(i + 1) * P], h2full, ACT.Copy).then_inc(n_hi, 1)

            act.preload_act_table(ACT.Silu)

            def ffn(f, odd, tail=False):
                act.wait_ge(w_used, HEADS + f * 2 + 1)
                after(act, m_sb, f - 1)
                nc.scalar.activation(silu_g[:, odd, :], bank(2 * odd), ACT.Silu).then_inc(g_silu, 1)
                rest_part(W_GU + f * 2 + 4, 2 * odd)
                rest_part(W_GU + f * 2 + 5, 2 * odd + 1)

            ffn(0, 0)
            ffn(1, 1)
            act.wait_ge(g_base, ST)
            act.dma_start(base_rows.rearrange("(i p) n -> p i n", p=P), xsel).then_inc(d_base, 16)
            with act.Fori(1, FT // 2) as k:
                ffn(k * 2, 0)
                ffn(k * 2 + 1, 1)

            def m_part(f, s):
                if isinstance(f, int) and f < 2:
                    act.wait_ge(m_sb, f + 1)
                else:
                    act.wait_ge(w_used, W_DOWN - W_O + f - 1)
                nc.scalar.activation(m_hl[:, s % 2, 0, :], m[:, bass.ds(f, 1), :].rearrange("p a n -> p (a n)"),
                                     ACT.Copy).then_inc(m_hi, 1)

            def down_parts(k):
                for s in range(4):
                    rest_part(W_DOWN + k * 4 + s, s)
                    m_part(k * 4 + s, s)

            for s in range(4):
                m_part(s, s)
            with act.Fori(1, 3) as k:
                down_parts(k)
            act.wait_ge(m_lo, 8)
            act.wait_ge(m_hi, 8)
            for i in range(ST):
                act.dma_start(base[:, i, :], base_rows[i * P:(i + 1) * P, :]).then_inc(d_baseld[i], 16)
            with act.Fori(3, FT // 4) as k:
                down_parts(k)

        @block.gpsimd
        def _(pool):
            def w_part(n, raw_slot, dst_slot):
                pool.wait_ge(w_hi, n + 1)
                nc.gpsimd.tensor_tensor(dst_slot[:, 1, :], raw[:, raw_slot, :], as_f32(dst_slot[:, 0, :]),
                                        ALU.subtract).then_inc(w_lo, 1)

            def x_plus_y(b, j):
                t = b * TT + j
                pool.wait_ge(y_relu, t + 1)
                pool.wait_ge(d_x[j], 16 * b + 16)
                nc.gpsimd.tensor_tensor(xrow[:, j, :], xrow[:, j, :], y[:, j % 2, :], ALU.add).then_inc(out_row, 1)

            def gather_angles(k):
                pool.wait_ge(idx_u, 3 * (k + 1))
                after(pool, ang_T, k)
                pool.indirect_dma_start(ang, None, angles,
                                        bass.IndirectOffsetOnAxis(ap=idx[:, ST + k:ST + k + 1], axis=0)).then_inc(d_ang[k], 16)

            def gather(k):
                pool.wait_ge(idx_u, 3 * (k + 1))
                for s in range(2):
                    pool.wait_ge(d_y[s], 16 * TT * (k + 1))
                after(pool, h_norm, k - 1)
                after(pool, h_sel, k - 1)
                pool.indirect_dma_start(ysel[:, k % 2, :], None, y_of[k],
                                        bass.IndirectOffsetOnAxis(ap=idx[:, 2 * ST + k:2 * ST + k + 1], axis=0)).then_inc(d_ysel[k], 16)

            for n in range(KC):
                w_part(n, n % 2, w8[:, n])
            with pool.Fori(0, ST - 1) as i:
                for p in range(2):
                    for j in range(TT):
                        x_plus_y(i * 2 + p, j)
            b = BATCH - 2
            for p in range(2):
                for j in range(TT):
                    x_plus_y(b + p, j)
                    if p == 0 and j == 0:
                        gather_angles(0)
                        gather(0)
                        gather(1)
                    if p == 1 and j == 0:
                        gather(2)
                    if p == 1 and j in (1, 2):
                        gather_angles(j)
            for kc in range(KC):
                w_part(W_V + kc, kc % 2, w8[:, kc])
            gather(3)
            gather_angles(3)
            for u in range(3):
                w_part(W_QK + u, u, w4[:, u])

            def head(g, side, last_group=False):
                h = g * 2 + side
                apart(pool, s_rl, h + 1, pool_passed)
                for i in range(ST):
                    n = (i + 1) * P
                    nc.gpsimd.tensor_scalar(prob[:, i, 0:n], prob[:, i, 0:n], rl[:, i:i + 1], None,
                                            ALU.mult).then_inc(s_prob, 1)
                if not last_group:
                    for u in ((0, 1) if side == 0 else (2,)):
                        w_part(W_QK + 3 * g + 3 + u, u, w4[:, u])

            head(0, 0)
            head(0, 1)
            with pool.Fori(1, KV_HEADS - 1) as g:
                head(g, 0)
                head(g, 1)
            head(KV_HEADS - 1, 0, last_group=True)
            head(KV_HEADS - 1, 1, last_group=True)

            def gather_rows(dst, src, c, landed):
                pool.indirect_dma_start(dst, None, src,
                                        bass.IndirectOffsetOnAxis(ap=idx[:, c:c + 1], axis=0)).then_inc(landed, 16)

            w_part(W_O, 0, w4[:, 0])
            pool.wait_ge(p_T, HEADS * ST)
            for k in range(2):
                gather_rows(ysel4[k], y_of[k], 2 * ST + k, d_ysel4[k])
            for s in range(1, 4):
                w_part(W_O + s, s % 2, w4[:, s])
            with pool.Fori(1, HEADS // 4) as k:
                for s in range(4):
                    w_part(W_O + k * 4 + s, s % 2, w4[:, s])
            pool.wait_ge(a_lo, HEADS)
            for k in (2, 3):
                gather_rows(ysel4[k], y_of[k], 2 * ST + k, d_ysel4[k])
            for k in range(ST):
                gather_rows(xsel[:, k, :], x_rows, k, d_xsel[k])
            with pool.Fori(0, (W_END - W_GU) // 4) as k:
                for s in range(4):
                    w_part(W_GU + k * 4 + s, s % 2, w4[:, s])
            for j in range(TT):
                pool.wait_ge(d_out[j], 16 * BATCH)
            for i in range(ST):
                pool.wait_ge(fin, i + 1)
                pool.indirect_dma_start(out, bass.IndirectOffsetOnAxis(ap=idx[:, i:i + 1], axis=0),
                                        base[:, i, :], None).then_inc(d_fin, 16)

        @block.vector
        def _(dve):
            dve.wait_ge(qe_mm, 1)
            dve.wait_ge(d_cols, 16)
            q_ps = psum[:, 7, 0:KC * BATCH].rearrange("p (k b) -> p k b", b=BATCH)
            b3 = col[:, C_B3:C_B3 + KC].rearrange("p (k a) -> p k a", a=1).broadcast_to([P, KC, BATCH])
            nc.vector.tensor_tensor(qe, q_ps, b3, ALU.add).then_inc(qe_b, 1)
            dve.wait_ge(qe_b, 1)
            nc.vector.tensor_scalar(qe, qe, 0.0, float(SEQ), ALU.max, ALU.mult).then_inc(qe_done, 1)
            dve.wait_ge(qe_done, 1)

            def x_chunks(b, p, kcs):
                for kc in kcs:
                    c = b * KC + kc
                    dve.wait_ge(x_sum, c + 1)
                    nc.vector.tensor_scalar(xT[:, kc % 4, :], xT[:, kc % 4, :], vs[:, p, kc:kc + 1],
                                            qe[:, kc, bass.ds(b, 1)], ALU.add, ALU.mult).then_inc(x_mod, 1)
                for kc in kcs:
                    c = b * KC + kc
                    dve.wait_ge(x_hi, c + 1)
                    nc.vector.tensor_tensor(xx[:, p, kc, 1, :], xT[:, kc % 4, :], as_f32(xx[:, p, kc, 0, :]),
                                            ALU.subtract).then_inc(x_lo, 1)

            def y_tile(i, p, j, final=False):
                b = i * 2 + p
                t, half = b * TT + j, 2 * b + j // 2
                if final:
                    dve.wait_ge(w2_used, KC)
                else:
                    dve.wait_ge(y_mm, t + 1)
                after(dve, d_y[j % 2], 16 * half)
                after(dve, y_score, t - 1)
                after(dve, out_row, t - 1)
                nc.vector.tensor_tensor(y[:, j % 2, :], pair(2 * (j % 2)), bias_row, ALU.add).then_inc(y_biased, 1)
                dve.wait_ge(y_relu, t + 1)
                after(dve, y_score, t)
                if p == 0 and j == 0:
                    after(dve, score_T, i)
                nc.vector.scalar_tensor_tensor(junk[:, 0:D], y[:, j % 2, :], 1.0, wr_row, ALU.mult, ALU.mult,
                                               accum_out=sc[:, j, p:p + 1]).then_inc(y_score, 1)

            score_ps = psum[0:2, 4, :]
            def top_rounds(k, rounds):
                for r in rounds:
                    src = score_ps if r == 0 else (rank_a, rank_b)[(r - 1) % 2][0:2, :]
                    dst = (rank_a, rank_b)[r % 2][0:2, :]
                    if r == 0:
                        after(dve, top_cut, k * 8)
                        apart(dve, score_T, k + 1, dve_passed)
                    else:
                        apart(dve, top_cut, k * 8 + r, dve_passed)
                    nc.vector.max(top8[0:2, :], src).then_inc(top_max, 1)
                    apart(dve, top_max, k * 8 + r + 1, dve_passed)
                    nc.vector.match_replace(dst, top8[0:2, :], src, LOWEST).then_inc(top_cut, 1)

            def top_ranks(k):
                dve.wait_ge(top_cut, k * 8 + 8)
                nc.vector.tensor_tensor(rank_a[0:2, :], rank_b[0:2, :], score_ps, ALU.not_equal).then_inc(top_mask, 1)
                dve.wait_ge(top_mask, k + 1)
                nc.vector.tensor_tensor_scan(rank_b[0:2, :], rank_a[0:2, :], rank_a[0:2, :], 0.0,
                                             ALU.add, ALU.max).then_inc(top_rank, 1)

            def top_index(k, scored):
                dve.wait_ge(rank_bc, k + 1)
                dve.wait_ge(y_score, scored)
                nc.vector.tensor_scalar(junk[:, 0:SEQ], bank(5), consts[:, Z_RANK:Z_RANK + 1], 0.0, ALU.is_le,
                                        ALU.add, accum_out=idxf[:, bass.ds(k, 1)]).then_inc(idx_f, 1)
                dve.wait_ge(idx_f, k + 1)
                nc.vector.tensor_scalar(idx[:, bass.ds(k, 1)], idxf[:, bass.ds(k, 1)],
                                        consts[:, bass.ds(Z_BASE + k, 1)], None, ALU.add).then_inc(idx_u, 1)
                nc.vector.tensor_copy(idx[:, bass.ds(ST + k, 1)], idxf[:, bass.ds(k, 1)]).then_inc(idx_u, 1)
                nc.vector.tensor_scalar(idx[:, bass.ds(2 * ST + k, 1)], idxf[:, bass.ds(k, 1)],
                                        consts[:, bass.ds(Z_YBASE + k, 1)], None, ALU.add).then_inc(idx_u, 1)

            def inverse_root(k, sq_sem, ms_sem, rt_sem, chain, done):
                a, r, q = ms[:, k:k + 1], rs[:, k:k + 1], na[:, k:k + 1]
                dve.wait_ge(sq_sem, k + 1)
                nc.vector.tensor_scalar(a, ssq[:, k:k + 1], 1.0 / D, EPS, ALU.mult, ALU.add).then_inc(ms_sem, 1)
                dve.wait_ge(rt_sem, k + 1)
                nc.vector.reciprocal(r, rt[:, k:k + 1]).then_inc(chain, 1)
                dve.wait_ge(chain, 3 * k + 1)
                nc.vector.scalar_tensor_tensor(q, r, a, r, ALU.mult, ALU.mult).then_inc(chain, 1)
                dve.wait_ge(chain, 3 * k + 2)
                nc.vector.tensor_scalar(q, q, -0.5, 1.5, ALU.mult, ALU.add).then_inc(chain, 1)
                dve.wait_ge(chain, 3 * k + 3)
                nc.vector.tensor_tensor(r, r, q, ALU.mult).then_inc(done, 1)

            def routed(k, scored):
                inverse_root(k, h_sq, h_ms, h_rt, h_chain, h_rs)
                dve.wait_ge(y_score, scored)
                dve.wait_ge(d_ysel[k], 16)
                after(dve, h_sel, k)
                nc.vector.scalar_tensor_tensor(junk[:, 0:D], ysel[:, k % 2, :], 1.0, wr_row, ALU.mult, ALU.mult,
                                               accum_out=sels[:, k:k + 1]).then_inc(h_sel, 1)
                dve.wait_ge(h_rs, k + 1)
                nc.vector.tensor_scalar(hs, ysel[:, k % 2, :], rs[:, k:k + 1], None, ALU.mult).then_inc(h_norm, 1)

            def routed_split(k):
                dve.wait_ge(h_T, k + 1)
                after(dve, h_lo, k)
                ln = col[:, C_LN1:C_LN1 + KC].rearrange("p (k a) -> p k a", a=1).broadcast_to([P, KC, P])
                h_ps = psum[:, 4:6, :].rearrange("p b (k n) -> p (b k) n", k=4)
                nc.vector.tensor_tensor(hfull, h_ps, ln, ALU.mult).then_inc(h_full, 1)
                dve.wait_ge(h_hi, k + 1)
                nc.vector.tensor_tensor(hT[:, :, 1, k * P:(k + 1) * P], hfull, as_f32(hT[:, :, 0, k * P:(k + 1) * P]),
                                        ALU.subtract).then_inc(h_lo, 1)

            for kc in range(0, KC, 2):
                x_chunks(0, 0, (kc, kc + 1))
            dve.wait_ge(d_b2, 16)
            dve.wait_ge(d_wr, 16)
            dve.wait_ge(d_consts, 16)

            def windows(i):
                first, end = isinstance(i, int) and i == 0, isinstance(i, int) and i == ST - 1
                for p in range(2):
                    b = i * 2 + p
                    for j in range(TT):
                        if not (end and p == 1):
                            x_chunks(b + 1, 1 - p, (2 * j, 2 * j + 1))
                        if not first and p == 0 and j > 0:
                            top_rounds(i - 1, ((), (0, 1, 2), (3, 4, 5), (6, 7))[j])
                        if not first and p == 0 and j == TT - 1:
                            top_ranks(i - 1)
                        if not first and p == 1 and j == 0:
                            top_index(i - 1, b * TT)
                        y_tile(i, p, j, final=end and p == 1 and j == TT - 1)
                        if end and p == 1:
                            if j > 0:
                                routed_split(j - 1)
                            if j < TT - 1:
                                routed(j, b * TT + j + 1)

            windows(0)
            with dve.Fori(1, ST - 1) as i:
                windows(i)
            windows(ST - 1)

            def v_out(i, banks):
                dve.wait_ge(d_bv, 16)
                for j in range(TT):
                    dve.wait_ge(d_out[j], 16 * BATCH)
                nc.vector.tensor_tensor(V[:, i, :], pair(banks), bias_row, ALU.add).then_inc(v_sb, 1)

            top_rounds(ST - 1, range(8))
            top_ranks(ST - 1)
            top_index(ST - 1, BATCH * TT)
            dve.wait_ge(v_mm, 1)
            v_out(0, 0)
            dve.wait_ge(v_mm, 2)
            v_out(1, 2)
            routed(3, BATCH * TT)
            routed_split(3)
            dve.wait_ge(v_mm, 3)
            v_out(2, 6)

            def rotate(u, b):
                after(dve, qk_lo, u)
                dve.wait_ge(qk_mm, u + 1)
                c = bass.ds(C_BQK + u, 1)
                cs = bass.ds(C_BQKS + u, 1)
                nc.vector.scalar_tensor_tensor(rope[:, 0, :], bank(b), col[:, c], cosT, ALU.add, ALU.mult).then_inc(rope_c, 1)
                for lo in (0, 64):
                    nc.vector.scalar_tensor_tensor(rope[lo:lo + 64, 1, :], psum[64 - lo:128 - lo, b, :], col[lo:lo + 64, cs],
                                                   sinT[lo:lo + 64, :], ALU.add, ALU.mult).then_inc(rope_s, 1)
                dve.wait_ge(rope_c, u + 1)
                dve.wait_ge(rope_s, 2 * u + 2)
                nc.vector.tensor_tensor(rope[:, 0, :], rope[:, 0, :], rope[:, 1, :], ALU.add).then_inc(rope_sum, 1)

            def qk_part(u, dst):
                dve.wait_ge(qk_hi, u + 1)
                nc.vector.tensor_tensor(dst[:, 1, :], rope[:, 0, :], as_f32(dst[:, 0, :]), ALU.subtract).then_inc(qk_lo, 1)

            def head(g, side, last_group=False):
                h = g * 2 + side
                for i in range(ST):
                    dve.wait_ge(s_mm, h * ST + i + 1)
                    nc.vector.reduce_max(mx[:, i:i + 1], bank(i, (i + 1) * P), AX).then_inc(s_max, 1)
                dve.wait_ge(s_max, h * ST + ST)
                nc.vector.tensor_scalar(nmx, mx, -SCALE, None, ALU.mult).then_inc(s_nmax, 1)
                if side == 0:
                    dve.wait_ge(v_hi, g + 1)
                    nc.vector.tensor_tensor(v_hl[:, 1, :, :], V[:, :, bass.ds(g * HD, HD)], as_f32(v_hl[:, 0, :, :]),
                                            ALU.subtract).then_inc(v_lo, 1)
                dve.wait_ge(s_exp, h * ST + ST)
                after(dve, s_prob, h * ST)
                nc.vector.reciprocal(rl, lsum).then_inc(s_rl, 1)
                if side == 1 and not last_group:
                    rotate(3 * g + 3, 5)
                    qk_part(3 * g + 3, k_hl)
                nxt = 3 * g + 2 if side == 0 else 3 * g + 4
                if side == 0 or not last_group:
                    rotate(nxt, 7)
                for j in range(ST):
                    dve.wait_ge(p_hi, h * ST + j + 1)
                    nc.vector.tensor_tensor(pT[:, j, 1, j * P:], psum[:, 4 + j % 2, j * P:], as_f32(pT[:, j, 0, j * P:]),
                                            ALU.subtract).then_inc(p_lo, 1)
                if side == 0 or not last_group:
                    qk_part(nxt, q_hl)

            dve.wait_ge(ang_sb, ST)
            rotate(0, 5)
            dve.wait_ge(wv_used, KC)
            v_out(3, 0)
            qk_part(0, k_hl)
            rotate(1, 7)
            qk_part(1, q_hl)
            head(0, 0)
            head(0, 1)
            with dve.Fori(1, KV_HEADS - 1) as g:
                head(g, 0)
                head(g, 1)
            head(KV_HEADS - 1, 0, last_group=True)
            head(KV_HEADS - 1, 1, last_group=True)

            def attn_part(h, s):
                dve.wait_ge(a_hi, h + 1)
                nc.vector.tensor_tensor(attn_hl[:, s % 2, 1, :], attn[:, bass.ds(h, 1), :].rearrange("p a n -> p (a n)"),
                                        as_f32(attn_hl[:, s % 2, 0, :]), ALU.subtract).then_inc(a_lo, 1)

            with dve.Fori(0, HEADS // 2) as k:
                for s in range(2):
                    attn_part(k * 2 + s, s)
            dve.wait_ge(g_sig, 1)
            nc.vector.tensor_scalar(ungate, gate, -1.0, 1.0, ALU.mult, ALU.add).then_inc(g_un, 1)

            for i in range(ST):
                if i < ST - 1:
                    dve.wait_ge(wo_mm, i + 1)
                else:
                    dve.wait_ge(w_used, HEADS)
                dve.wait_ge(d_ysel4[i], 16)
                nc.vector.tensor_tensor(x1[:, i, :], pair(2 * i), ysel4[i], ALU.add).then_inc(x1_sb, 1)
                inverse_root(i, n_sq, n_ms, n_rt, n_chain, n_rs)
                dve.wait_ge(n_rs, i + 1)
                nc.vector.tensor_scalar(h2s, x1[:, i, :], rs[:, i:i + 1], None, ALU.mult).then_inc(n_norm, 1)
                dve.wait_ge(n_T, i + 1)
                after(dve, n_lo, i)
                ln = col[:, C_LN2:C_LN2 + KC].rearrange("p (k a) -> p k a", a=1).broadcast_to([P, KC, P])
                n_ps = psum[:, 2 * i:2 * i + 2, :].rearrange("p b (k n) -> p (b k) n", k=4)
                nc.vector.tensor_tensor(h2full, n_ps, ln, ALU.mult).then_inc(n_full, 1)
                dve.wait_ge(n_hi, i + 1)
                nc.vector.tensor_tensor(hT[:, :, 1, i * P:(i + 1) * P], h2full, as_f32(hT[:, :, 0, i * P:(i + 1) * P]),
                                        ALU.subtract).then_inc(n_lo, 1)
            dve.wait_ge(g_un, 1)
            for i in range(ST):
                dve.wait_ge(d_xsel[i], 16)
                nc.vector.scalar_tensor_tensor(xsel[:, i, :], x1[:, i, :], gate[:, i:i + 1], xsel[:, i, :],
                                               ALU.mult, ALU.add).then_inc(g_mix, 1)
                dve.wait_ge(g_mix, i + 1)
                nc.vector.scalar_tensor_tensor(xsel[:, i, :], ysel4[i], ungate[:, i:i + 1], xsel[:, i, :],
                                               ALU.mult, ALU.add).then_inc(g_base, 1)
                dve.wait_ge(g_base, i + 1)

            def ffn(f, odd):
                dve.wait_ge(w_used, HEADS + f * 2 + 2)
                dve.wait_ge(g_silu, f + 1)
                nc.vector.tensor_tensor(m[:, bass.ds(f, 1), :].rearrange("p a n -> p (a n)"), silu_g[:, odd, :],
                                        bank(2 * odd + 1), ALU.mult).then_inc(m_sb, 1)

            for f in range(12):
                ffn(f, f % 2)
            dve.wait_ge(d_base, 16)
            with dve.Fori(6, FT // 2) as k:
                ffn(k * 2, 0)
                ffn(k * 2 + 1, 1)

            with dve.Fori(0, FT // 2) as k:
                for s in range(2):
                    dve.wait_ge(m_hi, k * 2 + s + 1)
                    nc.vector.tensor_tensor(m_hl[:, s, 1, :], m[:, bass.ds(k * 2 + s, 1), :].rearrange("p a n -> p (a n)"),
                                            as_f32(m_hl[:, s, 0, :]), ALU.subtract).then_inc(m_lo, 1)
            for i in range(ST):
                if i < ST - 1:
                    dve.wait_ge(dn_mm, i + 1)
                else:
                    dve.wait_ge(w_used, W_END - W_O)
                dve.wait_ge(d_baseld[i], 16)
                nc.vector.scalar_tensor_tensor(base[:, i, :], pair(2 * i), gate[:, i:i + 1], base[:, i, :],
                                               ALU.mult, ALU.add).then_inc(fin, 1)


_OUTS = [((BATCH, SEQ, D), "float32")]


def kernel(**inputs):
    import concourse.bacc as _bacc
    from concourse.bass_utils import run_bass_kernel_spmd as _run

    a = {k: np.asarray(v) for k, v in inputs.items()}
    x = a["x"]

    def columns(v):
        return v.reshape(-1, P).T

    x_t = np.ascontiguousarray(x.reshape(BATCH, SEQ, KC, P).transpose(0, 2, 3, 1)).reshape(BATCH * KC, P, SEQ)
    heads = lambda w: w.reshape(KC, P, -1, P).transpose(2, 1, 0, 3).reshape(-1, P, D)
    wq, wk = heads(a["L0_ffn_wq"]), heads(a["L0_ffn_wk"])
    qk = [t for g in range(KV_HEADS) for t in (wk[g], wq[2 * g], wq[2 * g + 1])]
    wg, wu = heads(a["L0_ffn_w_gate"]), heads(a["L0_ffn_w_up"])
    gu = [t for f in range(FT) for t in (wg[f], wu[f])]
    rows_of = lambda w: w.reshape(-1, P, D)
    wstream = np.concatenate([rows_of(a["L0_cond_W2"]), rows_of(a["L0_ffn_wv"]), np.stack(qk),
                              rows_of(a["L0_ffn_wo"]), np.stack(gu), rows_of(a["L0_ffn_w_down"])])
    bq, bk = a["L0_ffn_bq"].reshape(HEADS, HD), a["L0_ffn_bk"].reshape(KV_HEADS, HD)
    bqk = np.stack([t for g in range(KV_HEADS) for t in (bk[g], bq[2 * g], bq[2 * g + 1])])
    swapped = np.concatenate([bqk[:, HD // 2:], bqk[:, :HD // 2]], axis=1)
    cols = np.concatenate([columns(a["L0_cond_b3"]), columns(a["L0_ffn_ln1_w"]), columns(a["L0_ffn_ln2_w"]),
                           bqk.T, swapped.T], axis=1)
    rows = np.stack([a["L0_cond_b2"], a["L0_ffn_w_router"], a["L0_ffn_bv"]])

    part = np.arange(P)
    shape_consts = np.zeros((P, N_CONSTS), np.float32)
    shape_consts[:, Z_IDENT:Z_IDENT + P] = np.eye(P)
    shape_consts[:, Z_MASK:Z_MASK + P] = np.where(part[None, :] > part[:, None], LOWEST, 0.0)
    for half in range(2):
        shape_consts[half, Z_PAIR + half * PICK:Z_PAIR + (half + 1) * PICK] = 1.0
    shape_consts[:, Z_RANK] = part % PICK
    for k in range(ST):
        shape_consts[:, Z_BASE + k] = (2 * k + part // PICK) * SEQ
        shape_consts[:, Z_YBASE + k] = (2 * (k == 2) + part // PICK) * SEQ
    inv_freq = (np.float32(1.0) / np.float32(10000.0) ** (np.arange(0, HD, 2, dtype=np.float32) / np.float32(HD)))
    phase = (np.arange(SEQ, dtype=np.float32)[:, None] * inv_freq.astype(np.float32)).astype(np.float32)
    cos, sin = np.cos(phase), np.sin(phase)
    angles = np.concatenate([cos, cos, -sin, sin], axis=1).astype(np.float32)

    arrays = {
        "x_t": x_t, "x_rows": x.reshape(BATCH * SEQ, D),
        "cond_t": a["cond_1024"].T.reshape(COND // P, P, BATCH).transpose(1, 0, 2),
        "w3": a["L0_cond_W3"], "wstream": wstream, "cols": cols, "rows": rows,
        "shape_consts": shape_consts, "angles": angles,
    }
    arrays = {k: np.ascontiguousarray(v) for k, v in arrays.items()}
    nc = _bacc.Bacc("TRN2", target_bir_lowering=False, num_devices=1)
    args = {k: nc.dram_tensor(k, v.shape, mybir.dt.from_np(v.dtype), kind="ExternalInput").ap()
            for k, v in arrays.items()}
    out = nc.dram_tensor("out", (BATCH * SEQ, D), mybir.dt.float32, kind="ExternalOutput").ap()
    build(nc, out=out, **args)
    r = _run(nc, [arrays], core_ids=[0])
    return r.results[0]["out"].reshape(BATCH, SEQ, D)
```

```python
from contextlib import ExitStack

import numpy as np

import concourse.bass as bass
from concourse import mybir

P = 128
BATCH, SEQ, D = 8, 512, 1024
COND = 512
HEADS, KV_HEADS, HD = 16, 8, 128
FF = 4096
PICK = 64
S = BATCH * PICK
KC = D // P
TT = SEQ // P
ST = S // P
FT = FF // P
EPS = 1e-6
SCALE = 1.0 / float(np.sqrt(np.float32(HD)))
LOWEST = -3.0e38

W_V = KC
W_QK = W_V + KC
W_O = W_QK + HEADS + KV_HEADS
W_GU = W_O + HEADS
W_DOWN = W_GU + 2 * FT
W_END = W_DOWN + FT

C_B3, C_LN1, C_LN2 = 0, KC, 2 * KC
C_BQK = 3 * KC
C_BQKS = C_BQK + HEADS + KV_HEADS
N_COLS = C_BQKS + HEADS + KV_HEADS
Z_IDENT, Z_MASK, Z_PAIR, Z_RANK, Z_BASE = 0, P, 2 * P, 3 * P, 3 * P + 1
Z_YBASE = Z_BASE + ST
N_CONSTS = Z_YBASE + ST


def after(engine, sem, n):
    if isinstance(n, int) and n <= 0:
        return
    engine.wait_ge(sem, n)


def apart(engine, sem, n, passed):
    engine.wait_ge(sem, n)
    engine.sem_inc(passed, 1)


def build(nc, x_t, x_rows, cond_t, w3, wstream, cols, rows, shape_consts, angles, out):
    f32, f32r, bf16, u32 = mybir.dt.float32, mybir.dt.float32r, mybir.dt.bfloat16, mybir.dt.uint32
    ALU, ACT, AX = mybir.AluOpType, mybir.ActivationFunctionType, mybir.AxisListType.X

    PAIR = 2 * SEQ
    y_first = nc.dram_tensor("y_first", [PAIR, D], f32).ap()
    y_middle = nc.dram_tensor("y_middle", [2 * PAIR, D], f32).ap()
    y_last = nc.dram_tensor("y_last", [PAIR, D], f32).ap()
    y_of = [y_first, y_middle, y_middle, y_last]
    base_rows = nc.dram_tensor("base_rows", [S, D], f32).ap()

    ctx = ExitStack()
    with ctx:
        K = 256
        plain = ctx.enter_context(nc.sbuf_tensor("plain", [P, 76 * K], f32))
        split = ctx.enter_context(nc.sbuf_tensor("split", [P, 128 * K], f32r))
        ident_r = ctx.enter_context(nc.sbuf_tensor("ident_r", [P, P], f32r))
        mask_r = ctx.enter_context(nc.sbuf_tensor("mask_r", [P, P], f32r))
        consts = ctx.enter_context(nc.sbuf_tensor("consts", [P, N_CONSTS], f32))
        col = ctx.enter_context(nc.sbuf_tensor("col", [P, N_COLS], f32))
        small = ctx.enter_context(nc.sbuf_tensor("small", [P, 208], f32))
        idx = ctx.enter_context(nc.sbuf_tensor("idx", [P, 3 * ST], u32))
        psum = ctx.enter_context(nc.psum_tensor("psum", [P, 8, 512], f32))

        def kib(a, b):
            return plain[:, a * K:b * K]

        def skib(a, b):
            return split[:, int(a * K):int(b * K)]

        xT = kib(0, 8).rearrange("p (s n) -> p s n", s=4)
        xrow = kib(8, 24).rearrange("p (s n) -> p s n", s=TT)
        y = kib(24, 32).rearrange("p (s n) -> p s n", s=2)
        w3_sb = kib(32, 48).rearrange("p (k n) -> p k n", k=COND // P)
        ysel = kib(32, 40).rearrange("p (s n) -> p s n", s=2)
        hs = kib(40, 44)
        rank_a, rank_b = plain[:, 40 * K:42 * K], plain[:, 42 * K:44 * K]
        hfull = kib(44, 48).rearrange("p (k n) -> p k n", k=KC)
        bias_row = kib(48, 52)
        wr_row = kib(52, 56)
        cosT, sinT = kib(56, 58), kib(58, 60)
        junk = kib(60, 62).bitcast(bf16)
        junk_sum = kib(62, 63).bitcast(bf16)
        ang = kib(63, 64)
        raw = kib(64, 76).rearrange("p (s n) -> p s n", s=3)
        prob_all = kib(0, 5)
        k_rope = kib(6, 8)
        V = kib(8, 24).rearrange("p (i n) -> p i n", i=ST)
        attn = kib(24, 56).rearrange("p (h n) -> p h n", h=HEADS)
        q_rope, sin_term = kib(60, 62), kib(62, 64)
        ysel4 = [kib(0, 4), kib(4, 8), kib(48, 52), kib(52, 56)]
        x1 = kib(8, 24).rearrange("p (i n) -> p i n", i=ST)
        h2s = kib(24, 28)
        h2full = kib(28, 32).rearrange("p (k n) -> p k n", k=KC)
        xsel = kib(32, 48).rearrange("p (i n) -> p i n", i=ST)
        m = kib(0, 64).rearrange("p (f n) -> p f n", f=FT)
        silu_g = kib(72, 76).rearrange("p (s n) -> p s n", s=2)
        base = kib(0, 16).rearrange("p (i n) -> p i n", i=ST)

        w8 = skib(0, 64).rearrange("p (s q n) -> p s q n", s=KC, q=2)
        xx = skib(64, 128).rearrange("p (b k q n) -> p b k q n", b=2, k=KC, q=2)
        hT = skib(64, 96).rearrange("p (k q n) -> p k q n", k=KC, q=2)
        w4 = skib(96, 128).rearrange("p (s q n) -> p s q n", s=4, q=2)
        k_hl = skib(0, 4).rearrange("p (q n) -> p q n", q=2)
        q_hl = skib(4, 8).rearrange("p (q n) -> p q n", q=2)
        v_hl = skib(8, 12).rearrange("p (q i n) -> p q i n", q=2, i=ST)
        pT = skib(12, 28).rearrange("p (j q n) -> p j q n", j=ST, q=2)
        attn_hl = skib(28, 60).rearrange("p (s q n) -> p s q n", s=8, q=2)
        m_hl = skib(0, 16).rearrange("p (s q n) -> p s q n", s=4, q=2)

        ident = consts[:, Z_IDENT:Z_IDENT + P]
        qe = small[:, 0:KC * BATCH].rearrange("p (k b) -> p k b", b=BATCH)
        vs = small[:, 64:80].rearrange("p (b k) -> p b k", b=2)
        sc = small[:, 80:88].rearrange("p (j b) -> p j b", b=2)
        top8 = small[:, 112:120]
        idxf = small[:, 120:124]
        ssq, rt, rs, na = small[:, 124:128], small[:, 128:132], small[:, 132:136], small[:, 136:140]
        sels = small[:, 140:144]
        mx, nmx = small[:, 144:148], small[:, 148:152]
        lsum, rl = small[:, 152:156], small[:, 156:160]
        gate, ungate = small[:, 160:164], small[:, 164:168]
        ms = small[:, 168:172]
        condT = small[:, 176:208].rearrange("p (k b) -> p k b", b=BATCH)

        def sem(name):
            return ctx.enter_context(nc.semaphore(name))

        d_consts, d_cols, d_cond, d_w3, d_b2, d_wr, d_bv = (sem(n) for n in (
            "d_consts", "d_cols", "d_cond", "d_w3", "d_b2", "d_wr", "d_bv"))
        d_xT = [sem(f"d_xT{s}") for s in range(4)]
        d_x = [sem(f"d_x{s}") for s in range(TT)]
        d_y = [sem(f"d_y{s}") for s in range(2)]
        d_out = [sem(f"d_out{s}") for s in range(TT)]
        d_raw2 = [sem(f"d_raw2_{s}") for s in range(2)]
        d_raw3 = [sem(f"d_raw3_{s}") for s in range(3)]
        d_raw = [sem(f"d_raw{s}") for s in range(2)]
        d_ysel = [sem(f"d_ysel{s}") for s in range(ST)]
        d_ang = [sem(f"d_ang{s}") for s in range(ST)]
        d_ysel4 = [sem(f"d_ysel4_{s}") for s in range(ST)]
        d_xsel = [sem(f"d_xsel{s}") for s in range(ST)]
        d_base = sem("d_base")
        d_baseld = [sem(f"d_baseld{s}") for s in range(ST)]
        d_fin = sem("d_fin")
        dve_passed, pool_passed = sem("dve_passed"), sem("pool_passed")
        qe_mm, qe_b, qe_done = sem("qe_mm"), sem("qe_b"), sem("qe_done")
        const_r = sem("const_r")
        x_sum, x_mod, x_hi, x_lo = sem("x_sum"), sem("x_mod"), sem("x_hi"), sem("x_lo")
        w_hi, w_lo = sem("w_hi"), sem("w_lo")
        w2_used, wv_used, w_used = sem("w2_used"), sem("wv_used"), sem("w_used")
        y_mm, y_biased, y_relu, y_score, out_row = (sem(n) for n in (
            "y_mm", "y_biased", "y_relu", "y_score", "out_row"))
        score_T, top_max, top_cut, top_mask, top_rank, rank_bc = (sem(n) for n in (
            "score_T", "top_max", "top_cut", "top_mask", "top_rank", "rank_bc"))
        idx_f, idx_u = sem("idx_f"), sem("idx_u")
        h_sq, h_ms, h_rt, h_chain, h_rs, h_sel, h_norm = (sem(n) for n in (
            "h_sq", "h_ms", "h_rt", "h_chain", "h_rs", "h_sel", "h_norm"))
        h_T, h_full, h_hi, h_lo, ang_T, ang_sb = (sem(n) for n in (
            "h_T", "h_full", "h_hi", "h_lo", "ang_T", "ang_sb"))
        v_mm, v_sb, v_hi, v_lo = sem("v_mm"), sem("v_sb"), sem("v_hi"), sem("v_lo")
        k_mm, k_sum, k_hi, k_lo = sem("k_mm"), sem("k_sum"), sem("k_hi"), sem("k_lo")
        q_mm, q_sum, q_hi, q_lo = sem("q_mm"), sem("q_sum"), sem("q_hi"), sem("q_lo")
        rope_c, rope_s = sem("rope_c"), sem("rope_s")
        s_mm, s_max, s_nmax, s_exp, s_rl, s_prob = (sem(n) for n in (
            "s_mm", "s_max", "s_nmax", "s_exp", "s_rl", "s_prob"))
        p_T, p_hi, p_lo, pv_mm, o_sb = sem("p_T"), sem("p_hi"), sem("p_lo"), sem("pv_mm"), sem("o_sb")
        a_hi, a_lo, wo_mm, x1_sb = sem("a_hi"), sem("a_lo"), sem("wo_mm"), sem("x1_sb")
        g_sig, g_un, g_mix, g_base = sem("g_sig"), sem("g_un"), sem("g_mix"), sem("g_base")
        n_sq, n_ms, n_rt, n_chain, n_rs, n_norm = (sem(n) for n in (
            "n_sq", "n_ms", "n_rt", "n_chain", "n_rs", "n_norm"))
        n_T, n_full, n_hi, n_lo = sem("n_T"), sem("n_full"), sem("n_hi"), sem("n_lo")
        g_silu, m_sb, m_hi, m_lo, dn_mm, fin = (sem(n) for n in (
            "g_silu", "m_sb", "m_hi", "m_lo", "dn_mm", "fin"))

        def bank(b, n=512):
            return psum[:, b, 0:n]

        def pair(b):
            return psum[:, b:b + 2, :].rearrange("p b n -> p (b n)")

        def as_f32(ap):
            return ap.bitcast(f32)

        TILE_ORDER = (0, 2, 1, 3)

        def score_ps_of(i, a=0, b=None):
            at = (0, 0, P, 0)[i]
            return psum[:, (0, 1, 0, 2)[i], at + a:at + ((i + 1) * P if b is None else b)]

        def prob(i, a=0, b=None):
            at = i * (i + 1) // 2 * P
            return prob_all[:, at + a:at + ((i + 1) * P if b is None else b)]

        def row(ap, i):
            return ap[:, bass.ds(i, 1), :].rearrange("p a n -> p (a n)")

        block = ctx.enter_context(nc.Block())

        @block.sync
        def _(sp):
            def load_w(n, slot, slot_sem):
                sp.dma_start(raw[:, slot, :], wstream[n]).then_inc(slot_sem, 16)

            def load_xT(b, kc):
                c = b * KC + kc
                after(sp, x_lo, c - 3)
                sp.dma_start(xT[:, kc % 4, :], x_t[c]).then_inc(d_xT[kc % 4], 16)

            def load_x(b, j):
                sp.dma_start(xrow[:, j, :], x_rows[bass.ds((b * TT + j) * P, P), :]).then_inc(d_x[j], 16)

            sp.dma_start(condT, cond_t).then_inc(d_cond, 16)
            sp.dma_start(col[:], cols).then_inc(d_cols, 16)
            sp.dma_start(w3_sb, w3.rearrange("(k p) n -> p k n", p=P)).then_inc(d_w3, 16)
            for kc in range(4):
                load_xT(0, kc)
            load_w(0, 0, d_raw2[0])
            load_w(1, 1, d_raw2[1])
            sp.dma_start(consts[:], shape_consts).then_inc(d_consts, 16)
            for n in range(2, KC):
                if n < 6:
                    load_xT(0, n + 2)
                sp.wait_ge(w_hi, n - 1)
                sp.wait_ge(w_lo, n - 1)
                load_w(n, n % 2, d_raw2[n % 2])
            sp.dma_start(bias_row, rows[0:1, :].broadcast_to([P, D])).then_inc(d_b2, 16)
            sp.dma_start(wr_row, rows[1:2, :].broadcast_to([P, D])).then_inc(d_wr, 16)
            for j in range(TT):
                load_x(0, j)

            def window(b, last=False):
                if not last:
                    for kc in range(KC):
                        load_xT(b + 1, kc)
                for j in range(TT):
                    t = b * TT + j
                    sp.wait_ge(out_row, t + 1)
                    sp.dma_start(out[bass.ds(t * P, P), :], xrow[:, j, :]).then_inc(d_out[j], 16)
                    if not last and j >= 1:
                        sp.wait_ge(d_out[j - 1], 16 * b + 16)
                        load_x(b + 1, j - 1)
                if not last:
                    sp.wait_ge(d_out[TT - 1], 16 * b + 16)
                    load_x(b + 1, TT - 1)

            window(0)
            with sp.Fori(1, BATCH - 1) as b:
                window(b)
            for n in range(W_V, W_V + 2):
                sp.wait_ge(w_hi, n - 1)
                sp.wait_ge(w_lo, n - 1)
                load_w(n, n % 2, d_raw2[n % 2])
            window(BATCH - 1, last=True)
            sp.wait_ge(y_biased, BATCH * TT)
            sp.dma_start(bias_row, rows[2:3, :].broadcast_to([P, D])).then_inc(d_bv, 16)
            for n in range(W_V + 2, W_QK):
                sp.wait_ge(w_hi, n - 1)
                sp.wait_ge(w_lo, n - 1)
                load_w(n, n % 2, d_raw2[n % 2])
            for u, need in ((0, W_QK - 1), (1, W_QK), (2, 0)):
                after(sp, w_hi, need)
                after(sp, w_lo, need)
                load_w(W_QK + u, u, d_raw3[u])
            with sp.Fori(1, KV_HEADS) as g:
                for u in range(3):
                    sp.wait_ge(w_hi, W_QK + 3 * (g - 1) + u + 1)
                    sp.wait_ge(w_lo, W_QK + 3 * (g - 1) + u + 1)
                    load_w(W_QK + 3 * g + u, u, d_raw3[u])
            for s in range(2):
                sp.wait_ge(w_hi, W_O - 2 + s)
                sp.wait_ge(w_lo, W_O - 2 + s)
                load_w(W_O + s, s, d_raw[s])
            with sp.Fori(1, (W_END - W_O) // 2) as k:
                for s in range(2):
                    sp.wait_ge(w_hi, W_O + 2 * k + s - 1)
                    sp.wait_ge(w_lo, W_O + 2 * k + s - 1)
                    load_w(W_O + 2 * k + s, s, d_raw[s])
            for j in range(TT):
                sp.wait_ge(d_out[j], 16 * BATCH)
            sp.wait_ge(d_fin, 16 * ST)

        @block.tensor
        def _(pe):
            def three(out_ap, w_hl, x_hl, start, stop):
                nc.tensor.matmul(out_ap, w_hl[0], x_hl[0], start=start, stop=False, skip_group_check=True)
                nc.tensor.matmul(out_ap, w_hl[0], x_hl[1], start=False, stop=False, skip_group_check=True)
                return nc.tensor.matmul(out_ap, w_hl[1], x_hl[0], start=False, stop=stop, skip_group_check=True)

            pe.wait_ge(d_cond, 16)
            pe.wait_ge(d_w3, 16)
            for mo in range(KC):
                for kc in range(COND // P):
                    last = nc.tensor.matmul(psum[:, 7, mo * BATCH:(mo + 1) * BATCH],
                                            w3_sb[:, kc, mo * P:(mo + 1) * P], condT[:, kc, :],
                                            start=(kc == 0), stop=(kc == COND // P - 1),
                                            skip_group_check=True)
            last.then_inc(qe_mm, 1)

            def y_tile(t, p, j, chunks, final=False):
                after(pe, y_biased, t - 1)
                for kc in range(KC):
                    if j == 0:
                        pe.wait_ge(x_lo, chunks + kc + 1)
                    if isinstance(t, int) and t == 0:
                        pe.wait_ge(w_lo, kc + 1)
                    xa = xx[:, p, kc, 0, j * P:(j + 1) * P]
                    xb = xx[:, p, kc, 1, j * P:(j + 1) * P]
                    for half in range(2):
                        o = bank(2 * (j % 2) + half)
                        cut = slice(half * 512, half * 512 + 512)
                        last = three(o, (xa, xb), (w8[:, kc, 0, cut], w8[:, kc, 1, cut]),
                                     kc == 0, kc == KC - 1)
                    if final:
                        last.then_inc(w2_used, 1)
                if not final:
                    last.then_inc(y_mm, 1)

            def score_rows(k):
                pe.wait_ge(y_score, 2 * TT * (k + 1))
                after(pe, top_mask, k)
                for j in range(TT):
                    last = nc.tensor.transpose(psum[0:2, 4, j * P:(j + 1) * P],
                                               sc[:, j, :], ident)
                last.then_inc(score_T, 1)

            def spread_ranks(k):
                pe.wait_ge(top_rank, k + 1)
                nc.tensor.matmul(bank(5), consts[0:2, Z_PAIR:Z_PAIR + P], rank_b[0:2, :],
                                 start=True, stop=True, skip_group_check=True).then_inc(rank_bc, 1)

            def routed_T(k, ang_bank):
                pe.wait_ge(d_ang[k], 16)
                after(pe, ang_sb, k)
                for q in range(2):
                    last = nc.tensor.transpose(psum[:, ang_bank, q * P:(q + 1) * P],
                                               ang[:, q * P:(q + 1) * P], ident)
                last.then_inc(ang_T, 1)
                pe.wait_ge(h_norm, k + 1)
                after(pe, h_full, k)
                for kc in range(KC):
                    last = nc.tensor.transpose(psum[:, 4 + kc // 4, (kc % 4) * P:(kc % 4 + 1) * P],
                                               hs[:, kc * P:(kc + 1) * P], ident)
                last.then_inc(h_T, 1)

            def windows(i):
                first, end = isinstance(i, int) and i == 0, isinstance(i, int) and i == ST - 1
                for p in range(2):
                    for j in range(TT):
                        t = i * 2 * TT + p * TT + j
                        y_tile(t, p, j, (i * 2 + p) * KC, final=end and p == 1 and j == TT - 1)
                        if not first and p == 0 and j == 0:
                            score_rows(i - 1)
                        if not first and p == 0 and j == TT - 1:
                            spread_ranks(i - 1)
                        if end and p == 1 and j > 0:
                            routed_T(j - 1, 6)

            pe.wait_ge(d_consts, 16)
            windows(0)
            with pe.Fori(1, ST - 1) as i:
                windows(i)
            windows(ST - 1)

            def v_part(i, kc, banks):
                for half in range(2):
                    cut = slice(half * 512, half * 512 + 512)
                    last = three(bank(banks + half),
                                 (hT[:, kc, 0, i * P:(i + 1) * P], hT[:, kc, 1, i * P:(i + 1) * P]),
                                 (w8[:, kc, 0, cut], w8[:, kc, 1, cut]), kc == 0, kc == KC - 1)
                return last

            for kc in range(KC):
                pe.wait_ge(w_lo, W_V + kc + 1)
                if kc == 0:
                    pe.wait_ge(y_biased, BATCH * TT)
                    pe.wait_ge(h_lo, 2)
                for i in range(2):
                    last = v_part(i, kc, 2 * i)
                    if kc == KC - 1:
                        last.then_inc(v_mm, 1)
                if kc == 0:
                    pe.wait_ge(h_full, ST - 1)
                    score_rows(ST - 1)
                if kc == 5:
                    spread_ranks(ST - 1)
            pe.wait_ge(h_lo, 3)
            pe.wait_ge(ang_sb, 3)
            for kc in range(KC):
                last = v_part(2, kc, 6)
            last.then_inc(v_mm, 1)
            pe.wait_ge(v_sb, 2)
            routed_T(ST - 1, 3)
            pe.wait_ge(h_lo, ST)
            for kc in range(KC):
                last = v_part(3, kc, 0)
                last.then_inc(wv_used, 1)

            def project(slot, b, kcs):
                for kc in kcs:
                    wt = [w4[:, slot, q, kc * P:(kc + 1) * P] for q in range(2)]
                    last = three(bank(b), wt, (hT[:, kc, 0, :], hT[:, kc, 1, :]), kc == 0, kc == KC - 1)
                return last

            def scores(h):
                pe.wait_ge(q_lo, h + 1)
                for i in TILE_ORDER:
                    n = (i + 1) * P
                    qt = [q_hl[:, q, i * P:(i + 1) * P] for q in range(2)]
                    three(score_ps_of(i), qt, (k_hl[:, 0, 0:n], k_hl[:, 1, 0:n]), True, False)
                    last = nc.tensor.matmul(score_ps_of(i, n - P, n), ident_r[:], mask_r[:], start=False, stop=True,
                                            skip_group_check=True)
                    if i > 0:
                        last.then_inc(s_mm, 1)

            def flip(h, j):
                if j == 0:
                    pe.wait_ge(s_prob, (h + 1) * ST)
                after(pe, p_lo, h * ST + j - 1)
                for i in range(j, ST):
                    last = nc.tensor.transpose(psum[:, 4 + j % 2, i * P:(i + 1) * P],
                                               prob(i, j * P, (j + 1) * P), ident)
                last.then_inc(p_T, 1)

            def weigh(h, j):
                pe.wait_ge(p_lo, h * ST + j + 1)
                vt = [v_hl[:, q, j, :] for q in range(2)]
                last = three(psum[:, 6, j * P:], vt, (pT[:, j, 0, j * P:], pT[:, j, 1, j * P:]),
                             j == 0, j == ST - 1)
                last.then_inc(pv_mm, 1)

            def wo_part(h, b, slot, first=False, final=False):
                i, cut = b // 2, slice((b % 2) * 512, (b % 2) * 512 + 512)
                at = [attn_hl[:, slot, q, i * P:(i + 1) * P] for q in range(2)]
                return three(bank(b), at, (w4[:, slot % 4, 0, cut], w4[:, slot % 4, 1, cut]), first, final)

            def next_keys(g, side, part):
                if side == 1 and part == 0:
                    pe.wait_ge(w_lo, W_QK + 3 * g + 6)
                    pe.wait_ge(rope_s, 2 * (3 * g + 4))
                kc = (4 if side == 0 else 0) + 2 * part
                last = project(2, 3, (kc, kc + 1))
                if side == 0 and part == 1:
                    last.then_inc(k_mm, 1)

            def half(g, side, keys=True, query=True, score=True, fill=None):
                h = g * 2 + side
                flip(h, 0)
                flip(h, 1)
                if keys:
                    next_keys(g, side, 0)
                if fill:
                    fill(0)
                if side == 0:
                    pe.wait_ge(v_lo, g + 1)
                after(pe, o_sb, h)
                weigh(h, 0)
                flip(h, 2)
                if keys:
                    next_keys(g, side, 1)
                if fill:
                    fill(1)
                weigh(h, 1)
                flip(h, 3)
                if score:
                    if side == 1:
                        pe.wait_ge(k_lo, g + 2)
                    scores(h + 1)
                if fill:
                    fill(2)
                weigh(h, 2)
                weigh(h, 3)
                if query:
                    u, slot = (3 * g + 4, 1) if side == 0 else (3 * g + 6, 0)
                    if side == 1 and not keys:
                        u, slot = 3 * g + 5, 2
                    pe.wait_ge(w_lo, W_QK + u + 1)
                    pe.wait_ge(rope_s, 2 * (3 * g + 3 + 2 * side))
                    project(slot, 7, range(KC)).then_inc(q_mm, 1)

            pe.wait_ge(h_full, ST)
            pe.wait_ge(ang_sb, ST)
            pe.wait_ge(w_lo, W_QK + 1)
            project(0, 3, range(KC)).then_inc(k_mm, 1)
            pe.wait_ge(v_sb, 3)
            pe.wait_ge(w_lo, W_QK + 2)
            project(1, 7, range(KC)).then_inc(q_mm, 1)
            pe.wait_ge(w_lo, W_QK + 3)
            pe.wait_ge(rope_s, 2)
            project(2, 3, range(4))
            pe.wait_ge(v_sb, ST)
            pe.wait_ge(const_r, 2)
            pe.wait_ge(k_lo, 1)
            scores(0)
            pe.wait_ge(w_lo, W_QK + 4)
            pe.wait_ge(rope_s, 4)
            project(0, 7, range(KC)).then_inc(q_mm, 1)
            half(0, 0)
            half(0, 1)
            with pe.Fori(1, KV_HEADS - 2) as g:
                half(g, 0)
                half(g, 1)
            half(KV_HEADS - 2, 0)
            half(KV_HEADS - 2, 1, keys=False)

            half(KV_HEADS - 1, 0, keys=False, query=False)
            for h in range(4):
                pe.wait_ge(w_lo, W_O + h + 1)
                pe.wait_ge(a_lo, h + 1)
                for b in (3, 7):
                    wo_part(h, b, h, first=(h == 0))

            def fill_banks(b):
                for h in range(4):
                    wo_part(h, b, h, first=(h == 0))

            half(KV_HEADS - 1, 1, keys=False, query=False, score=False, fill=fill_banks)
            for h in range(4):
                for b in (4, 5, 6):
                    if h == 0 and b == 6:
                        pe.wait_ge(o_sb, HEADS)
                    last = wo_part(h, b, h, first=(h == 0))
                last.then_inc(w_used, 1)

            def wo_head(h, slot):
                pe.wait_ge(w_lo, W_O + h + 1)
                pe.wait_ge(a_lo, h + 1)
                for b in range(8):
                    last = wo_part(h, b, slot)
                last.then_inc(w_used, 1)

            for h in range(4, 12):
                wo_head(h, h % 8)

            def norm_T(i):
                pe.wait_ge(n_norm, i + 1)
                for kc in range(KC):
                    last = nc.tensor.transpose(psum[:, 2 * i + kc // 4, (kc % 4) * P:(kc % 4 + 1) * P],
                                               h2s[:, kc * P:(kc + 1) * P], ident)
                last.then_inc(n_T, 1)

            for i in range(ST):
                for h in range(12, HEADS):
                    if i == 0:
                        pe.wait_ge(w_lo, W_O + h + 1)
                        pe.wait_ge(a_lo, h + 1)
                    for b in (2 * i, 2 * i + 1):
                        last = wo_part(h, b, h % 8, final=(h == HEADS - 1))
                    if i == ST - 1:
                        last.then_inc(w_used, 1)
                if i < ST - 1:
                    last.then_inc(wo_mm, 1)
                if i > 0:
                    norm_T(i - 1)

            def ffn_part(s, cols=slice(0, S)):
                for kc in range(KC):
                    wt = [w4[:, s, q, kc * P:(kc + 1) * P] for q in range(2)]
                    last = three(psum[:, s, cols], wt, (hT[:, kc, 0, cols], hT[:, kc, 1, cols]),
                                 kc == 0, kc == KC - 1)
                return last

            def ffn_tile(f, odd):
                for gu in range(2):
                    pe.wait_ge(w_lo, W_GU + f * 2 + gu + 1)
                    pe.wait_ge(m_sb, f - 1)
                    ffn_part(2 * odd + gu).then_inc(w_used, 1)

            pe.wait_ge(n_full, 2)
            pe.wait_ge(n_lo, 2)
            for s in range(4):
                pe.wait_ge(w_lo, W_GU + s + 1)
                ffn_part(s, slice(0, S // 2))
                if s == 1:
                    norm_T(ST - 1)
            pe.wait_ge(n_lo, ST)
            for s in range(4):
                ffn_part(s, slice(S // 2, S)).then_inc(w_used, 1)
            with pe.Fori(1, FT // 2) as k:
                ffn_tile(k * 2, 0)
                ffn_tile(k * 2 + 1, 1)

            def down_tile(f, s, first=False, final=False):
                pe.wait_ge(w_lo, W_DOWN + f + 1)
                pe.wait_ge(m_lo, f + 1)
                order = (2, 3, 0, 1) if first else range(ST)
                for i in order:
                    if first and i == 0:
                        pe.wait_ge(m_sb, FT)
                    mt = [m_hl[:, s, q, i * P:(i + 1) * P] for q in range(2)]
                    for half in range(2):
                        cut = slice(half * 512, half * 512 + 512)
                        last = three(bank(2 * i + half), mt, (w4[:, s, 0, cut], w4[:, s, 1, cut]),
                                     first, final)
                    if final and i < ST - 1:
                        last.then_inc(dn_mm, 1)
                last.then_inc(w_used, 1)

            for s in range(4):
                down_tile(s, s, first=(s == 0))
            with pe.Fori(1, FT // 4 - 1) as k:
                for s in range(4):
                    down_tile(k * 4 + s, s)
            for s in range(4):
                down_tile(FT - 4 + s, s, final=(s == 3))

        @block.scalar
        def _(act):
            act.preload_act_table(ACT.Sqrt)

            def w_part(n, raw_slot, landed, count, dst, free=None, used=0):
                act.wait_ge(landed, count)
                if free is not None:
                    act.wait_ge(free, used)
                nc.scalar.activation(dst, raw[:, raw_slot, :], ACT.Copy).then_inc(w_hi, 1)

            def x_chunks(b, p, kcs, gemm_done):
                for kc in kcs:
                    c = b * KC + kc
                    act.wait_ge(d_xT[kc % 4], 16 * (2 * b + kc // 4) + 16)
                    after(act, x_sum, c)
                    nc.scalar.activation(junk_sum[:, 0:SEQ], xT[:, kc % 4, :], ACT.Identity,
                                         scale=1.0 / SEQ, accum_out=vs[:, p, kc:kc + 1]).then_inc(x_sum, 1)
                for kc in kcs:
                    c = b * KC + kc
                    act.wait_ge(x_mod, c + 1)
                    after(act, y_mm, gemm_done)
                    nc.scalar.activation(xx[:, p, kc, 0, :], xT[:, kc % 4, :], ACT.Copy).then_inc(x_hi, 1)

            def y_out(t, j, dst, row):
                act.wait_ge(y_biased, t + 1)
                nc.scalar.activation(y[:, j % 2, :], y[:, j % 2, :], ACT.Relu).then_inc(y_relu, 1)
                act.wait_ge(y_relu, t + 1)
                act.dma_start(dst[bass.ds(row, P), :], y[:, j % 2, :]).then_inc(d_y[j % 2], 16)

            def routed(k):
                act.wait_ge(d_ysel[k], 16)
                if k == 0:
                    act.wait_ge(rank_bc, ST - 1)
                after(act, h_T, k)
                nc.scalar.activation(hs, ysel[:, k % 2, :], ACT.Square, accum_out=ssq[:, k:k + 1]).then_inc(h_sq, 1)
                act.wait_ge(h_ms, k + 1)
                nc.scalar.activation(rt[:, k:k + 1], ms[:, k:k + 1], ACT.Sqrt).then_inc(h_rt, 1)

            def routed_split(k):
                act.wait_ge(ang_T, k + 1)
                b = 3 if k == ST - 1 else 6
                nc.scalar.activation(cosT[:, k * P:(k + 1) * P], psum[:, b, 0:P], ACT.Copy)
                nc.scalar.activation(sinT[:, k * P:(k + 1) * P], psum[:, b, P:2 * P], ACT.Copy).then_inc(ang_sb, 1)
                act.wait_ge(h_full, k + 1)
                nc.scalar.activation(hT[:, :, 0, k * P:(k + 1) * P], hfull, ACT.Copy).then_inc(h_hi, 1)

            for kc in range(0, KC, 2):
                x_chunks(0, 0, (kc, kc + 1), 0)
                for n in (kc, kc + 1):
                    w_part(n, n % 2, d_raw2[n % 2], 16 * (n // 2) + 16, w8[:, n, 0, :])
            act.wait_ge(d_consts, 16)
            nc.scalar.activation(ident_r[:], ident, ACT.Copy).then_inc(const_r, 1)
            nc.scalar.activation(mask_r[:], consts[:, Z_MASK:Z_MASK + P], ACT.Copy).then_inc(const_r, 1)

            def windows(i):
                end = isinstance(i, int) and i == ST - 1
                for p in range(2):
                    b = i * 2 + p
                    for j in range(TT):
                        if not (end and p == 1):
                            x_chunks(b + 1, 1 - p, (2 * j, 2 * j + 1), b * TT)
                        elif j == 0:
                            act.wait_ge(y_mm, b * TT)
                        row = (p * TT + j) * P
                        if end:
                            y_out(b * TT + j, j, y_last, row)
                        elif isinstance(i, int):
                            y_out(b * TT + j, j, y_first, row)
                        else:
                            y_out(b * TT + j, j, y_middle, (i - 1) * PAIR + row)
                        if end and p == 1:
                            if j > 0:
                                routed_split(j - 1)
                            if j < TT - 1:
                                routed(j)

            windows(0)
            with act.Fori(1, ST - 1) as i:
                windows(i)
            windows(ST - 1)

            for kc in range(KC):
                n = W_V + kc
                w_part(n, n % 2, d_raw2[n % 2], 16 * (n // 2) + 16, w8[:, kc, 0, :], w2_used, kc + 1)
            for u in range(3):
                w_part(W_QK + u, u, d_raw3[u], 16, w4[:, u, 0, :], w2_used, KC)
            routed(3)
            routed_split(3)

            act.preload_act_table(ACT.Exp)

            def exponentials(h):
                after(act, p_T, h * ST)
                for c, i in enumerate(TILE_ORDER):
                    if c % 2 == 0:
                        act.wait_ge(s_nmax, 2 * h + c // 2 + 1)
                    nc.scalar.activation(prob(i), score_ps_of(i), ACT.Exp, bias=nmx[:, c:c + 1],
                                         scale=SCALE, accum_out=lsum[:, c:c + 1]).then_inc(s_exp, 1)

            def qk_weights(u, slot, landed, free, used):
                w_part(W_QK + u, slot, d_raw3[slot], landed, w4[:, slot, 0, :], free, used)

            def key_hi(g):
                act.wait_ge(k_sum, g + 1)
                after(act, s_mm, 3 * 2 * g)
                nc.scalar.activation(k_hl[:, 0, :], k_rope, ACT.Copy).then_inc(k_hi, 1)

            def query_hi(h):
                act.wait_ge(q_sum, h + 1)
                after(act, s_mm, 3 * h)
                nc.scalar.activation(q_hl[:, 0, :], q_rope, ACT.Copy).then_inc(q_hi, 1)

            def value_hi(g):
                after(act, pv_mm, g * 2 * ST)
                nc.scalar.activation(v_hl[:, 0, :, :], V[:, :, bass.ds(g * HD, HD)], ACT.Copy).then_inc(v_hi, 1)

            def prob_hi(h, j):
                act.wait_ge(p_T, h * ST + j + 1)
                after(act, pv_mm, h * ST)
                nc.scalar.activation(pT[:, j, 0, j * P:], psum[:, 4 + j % 2, j * P:], ACT.Copy).then_inc(p_hi, 1)

            def rest_part(n, s, first=None):
                k = n - W_O
                act.wait_ge(d_raw[s % 2], 8 * (k - s % 2) + 16)
                if first is None:
                    act.wait_ge(w_used, k - 3)
                else:
                    act.wait_ge(q_mm, first)
                nc.scalar.activation(w4[:, s, 0, :], raw[:, s % 2, :], ACT.Copy).then_inc(w_hi, 1)

            def attn_part(h, slot):
                act.wait_ge(o_sb, h + 1)
                if h >= 8:
                    act.wait_ge(w_used, h - 7)
                nc.scalar.activation(attn_hl[:, slot, 0, :], attn[:, h, :], ACT.Copy).then_inc(a_hi, 1)

            def half(g, side, before=None, behind=None, key=True, score=True, value=True):
                h = g * 2 + side
                prob_hi(h, 0)
                prob_hi(h, 1)
                if side == 1 and key:
                    key_hi(g + 1)
                if score:
                    query_hi(h + 1)
                prob_hi(h, 2)
                prob_hi(h, 3)
                if before:
                    before(g)
                if score:
                    exponentials(h + 1)
                act.wait_ge(pv_mm, (h + 1) * ST)
                nc.scalar.activation(row(attn, h), bank(6), ACT.Copy).then_inc(o_sb, 1)
                if side == 1 and value:
                    value_hi(g + 1)
                if behind:
                    behind(g)

            def weights_k(g):
                qk_weights(3 * g + 5, 2, 16 * g + 32, k_mm, g + 2)

            def weights_qb(g):
                qk_weights(3 * g + 6, 0, 16 * g + 48, q_mm, 2 * g + 2)

            def weights_qa(g):
                qk_weights(3 * g + 7, 1, 16 * g + 48, q_mm, 2 * g + 3)

            act.wait_ge(wv_used, KC)
            qk_weights(3, 0, 32, k_mm, 1)
            key_hi(0)
            query_hi(0)
            act.wait_ge(v_sb, ST)
            value_hi(0)
            exponentials(0)
            qk_weights(4, 1, 32, q_mm, 1)
            half(0, 0, weights_k, weights_qb)
            half(0, 1, None, weights_qa)
            with act.Fori(1, KV_HEADS - 2) as g:
                half(g, 0, weights_k, weights_qb)
                half(g, 1, None, weights_qa)

            def first_wo(g):
                for h in range(2):
                    rest_part(W_O + h, h, first=HEADS - 2 + h)
                    attn_part(h, h)
                for h in range(2, 4):
                    attn_part(h, h)

            def second_wo(g):
                for h in range(2, 4):
                    rest_part(W_O + h, h, first=HEADS)

            half(KV_HEADS - 2, 0, weights_k)
            half(KV_HEADS - 2, 1, None, first_wo)
            half(KV_HEADS - 1, 0, second_wo)
            half(KV_HEADS - 1, 1, key=False, score=False, value=False)

            for h in range(4, HEADS):
                rest_part(W_O + h, h % 4)
                attn_part(h, h % 8)
            act.preload_act_table(ACT.Sigmoid)
            nc.scalar.activation(gate, sels, ACT.Sigmoid).then_inc(g_sig, 1)
            act.preload_act_table(ACT.Sqrt)

            def squares(i):
                act.wait_ge(x1_sb, i + 1)
                after(act, n_sq, i)
                nc.scalar.activation(junk[:, 0:D], x1[:, i, :], ACT.Square, accum_out=ssq[:, i:i + 1]).then_inc(n_sq, 1)

            def root(i):
                act.wait_ge(n_ms, i + 1)
                nc.scalar.activation(rt[:, i:i + 1], ms[:, i:i + 1], ACT.Sqrt).then_inc(n_rt, 1)

            def norm_hi(i):
                act.wait_ge(n_full, i + 1)
                nc.scalar.activation(hT[:, :, 0, i * P:(i + 1) * P], h2full, ACT.Copy).then_inc(n_hi, 1)

            squares(0)
            root(0)
            squares(1)
            root(1)
            norm_hi(0)
            squares(2)
            root(2)
            norm_hi(1)
            for n in range(3):
                rest_part(W_GU + n, n)
            squares(3)
            rest_part(W_GU + 3, 3)
            root(3)
            norm_hi(2)
            norm_hi(3)

            act.preload_act_table(ACT.Silu)

            def ffn(f, odd, tail=False):
                act.wait_ge(w_used, HEADS + f * 2 + 1)
                after(act, m_sb, f - 1)
                nc.scalar.activation(silu_g[:, odd, :], bank(2 * odd), ACT.Silu).then_inc(g_silu, 1)
                rest_part(W_GU + f * 2 + 4, 2 * odd)
                rest_part(W_GU + f * 2 + 5, 2 * odd + 1)

            ffn(0, 0)
            ffn(1, 1)
            act.wait_ge(g_base, ST)
            act.dma_start(base_rows.rearrange("(i p) n -> p i n", p=P), xsel).then_inc(d_base, 16)
            with act.Fori(1, FT // 2 - 1) as k:
                ffn(k * 2, 0)
                ffn(k * 2 + 1, 1)

            def m_part(f, s):
                if not isinstance(f, int):
                    act.wait_ge(w_used, W_DOWN - W_O + f - 3)
                nc.scalar.activation(m_hl[:, s, 0, :], row(m, f), ACT.Copy).then_inc(m_hi, 1)

            for f in range(4):
                m_part(f, f)
            ffn(FT - 2, 0)
            ffn(FT - 1, 1)

            def down_parts(k):
                for s in range(4):
                    rest_part(W_DOWN + k * 4 + s, s)
                    m_part(k * 4 + s, s)

            with act.Fori(1, 3) as k:
                down_parts(k)
            act.wait_ge(m_lo, 8)
            act.wait_ge(m_hi, 8)
            for i in range(ST):
                act.dma_start(base[:, i, :], base_rows[i * P:(i + 1) * P, :]).then_inc(d_baseld[i], 16)
            with act.Fori(3, FT // 4) as k:
                down_parts(k)

        @block.gpsimd
        def _(pool):
            def w_part(n, raw_slot, dst_slot):
                pool.wait_ge(w_hi, n + 1)
                nc.gpsimd.tensor_tensor(dst_slot[:, 1, :], raw[:, raw_slot, :], as_f32(dst_slot[:, 0, :]),
                                        ALU.subtract).then_inc(w_lo, 1)

            def x_plus_y(b, j):
                t = b * TT + j
                pool.wait_ge(y_relu, t + 1)
                pool.wait_ge(d_x[j], 16 * b + 16)
                nc.gpsimd.tensor_tensor(xrow[:, j, :], xrow[:, j, :], y[:, j % 2, :], ALU.add).then_inc(out_row, 1)

            def gather_angles(k):
                pool.wait_ge(idx_u, 3 * (k + 1))
                after(pool, ang_T, k)
                pool.indirect_dma_start(ang, None, angles,
                                        bass.IndirectOffsetOnAxis(ap=idx[:, ST + k:ST + k + 1], axis=0)).then_inc(d_ang[k], 16)

            def gather(k):
                pool.wait_ge(idx_u, 3 * (k + 1))
                for s in range(2):
                    pool.wait_ge(d_y[s], 16 * TT * (k + 1))
                after(pool, h_norm, k - 1)
                after(pool, h_sel, k - 1)
                pool.indirect_dma_start(ysel[:, k % 2, :], None, y_of[k],
                                        bass.IndirectOffsetOnAxis(ap=idx[:, 2 * ST + k:2 * ST + k + 1], axis=0)).then_inc(d_ysel[k], 16)

            for n in range(KC):
                w_part(n, n % 2, w8[:, n])
            with pool.Fori(0, ST - 1) as i:
                for p in range(2):
                    for j in range(TT):
                        x_plus_y(i * 2 + p, j)
            b = BATCH - 2
            for p in range(2):
                for j in range(TT):
                    x_plus_y(b + p, j)
                    if p == 0 and j == 0:
                        gather_angles(0)
                        gather(0)
                        gather(1)
                    if p == 1 and j == 0:
                        gather(2)
                    if p == 1 and j in (1, 2):
                        gather_angles(j)
            for kc in range(KC):
                w_part(W_V + kc, kc % 2, w8[:, kc])
            gather(3)
            gather_angles(3)
            for u in range(3):
                w_part(W_QK + u, u, w4[:, u])

            def key_sum(g):
                pool.wait_ge(rope_s, 6 * g + 2)
                nc.gpsimd.tensor_tensor(k_rope, k_rope, sin_term, ALU.add).then_inc(k_sum, 1)

            def key_lo(g):
                pool.wait_ge(k_hi, g + 1)
                nc.gpsimd.tensor_tensor(k_hl[:, 1, :], k_rope, as_f32(k_hl[:, 0, :]), ALU.subtract).then_inc(k_lo, 1)

            def value_lo(g):
                pool.wait_ge(v_hi, g + 1)
                nc.gpsimd.tensor_tensor(v_hl[:, 1, :, :], V[:, :, bass.ds(g * HD, HD)], as_f32(v_hl[:, 0, :, :]),
                                        ALU.subtract).then_inc(v_lo, 1)

            def group(g, last=False):
                w_part(W_QK + 3 * g + 5, 2, w4[:, 2])
                key_sum(g + 1)
                if not last:
                    w_part(W_QK + 3 * g + 6, 0, w4[:, 0])
                key_lo(g + 1)
                value_lo(g + 1)
                if not last:
                    w_part(W_QK + 3 * g + 7, 1, w4[:, 1])

            key_sum(0)
            w_part(W_QK + 3, 0, w4[:, 0])
            key_lo(0)
            value_lo(0)
            w_part(W_QK + 4, 1, w4[:, 1])
            group(0)
            with pool.Fori(1, KV_HEADS - 2) as g:
                group(g)
            group(KV_HEADS - 2, last=True)

            def gather_rows(dst, src, c, landed):
                pool.indirect_dma_start(dst, None, src,
                                        bass.IndirectOffsetOnAxis(ap=idx[:, c:c + 1], axis=0)).then_inc(landed, 16)

            for s in range(4):
                w_part(W_O + s, s % 2, w4[:, s])
            pool.wait_ge(p_T, HEADS * ST)
            for k in range(2):
                gather_rows(ysel4[k], y_of[k], 2 * ST + k, d_ysel4[k])
            with pool.Fori(1, HEADS // 4) as k:
                for s in range(4):
                    w_part(W_O + k * 4 + s, s % 2, w4[:, s])
            pool.wait_ge(a_lo, HEADS)
            for k in (2, 3):
                gather_rows(ysel4[k], y_of[k], 2 * ST + k, d_ysel4[k])
            for k in range(ST):
                gather_rows(xsel[:, k, :], x_rows, k, d_xsel[k])
            with pool.Fori(0, (W_END - W_GU) // 4) as k:
                for s in range(4):
                    w_part(W_GU + k * 4 + s, s % 2, w4[:, s])
            for j in range(TT):
                pool.wait_ge(d_out[j], 16 * BATCH)
            for i in range(ST):
                pool.wait_ge(fin, i + 1)
                pool.indirect_dma_start(out, bass.IndirectOffsetOnAxis(ap=idx[:, i:i + 1], axis=0),
                                        base[:, i, :], None).then_inc(d_fin, 16)

        @block.vector
        def _(dve):
            dve.wait_ge(qe_mm, 1)
            dve.wait_ge(d_cols, 16)
            q_ps = psum[:, 7, 0:KC * BATCH].rearrange("p (k b) -> p k b", b=BATCH)
            b3 = col[:, C_B3:C_B3 + KC].rearrange("p (k a) -> p k a", a=1).broadcast_to([P, KC, BATCH])
            nc.vector.tensor_tensor(qe, q_ps, b3, ALU.add).then_inc(qe_b, 1)
            dve.wait_ge(qe_b, 1)
            nc.vector.tensor_scalar(qe, qe, 0.0, float(SEQ), ALU.max, ALU.mult).then_inc(qe_done, 1)
            dve.wait_ge(qe_done, 1)

            def x_chunks(b, p, kcs):
                for kc in kcs:
                    c = b * KC + kc
                    dve.wait_ge(x_sum, c + 1)
                    nc.vector.tensor_scalar(xT[:, kc % 4, :], xT[:, kc % 4, :], vs[:, p, kc:kc + 1],
                                            qe[:, kc, bass.ds(b, 1)], ALU.add, ALU.mult).then_inc(x_mod, 1)
                for kc in kcs:
                    c = b * KC + kc
                    dve.wait_ge(x_hi, c + 1)
                    nc.vector.tensor_tensor(xx[:, p, kc, 1, :], xT[:, kc % 4, :], as_f32(xx[:, p, kc, 0, :]),
                                            ALU.subtract).then_inc(x_lo, 1)

            def y_tile(i, p, j, final=False):
                b = i * 2 + p
                t, half = b * TT + j, 2 * b + j // 2
                if final:
                    dve.wait_ge(w2_used, KC)
                else:
                    dve.wait_ge(y_mm, t + 1)
                after(dve, d_y[j % 2], 16 * half)
                after(dve, y_score, t - 1)
                after(dve, out_row, t - 1)
                nc.vector.tensor_tensor(y[:, j % 2, :], pair(2 * (j % 2)), bias_row, ALU.add).then_inc(y_biased, 1)
                dve.wait_ge(y_relu, t + 1)
                after(dve, y_score, t)
                if p == 0 and j == 0:
                    after(dve, score_T, i)
                nc.vector.scalar_tensor_tensor(junk[:, 0:D], y[:, j % 2, :], 1.0, wr_row, ALU.mult, ALU.mult,
                                               accum_out=sc[:, j, p:p + 1]).then_inc(y_score, 1)

            score_ps = psum[0:2, 4, :]
            def top_rounds(k, rounds):
                for r in rounds:
                    src = score_ps if r == 0 else (rank_a, rank_b)[(r - 1) % 2][0:2, :]
                    dst = (rank_a, rank_b)[r % 2][0:2, :]
                    if r == 0:
                        after(dve, top_cut, k * 8)
                        apart(dve, score_T, k + 1, dve_passed)
                    else:
                        apart(dve, top_cut, k * 8 + r, dve_passed)
                    nc.vector.max(top8[0:2, :], src).then_inc(top_max, 1)
                    apart(dve, top_max, k * 8 + r + 1, dve_passed)
                    nc.vector.match_replace(dst, top8[0:2, :], src, LOWEST).then_inc(top_cut, 1)

            def top_ranks(k):
                dve.wait_ge(top_cut, k * 8 + 8)
                nc.vector.tensor_tensor(rank_a[0:2, :], rank_b[0:2, :], score_ps, ALU.not_equal).then_inc(top_mask, 1)
                dve.wait_ge(top_mask, k + 1)
                nc.vector.tensor_tensor_scan(rank_b[0:2, :], rank_a[0:2, :], rank_a[0:2, :], 0.0,
                                             ALU.add, ALU.max).then_inc(top_rank, 1)

            def top_index(k, scored):
                dve.wait_ge(rank_bc, k + 1)
                dve.wait_ge(y_score, scored)
                nc.vector.tensor_scalar(junk[:, 0:SEQ], bank(5), consts[:, Z_RANK:Z_RANK + 1], 0.0, ALU.is_le,
                                        ALU.add, accum_out=idxf[:, bass.ds(k, 1)]).then_inc(idx_f, 1)
                dve.wait_ge(idx_f, k + 1)
                nc.vector.tensor_scalar(idx[:, bass.ds(k, 1)], idxf[:, bass.ds(k, 1)],
                                        consts[:, bass.ds(Z_BASE + k, 1)], None, ALU.add).then_inc(idx_u, 1)
                nc.vector.tensor_copy(idx[:, bass.ds(ST + k, 1)], idxf[:, bass.ds(k, 1)]).then_inc(idx_u, 1)
                nc.vector.tensor_scalar(idx[:, bass.ds(2 * ST + k, 1)], idxf[:, bass.ds(k, 1)],
                                        consts[:, bass.ds(Z_YBASE + k, 1)], None, ALU.add).then_inc(idx_u, 1)

            def inverse_root(k, sq_sem, ms_sem, rt_sem, chain, done):
                a, r, q = ms[:, k:k + 1], rs[:, k:k + 1], na[:, k:k + 1]
                dve.wait_ge(sq_sem, k + 1)
                nc.vector.tensor_scalar(a, ssq[:, k:k + 1], 1.0 / D, EPS, ALU.mult, ALU.add).then_inc(ms_sem, 1)
                dve.wait_ge(rt_sem, k + 1)
                nc.vector.reciprocal(r, rt[:, k:k + 1]).then_inc(chain, 1)
                dve.wait_ge(chain, 3 * k + 1)
                nc.vector.scalar_tensor_tensor(q, r, a, r, ALU.mult, ALU.mult).then_inc(chain, 1)
                dve.wait_ge(chain, 3 * k + 2)
                nc.vector.tensor_scalar(q, q, -0.5, 1.5, ALU.mult, ALU.add).then_inc(chain, 1)
                dve.wait_ge(chain, 3 * k + 3)
                nc.vector.tensor_tensor(r, r, q, ALU.mult).then_inc(done, 1)

            def routed(k, scored):
                inverse_root(k, h_sq, h_ms, h_rt, h_chain, h_rs)
                dve.wait_ge(y_score, scored)
                dve.wait_ge(d_ysel[k], 16)
                after(dve, h_sel, k)
                nc.vector.scalar_tensor_tensor(junk[:, 0:D], ysel[:, k % 2, :], 1.0, wr_row, ALU.mult, ALU.mult,
                                               accum_out=sels[:, k:k + 1]).then_inc(h_sel, 1)
                dve.wait_ge(h_rs, k + 1)
                nc.vector.tensor_scalar(hs, ysel[:, k % 2, :], rs[:, k:k + 1], None, ALU.mult).then_inc(h_norm, 1)

            def routed_split(k):
                dve.wait_ge(h_T, k + 1)
                after(dve, h_lo, k)
                ln = col[:, C_LN1:C_LN1 + KC].rearrange("p (k a) -> p k a", a=1).broadcast_to([P, KC, P])
                h_ps = psum[:, 4:6, :].rearrange("p b (k n) -> p (b k) n", k=4)
                nc.vector.tensor_tensor(hfull, h_ps, ln, ALU.mult).then_inc(h_full, 1)
                dve.wait_ge(h_hi, k + 1)
                nc.vector.tensor_tensor(hT[:, :, 1, k * P:(k + 1) * P], hfull, as_f32(hT[:, :, 0, k * P:(k + 1) * P]),
                                        ALU.subtract).then_inc(h_lo, 1)

            for kc in range(0, KC, 2):
                x_chunks(0, 0, (kc, kc + 1))
            dve.wait_ge(d_b2, 16)
            dve.wait_ge(d_wr, 16)
            dve.wait_ge(d_consts, 16)

            def windows(i):
                first, end = isinstance(i, int) and i == 0, isinstance(i, int) and i == ST - 1
                for p in range(2):
                    b = i * 2 + p
                    for j in range(TT):
                        if not (end and p == 1):
                            x_chunks(b + 1, 1 - p, (2 * j, 2 * j + 1))
                        if not first and p == 0 and j > 0:
                            top_rounds(i - 1, ((), (0, 1, 2), (3, 4, 5), (6, 7))[j])
                        if not first and p == 0 and j == TT - 1:
                            top_ranks(i - 1)
                        if not first and p == 1 and j == 0:
                            top_index(i - 1, b * TT)
                        y_tile(i, p, j, final=end and p == 1 and j == TT - 1)
                        if end and p == 1:
                            if j > 0:
                                routed_split(j - 1)
                            if j < TT - 1:
                                routed(j, b * TT + j + 1)

            windows(0)
            with dve.Fori(1, ST - 1) as i:
                windows(i)
            windows(ST - 1)

            def v_out(i, banks):
                dve.wait_ge(d_bv, 16)
                for j in range(TT):
                    dve.wait_ge(d_out[j], 16 * BATCH)
                nc.vector.tensor_tensor(V[:, i, :], pair(banks), bias_row, ALU.add).then_inc(v_sb, 1)

            top_rounds(ST - 1, range(8))
            top_ranks(ST - 1)
            top_index(ST - 1, BATCH * TT)
            dve.wait_ge(v_mm, 1)
            v_out(0, 0)
            dve.wait_ge(v_mm, 2)
            v_out(1, 2)
            routed(3, BATCH * TT)
            routed_split(3)
            dve.wait_ge(v_mm, 3)
            v_out(2, 6)

            def rope_cos(r, dst, b):
                nc.vector.scalar_tensor_tensor(dst, bank(b), col[:, bass.ds(C_BQK + r, 1)], cosT,
                                               ALU.add, ALU.mult).then_inc(rope_c, 1)

            def rope_sin(r, b, lo):
                nc.vector.scalar_tensor_tensor(sin_term[lo:lo + 64, :], psum[64 - lo:128 - lo, b, :],
                                               col[lo:lo + 64, bass.ds(C_BQKS + r, 1)], sinT[lo:lo + 64, :],
                                               ALU.add, ALU.mult).then_inc(rope_s, 1)

            def query_cos(h, r):
                dve.wait_ge(q_mm, h + 1)
                after(dve, q_lo, h)
                rope_cos(r, q_rope, 7)

            def query_sum(h, r):
                dve.wait_ge(rope_c, r + 1)
                dve.wait_ge(rope_s, 2 * r + 2)
                nc.vector.tensor_tensor(q_rope, q_rope, sin_term, ALU.add).then_inc(q_sum, 1)

            def query_lo(h):
                dve.wait_ge(q_hi, h + 1)
                nc.vector.tensor_tensor(q_hl[:, 1, :], q_rope, as_f32(q_hl[:, 0, :]), ALU.subtract).then_inc(q_lo, 1)

            def key_terms(g, r):
                dve.wait_ge(k_mm, g + 1)
                after(dve, k_lo, g)
                rope_cos(r, k_rope, 3)
                after(dve, q_sum, 2 * g)
                rope_sin(r, 3, 0)
                rope_sin(r, 3, 64)

            def prob_lo(h, j):
                dve.wait_ge(p_hi, h * ST + j + 1)
                nc.vector.tensor_tensor(pT[:, j, 1, j * P:], psum[:, 4 + j % 2, j * P:], as_f32(pT[:, j, 0, j * P:]),
                                        ALU.subtract).then_inc(p_lo, 1)

            def maxima(h):
                def largest(c):
                    if c != 1:
                        dve.wait_ge(s_mm, 3 * h + (1, 1, 2, 3)[c])
                    nc.vector.reduce_max(mx[:, c:c + 1], score_ps_of(TILE_ORDER[c]), AX).then_inc(s_max, 1)

                def negate(c, cs):
                    dve.wait_ge(s_max, h * ST + c)
                    nc.vector.tensor_scalar(nmx[:, cs], mx[:, cs], -SCALE, None, ALU.mult).then_inc(s_nmax, 1)

                after(dve, s_nmax, 2 * h)
                after(dve, s_exp, h * ST)
                largest(0)
                largest(1)
                largest(2)
                negate(2, slice(0, 2))
                largest(3)
                negate(4, slice(2, 4))

            def normalize(h):
                after(dve, s_prob, h * ST)
                for c, i in enumerate(TILE_ORDER):
                    dve.wait_ge(s_exp, h * ST + c + 1)
                    nc.vector.reciprocal(rl[:, c:c + 1], lsum[:, c:c + 1]).then_inc(s_rl, 1)
                    dve.wait_ge(s_rl, h * ST + c + 1)
                    nc.vector.tensor_scalar(prob(i), prob(i), rl[:, c:c + 1], None,
                                            ALU.mult).then_inc(s_prob, 1)

            def half(g, side, key=True, score=True):
                h = g * 2 + side
                r = 3 * g + 2 + 2 * side
                if score:
                    query_cos(h + 1, r)
                prob_lo(h, 0)
                if score:
                    if side == 1 and key:
                        dve.wait_ge(k_sum, g + 2)
                    rope_sin(r, 7, 0)
                prob_lo(h, 1)
                if score:
                    rope_sin(r, 7, 64)
                    query_sum(h + 1, r)
                prob_lo(h, 2)
                if score:
                    query_lo(h + 1)
                prob_lo(h, 3)
                if score:
                    maxima(h + 1)
                    normalize(h + 1)
                if side == 0 and key:
                    key_terms(g + 1, r + 1)

            dve.wait_ge(ang_sb, ST)
            key_terms(0, 0)
            dve.wait_ge(wv_used, KC)
            v_out(3, 0)
            query_cos(0, 1)
            dve.wait_ge(k_sum, 1)
            rope_sin(1, 7, 0)
            rope_sin(1, 7, 64)
            query_sum(0, 1)
            query_lo(0)
            maxima(0)
            normalize(0)
            half(0, 0)
            half(0, 1)
            with dve.Fori(1, KV_HEADS - 2) as g:
                half(g, 0)
                half(g, 1)

            def attn_part(h, slot):
                dve.wait_ge(a_hi, h + 1)
                nc.vector.tensor_tensor(attn_hl[:, slot, 1, :], attn[:, h, :], as_f32(attn_hl[:, slot, 0, :]),
                                        ALU.subtract).then_inc(a_lo, 1)

            half(KV_HEADS - 2, 0)
            half(KV_HEADS - 2, 1)
            for h in range(4):
                attn_part(h, h)
            half(KV_HEADS - 1, 0, key=False)
            half(KV_HEADS - 1, 1, score=False)
            for h in range(4, HEADS):
                attn_part(h, h % 8)
            dve.wait_ge(g_sig, 1)
            nc.vector.tensor_scalar(ungate, gate, -1.0, 1.0, ALU.mult, ALU.add).then_inc(g_un, 1)

            def add_rows(i):
                if i < ST - 1:
                    dve.wait_ge(wo_mm, i + 1)
                else:
                    dve.wait_ge(w_used, HEADS)
                dve.wait_ge(d_ysel4[i], 16)
                nc.vector.tensor_tensor(x1[:, i, :], pair(2 * i), ysel4[i], ALU.add).then_inc(x1_sb, 1)

            def norm(i):
                inverse_root(i, n_sq, n_ms, n_rt, n_chain, n_rs)
                dve.wait_ge(n_rs, i + 1)
                after(dve, n_T, i)
                nc.vector.tensor_scalar(h2s, x1[:, i, :], rs[:, i:i + 1], None, ALU.mult).then_inc(n_norm, 1)

            def norm_full(i):
                dve.wait_ge(n_T, i + 1)
                after(dve, n_lo, i)
                ln = col[:, C_LN2:C_LN2 + KC].rearrange("p (k a) -> p k a", a=1).broadcast_to([P, KC, P])
                n_ps = psum[:, 2 * i:2 * i + 2, :].rearrange("p b (k n) -> p (b k) n", k=4)
                nc.vector.tensor_tensor(h2full, n_ps, ln, ALU.mult).then_inc(n_full, 1)

            def norm_lo(i):
                dve.wait_ge(n_hi, i + 1)
                nc.vector.tensor_tensor(hT[:, :, 1, i * P:(i + 1) * P], h2full, as_f32(hT[:, :, 0, i * P:(i + 1) * P]),
                                        ALU.subtract).then_inc(n_lo, 1)

            for i in range(ST):
                add_rows(i)
                if i > 1:
                    norm_lo(i - 2)
                if i > 0:
                    norm_full(i - 1)
                norm(i)
            norm_lo(ST - 2)
            norm_full(ST - 1)
            norm_lo(ST - 1)
            dve.wait_ge(g_un, 1)
            for i in range(ST):
                dve.wait_ge(d_xsel[i], 16)
                nc.vector.scalar_tensor_tensor(xsel[:, i, :], x1[:, i, :], gate[:, i:i + 1], xsel[:, i, :],
                                               ALU.mult, ALU.add).then_inc(g_mix, 1)
                dve.wait_ge(g_mix, i + 1)
                nc.vector.scalar_tensor_tensor(xsel[:, i, :], ysel4[i], ungate[:, i:i + 1], xsel[:, i, :],
                                               ALU.mult, ALU.add).then_inc(g_base, 1)
                dve.wait_ge(g_base, i + 1)

            def ffn(f, odd):
                dve.wait_ge(w_used, HEADS + f * 2 + 2)
                dve.wait_ge(g_silu, f + 1)
                nc.vector.tensor_tensor(m[:, bass.ds(f, 1), :].rearrange("p a n -> p (a n)"), silu_g[:, odd, :],
                                        bank(2 * odd + 1), ALU.mult).then_inc(m_sb, 1)

            for f in range(12):
                ffn(f, f % 2)
            dve.wait_ge(d_base, 16)
            with dve.Fori(6, FT // 2 - 1) as k:
                ffn(k * 2, 0)
                ffn(k * 2 + 1, 1)

            def m_part(f, s):
                dve.wait_ge(m_hi, f + 1)
                nc.vector.tensor_tensor(m_hl[:, s, 1, :], row(m, f), as_f32(m_hl[:, s, 0, :]), ALU.subtract).then_inc(m_lo, 1)

            for f in range(4):
                m_part(f, f)
            ffn(FT - 2, 0)
            ffn(FT - 1, 1)
            with dve.Fori(1, FT // 4) as k:
                for s in range(4):
                    m_part(k * 4 + s, s)
            for i in range(ST):
                if i < ST - 1:
                    dve.wait_ge(dn_mm, i + 1)
                else:
                    dve.wait_ge(w_used, W_END - W_O)
                dve.wait_ge(d_baseld[i], 16)
                nc.vector.scalar_tensor_tensor(base[:, i, :], pair(2 * i), gate[:, i:i + 1], base[:, i, :],
                                               ALU.mult, ALU.add).then_inc(fin, 1)


_OUTS = [((BATCH, SEQ, D), "float32")]


def kernel(**inputs):
    import concourse.bacc as _bacc
    from concourse.bass_utils import run_bass_kernel_spmd as _run

    a = {k: np.asarray(v) for k, v in inputs.items()}
    x = a["x"]

    def columns(v):
        return v.reshape(-1, P).T

    x_t = np.ascontiguousarray(x.reshape(BATCH, SEQ, KC, P).transpose(0, 2, 3, 1)).reshape(BATCH * KC, P, SEQ)
    heads = lambda w: w.reshape(KC, P, -1, P).transpose(2, 1, 0, 3).reshape(-1, P, D)
    wq, wk = heads(a["L0_ffn_wq"]), heads(a["L0_ffn_wk"])
    qk = [wk[0]] + [t for g in range(KV_HEADS) for t in (wq[2 * g], *wk[g + 1:g + 2], wq[2 * g + 1])]
    wg, wu = heads(a["L0_ffn_w_gate"]), heads(a["L0_ffn_w_up"])
    gu = [t for f in range(FT) for t in (wg[f], wu[f])]
    rows_of = lambda w: w.reshape(-1, P, D)
    wstream = np.concatenate([rows_of(a["L0_cond_W2"]), rows_of(a["L0_ffn_wv"]), np.stack(qk),
                              rows_of(a["L0_ffn_wo"]), np.stack(gu), rows_of(a["L0_ffn_w_down"])])
    bq, bk = a["L0_ffn_bq"].reshape(HEADS, HD), a["L0_ffn_bk"].reshape(KV_HEADS, HD)
    bqk = np.stack([bk[0], bq[0]] + [t for g in range(KV_HEADS) for t in (bq[2 * g + 1], *bk[g + 1:g + 2], *bq[2 * g + 2:2 * g + 3])])
    swapped = np.concatenate([bqk[:, HD // 2:], bqk[:, :HD // 2]], axis=1)
    cols = np.concatenate([columns(a["L0_cond_b3"]), columns(a["L0_ffn_ln1_w"]), columns(a["L0_ffn_ln2_w"]),
                           bqk.T, swapped.T], axis=1)
    rows = np.stack([a["L0_cond_b2"], a["L0_ffn_w_router"], a["L0_ffn_bv"]])

    part = np.arange(P)
    shape_consts = np.zeros((P, N_CONSTS), np.float32)
    shape_consts[:, Z_IDENT:Z_IDENT + P] = np.eye(P)
    shape_consts[:, Z_MASK:Z_MASK + P] = np.where(part[None, :] > part[:, None], LOWEST, 0.0)
    for half in range(2):
        shape_consts[half, Z_PAIR + half * PICK:Z_PAIR + (half + 1) * PICK] = 1.0
    shape_consts[:, Z_RANK] = part % PICK
    for k in range(ST):
        shape_consts[:, Z_BASE + k] = (2 * k + part // PICK) * SEQ
        shape_consts[:, Z_YBASE + k] = (2 * (k == 2) + part // PICK) * SEQ
    inv_freq = (np.float32(1.0) / np.float32(10000.0) ** (np.arange(0, HD, 2, dtype=np.float32) / np.float32(HD)))
    phase = (np.arange(SEQ, dtype=np.float32)[:, None] * inv_freq.astype(np.float32)).astype(np.float32)
    cos, sin = np.cos(phase), np.sin(phase)
    angles = np.concatenate([cos, cos, -sin, sin], axis=1).astype(np.float32)

    arrays = {
        "x_t": x_t, "x_rows": x.reshape(BATCH * SEQ, D),
        "cond_t": a["cond_1024"].T.reshape(COND // P, P, BATCH).transpose(1, 0, 2),
        "w3": a["L0_cond_W3"], "wstream": wstream, "cols": cols, "rows": rows,
        "shape_consts": shape_consts, "angles": angles,
    }
    arrays = {k: np.ascontiguousarray(v) for k, v in arrays.items()}
    nc = _bacc.Bacc("TRN2", target_bir_lowering=False, num_devices=1)
    args = {k: nc.dram_tensor(k, v.shape, mybir.dt.from_np(v.dtype), kind="ExternalInput").ap()
            for k, v in arrays.items()}
    out = nc.dram_tensor("out", (BATCH * SEQ, D), mybir.dt.float32, kind="ExternalOutput").ap()
    build(nc, out=out, **args)
    r = _run(nc, [arrays], core_ids=[0])
    return r.results[0]["out"].reshape(BATCH, SEQ, D)
```

```python
from contextlib import ExitStack

import numpy as np

import concourse.bass as bass
from concourse import mybir

P = 128
BATCH, SEQ, D = 8, 512, 1024
COND = 512
HEADS, KV_HEADS, HD = 16, 8, 128
FF = 4096
PICK = 64
S = BATCH * PICK
KC = D // P
TT = SEQ // P
ST = S // P
FT = FF // P
EPS = 1e-6
SCALE = 1.0 / float(np.sqrt(np.float32(HD)))
LOWEST = -3.0e38

W_V = KC
W_QK = W_V + KC
W_O = W_QK + HEADS + KV_HEADS
W_GU = W_O + HEADS
W_DOWN = W_GU + 2 * FT
W_END = W_DOWN + FT

C_B3, C_LN1, C_LN2 = 0, KC, 2 * KC
C_BQK = 3 * KC
C_BQKS = C_BQK + HEADS + KV_HEADS
N_COLS = C_BQKS + HEADS + KV_HEADS
Z_IDENT, Z_MASK, Z_PAIR, Z_RANK, Z_BASE = 0, P, 2 * P, 3 * P, 3 * P + 1
Z_YBASE = Z_BASE + ST
N_CONSTS = Z_YBASE + ST


def after(engine, sem, n):
    if isinstance(n, int) and n <= 0:
        return
    engine.wait_ge(sem, n)


def apart(engine, sem, n, passed):
    engine.wait_ge(sem, n)
    engine.sem_inc(passed, 1)


def build(nc, x_t, x_rows, cond_t, w3, wstream, cols, rows, shape_consts, angles, out):
    f32, f32r, bf16, u32 = mybir.dt.float32, mybir.dt.float32r, mybir.dt.bfloat16, mybir.dt.uint32
    ALU, ACT, AX = mybir.AluOpType, mybir.ActivationFunctionType, mybir.AxisListType.X

    PAIR = 2 * SEQ
    y_first = nc.dram_tensor("y_first", [PAIR, D], f32).ap()
    y_middle = nc.dram_tensor("y_middle", [2 * PAIR, D], f32).ap()
    y_last = nc.dram_tensor("y_last", [PAIR, D], f32).ap()
    y_of = [y_first, y_middle, y_middle, y_last]
    base_rows = nc.dram_tensor("base_rows", [S, D], f32).ap()

    ctx = ExitStack()
    with ctx:
        K = 256
        plain = ctx.enter_context(nc.sbuf_tensor("plain", [P, 76 * K], f32))
        split = ctx.enter_context(nc.sbuf_tensor("split", [P, 128 * K], f32r))
        ident_r = ctx.enter_context(nc.sbuf_tensor("ident_r", [P, P], f32r))
        mask_r = ctx.enter_context(nc.sbuf_tensor("mask_r", [P, P], f32r))
        consts = ctx.enter_context(nc.sbuf_tensor("consts", [P, N_CONSTS], f32))
        col = ctx.enter_context(nc.sbuf_tensor("col", [P, N_COLS], f32))
        small = ctx.enter_context(nc.sbuf_tensor("small", [P, 208], f32))
        idx = ctx.enter_context(nc.sbuf_tensor("idx", [P, 3 * ST], u32))
        psum = ctx.enter_context(nc.psum_tensor("psum", [P, 8, 512], f32))

        def kib(a, b):
            return plain[:, a * K:b * K]

        def skib(a, b):
            return split[:, int(a * K):int(b * K)]

        xT = kib(0, 8).rearrange("p (s n) -> p s n", s=4)
        xrow = kib(8, 24).rearrange("p (s n) -> p s n", s=TT)
        y = kib(24, 32).rearrange("p (s n) -> p s n", s=2)
        w3_sb = kib(32, 48).rearrange("p (m k n) -> p m k n", m=KC, k=COND // P)
        ysel = kib(32, 40).rearrange("p (s n) -> p s n", s=2)
        hs = kib(40, 44)
        rank_a, rank_b = plain[:, 40 * K:42 * K], plain[:, 42 * K:44 * K]
        hfull = kib(44, 48).rearrange("p (k n) -> p k n", k=KC)
        bias_row = kib(48, 52)
        wr_row = kib(52, 56)
        cosT, sinT = kib(56, 58), kib(58, 60)
        junk = kib(60, 62).bitcast(bf16)
        junk_sum = kib(62, 63).bitcast(bf16)
        ang = kib(63, 64)
        raw = kib(64, 76).rearrange("p (s n) -> p s n", s=3)
        raw_w2 = [raw[:, 0, :], raw[:, 1, :], raw[:, 2, :], y[:, 0, :], y[:, 1, :]] + [xrow[:, s, :] for s in range(3)]
        raw_wv = [raw[:, 0, :], raw[:, 1, :], raw[:, 2, :], kib(0, 4), kib(4, 8)]
        prob_all = kib(0, 5)
        k_rope = kib(6, 8)
        V = kib(8, 24).rearrange("p (i n) -> p i n", i=ST)
        attn = kib(24, 56).rearrange("p (h n) -> p h n", h=HEADS)
        q_rope, sin_term = kib(60, 62), kib(62, 64)
        ysel4 = [kib(0, 4), kib(4, 8), kib(48, 52), kib(52, 56)]
        x1 = kib(8, 24).rearrange("p (i n) -> p i n", i=ST)
        h2s = kib(24, 28)
        h2full = kib(28, 32).rearrange("p (k n) -> p k n", k=KC)
        xsel = kib(32, 48).rearrange("p (i n) -> p i n", i=ST)
        m = kib(0, 64).rearrange("p (f n) -> p f n", f=FT)
        silu_g = kib(72, 76).rearrange("p (s n) -> p s n", s=2)
        base = kib(0, 16).rearrange("p (i n) -> p i n", i=ST)

        w8 = skib(0, 64).rearrange("p (s q n) -> p s q n", s=KC, q=2)
        xx = skib(64, 128).rearrange("p (b k q n) -> p b k q n", b=2, k=KC, q=2)
        hT = skib(64, 96).rearrange("p (k q n) -> p k q n", k=KC, q=2)
        w4 = skib(96, 128).rearrange("p (s q n) -> p s q n", s=4, q=2)
        k_hl = skib(0, 4).rearrange("p (q n) -> p q n", q=2)
        q_hl = skib(4, 8).rearrange("p (q n) -> p q n", q=2)
        v_hl = skib(8, 12).rearrange("p (q i n) -> p q i n", q=2, i=ST)
        pT = skib(12, 28).rearrange("p (j q n) -> p j q n", j=ST, q=2)
        attn_hl = skib(28, 60).rearrange("p (s q n) -> p s q n", s=8, q=2)
        m_hl = skib(0, 16).rearrange("p (s q n) -> p s q n", s=4, q=2)

        ident = consts[:, Z_IDENT:Z_IDENT + P]
        qe = small[:, 0:KC * BATCH].rearrange("p (k b) -> p k b", b=BATCH)
        vs = small[:, 64:80].rearrange("p (b k) -> p b k", b=2)
        sc = small[:, 80:88].rearrange("p (j b) -> p j b", b=2)
        top8 = small[:, 112:120]
        idxf = small[:, 120:124]
        ssq, rt, rs, na = small[:, 124:128], small[:, 128:132], small[:, 132:136], small[:, 136:140]
        sels = small[:, 140:144]
        mx, nmx = small[:, 144:148], small[:, 148:152]
        lsum, rl = small[:, 152:156], small[:, 156:160]
        gate, ungate = small[:, 160:164], small[:, 164:168]
        ms = small[:, 168:172]
        condT = small[:, 176:208].rearrange("p (k b) -> p k b", b=BATCH)

        def sem(name):
            return ctx.enter_context(nc.semaphore(name))

        d_consts, d_cols, d_cond, d_b2, d_wr, d_bv = (sem(n) for n in (
            "d_consts", "d_cols", "d_cond", "d_b2", "d_wr", "d_bv"))
        d_w3 = [sem(f"d_w3_{mo}") for mo in range(KC)]
        d_xT = [sem(f"d_xT{s}") for s in range(4)]
        d_x = [sem(f"d_x{s}") for s in range(TT)]
        d_y = [sem(f"d_y{s}") for s in range(2)]
        d_out = [sem(f"d_out{s}") for s in range(TT)]
        d_w8 = [sem(f"d_w8_{kc}") for kc in range(KC)]
        d_raw3 = [sem(f"d_raw3_{s}") for s in range(3)]
        d_raw = [sem(f"d_raw{s}") for s in range(2)]
        d_ysel = [sem(f"d_ysel{s}") for s in range(ST)]
        d_ang = [sem(f"d_ang{s}") for s in range(ST)]
        d_xsel = [sem(f"d_xsel{s}") for s in range(ST)]
        d_base = sem("d_base")
        d_baseld = [sem(f"d_baseld{s}") for s in range(ST)]
        d_fin = sem("d_fin")
        dve_passed, pool_passed = sem("dve_passed"), sem("pool_passed")
        qe_mm, qe_b, qe_done = sem("qe_mm"), sem("qe_b"), sem("qe_done")
        const_r = sem("const_r")
        x_sum, x_mod, x_hi, x_lo = sem("x_sum"), sem("x_mod"), sem("x_hi"), sem("x_lo")
        w_hi, w_lo = sem("w_hi"), sem("w_lo")
        w2_used, wv_used, w_used = sem("w2_used"), sem("wv_used"), sem("w_used")
        y_mm, y_biased, y_relu, y_score, out_row = (sem(n) for n in (
            "y_mm", "y_biased", "y_relu", "y_score", "out_row"))
        score_T, top_max, top_cut, top_mask, top_rank, rank_bc = (sem(n) for n in (
            "score_T", "top_max", "top_cut", "top_mask", "top_rank", "rank_bc"))
        idx_f, idx_u = sem("idx_f"), sem("idx_u")
        h_sq, h_ms, h_rt, h_chain, h_rs, h_sel, h_norm = (sem(n) for n in (
            "h_sq", "h_ms", "h_rt", "h_chain", "h_rs", "h_sel", "h_norm"))
        h_T, h_full, h_hi, h_lo, ang_T, ang_sb = (sem(n) for n in (
            "h_T", "h_full", "h_hi", "h_lo", "ang_T", "ang_sb"))
        v_mm, v_sb, v_hi, v_lo = sem("v_mm"), sem("v_sb"), sem("v_hi"), sem("v_lo")
        k_mm, k_sum, k_hi, k_lo = sem("k_mm"), sem("k_sum"), sem("k_hi"), sem("k_lo")
        q_mm, q_sum, q_hi, q_lo = sem("q_mm"), sem("q_sum"), sem("q_hi"), sem("q_lo")
        rope_c, rope_s = sem("rope_c"), sem("rope_s")
        s_mm, s_max, s_nmax, s_exp, s_rl, s_prob = (sem(n) for n in (
            "s_mm", "s_max", "s_nmax", "s_exp", "s_rl", "s_prob"))
        p_T, p_hi, p_lo, pv_mm, o_sb = sem("p_T"), sem("p_hi"), sem("p_lo"), sem("pv_mm"), sem("o_sb")
        a_hi, a_lo, wo_mm, x1_sb = sem("a_hi"), sem("a_lo"), sem("wo_mm"), sem("x1_sb")
        g_sig, g_un, g_mix, g_base = sem("g_sig"), sem("g_un"), sem("g_mix"), sem("g_base")
        n_sq, n_ms, n_rt, n_chain, n_rs, n_norm = (sem(n) for n in (
            "n_sq", "n_ms", "n_rt", "n_chain", "n_rs", "n_norm"))
        n_T, n_full, n_hi, n_lo = sem("n_T"), sem("n_full"), sem("n_hi"), sem("n_lo")
        g_silu, m_sb, m_hi, m_lo, dn_mm, fin = (sem(n) for n in (
            "g_silu", "m_sb", "m_hi", "m_lo", "dn_mm", "fin"))

        def bank(b, n=512):
            return psum[:, b, 0:n]

        def pair(b):
            return psum[:, b:b + 2, :].rearrange("p b n -> p (b n)")

        def as_f32(ap):
            return ap.bitcast(f32)

        TILE_ORDER = (0, 2, 1, 3)

        def score_ps_of(i, a=0, b=None):
            at = (0, 0, P, 0)[i]
            return psum[:, (0, 1, 0, 2)[i], at + a:at + ((i + 1) * P if b is None else b)]

        def prob(i, a=0, b=None):
            at = i * (i + 1) // 2 * P
            return prob_all[:, at + a:at + ((i + 1) * P if b is None else b)]

        def row(ap, i):
            return ap[:, bass.ds(i, 1), :].rearrange("p a n -> p (a n)")

        block = ctx.enter_context(nc.Block())

        @block.sync
        def _(sp):
            def load_w(n, dst, landed):
                sp.dma_start(dst, wstream[n]).then_inc(landed, 16)

            def load_xT(b, kc):
                c = b * KC + kc
                after(sp, x_lo, c - 3)
                sp.dma_start(xT[:, kc % 4, :], x_t[c]).then_inc(d_xT[kc % 4], 16)

            def load_x(b, j):
                sp.dma_start(xrow[:, j, :], x_rows[bass.ds((b * TT + j) * P, P), :]).then_inc(d_x[j], 16)

            sp.dma_start(condT, cond_t).then_inc(d_cond, 16)
            for kc in range(KC):
                sp.dma_start(w3_sb[:, kc], w3[kc]).then_inc(d_w3[kc], 16)
                if kc == 0:
                    sp.dma_start(col[:], cols).then_inc(d_cols, 16)
                if kc < 4:
                    load_xT(0, kc)
                load_w(kc, raw_w2[kc], d_w8[kc])
                if kc >= 4:
                    load_xT(0, kc)
            sp.dma_start(consts[:], shape_consts).then_inc(d_consts, 16)
            sp.dma_start(bias_row, rows[0:1, :].broadcast_to([P, D])).then_inc(d_b2, 16)
            sp.dma_start(wr_row, rows[1:2, :].broadcast_to([P, D])).then_inc(d_wr, 16)
            for kc in range(4):
                load_xT(1, kc)
            for j in range(TT):
                if j < 3:
                    sp.wait_ge(w_lo, 6 + j)
                load_x(0, j)

            def store(b, j):
                t = b * TT + j
                sp.wait_ge(out_row, t + 1)
                sp.dma_start(out[bass.ds(t * P, P), :], xrow[:, j, :]).then_inc(d_out[j], 16)

            def window(b):
                known = isinstance(b, int)
                for j in range(TT):
                    ahead = b + 1 + j // 2
                    if not known or ahead < BATCH:
                        for kc in range((2 * j + 4) % KC, (2 * j + 4) % KC + 2):
                            load_xT(ahead, kc)
                    if j > 0:
                        store(b, j - 1)
                    elif not known or b > 0:
                        store(b - 1, TT - 1)
                    if j < 2 and (not known or b > 0):
                        sp.wait_ge(d_out[j + 2], 16 * b)
                        load_x(b, j + 2)
                    if j >= 2 and (not known or b < BATCH - 1):
                        sp.wait_ge(d_out[j - 2], 16 * b + 16)
                        load_x(b + 1, j - 2)

            window(0)
            with sp.Fori(1, BATCH - 2) as b:
                window(b)
            window(BATCH - 2)
            sp.wait_ge(x_lo, BATCH * KC)
            for kc in range(5):
                load_w(W_V + kc, raw_wv[kc], d_w8[kc])
            window(BATCH - 1)
            for kc in range(5, KC):
                sp.wait_ge(w_lo, W_V + kc - 4)
                load_w(W_V + kc, raw_wv[kc - 5], d_w8[kc])
            store(BATCH - 1, TT - 1)
            sp.wait_ge(y_biased, BATCH * TT)
            sp.dma_start(bias_row, rows[2:3, :].broadcast_to([P, D])).then_inc(d_bv, 16)
            for u in range(3):
                sp.wait_ge(w_lo, W_V + 5 + u + 1)
                load_w(W_QK + u, raw[:, u, :], d_raw3[u])
            with sp.Fori(1, KV_HEADS) as g:
                for u in range(3):
                    sp.wait_ge(w_hi, W_QK + 3 * (g - 1) + u + 1)
                    sp.wait_ge(w_lo, W_QK + 3 * (g - 1) + u + 1)
                    load_w(W_QK + 3 * g + u, raw[:, u, :], d_raw3[u])
            for s in range(2):
                sp.wait_ge(w_hi, W_O - 2 + s)
                sp.wait_ge(w_lo, W_O - 2 + s)
                load_w(W_O + s, raw[:, s, :], d_raw[s])
            with sp.Fori(1, (W_END - W_O) // 2) as k:
                for s in range(2):
                    sp.wait_ge(w_hi, W_O + 2 * k + s - 1)
                    sp.wait_ge(w_lo, W_O + 2 * k + s - 1)
                    load_w(W_O + 2 * k + s, raw[:, s, :], d_raw[s])
            for j in range(TT):
                sp.wait_ge(d_out[j], 16 * BATCH)
            sp.wait_ge(d_fin, 16 * ST)

        @block.tensor
        def _(pe):
            def three(out_ap, w_hl, x_hl, start, stop):
                nc.tensor.matmul(out_ap, w_hl[0], x_hl[0], start=start, stop=False, skip_group_check=True)
                nc.tensor.matmul(out_ap, w_hl[0], x_hl[1], start=False, stop=False, skip_group_check=True)
                return nc.tensor.matmul(out_ap, w_hl[1], x_hl[0], start=False, stop=stop, skip_group_check=True)

            def q_emb(mo):
                pe.wait_ge(d_w3[mo], 16)
                after(pe, qe_b, mo - 1)
                for k in range(COND // P):
                    last = nc.tensor.matmul(psum[:, 6 + mo % 2, 0:BATCH], w3_sb[:, mo, k, :], condT[:, k, :],
                                            start=(k == 0), stop=(k == COND // P - 1), skip_group_check=True)
                last.then_inc(qe_mm, 1)

            def y_chunk(p, kc, j, banks):
                xk = [xx[:, p, kc, q, j * P:(j + 1) * P] for q in range(2)]
                for half in range(2):
                    cut = slice(half * 512, half * 512 + 512)
                    last = three(bank(banks + half), xk, (w8[:, kc, 0, cut], w8[:, kc, 1, cut]), kc == 0, kc == KC - 1)
                return last

            def first_batch():
                pe.wait_ge(d_cond, 16)
                q_emb(0)
                for kc in range(KC):
                    if kc < KC - 1:
                        q_emb(kc + 1)
                    pe.wait_ge(x_lo, kc + 1)
                    pe.wait_ge(w_lo, kc + 1)
                    for j in range(TT - 1):
                        last = y_chunk(0, kc, j, 2 * j)
                        if kc == KC - 1:
                            last.then_inc(y_mm, 1)
                for kc in range(KC):
                    last = y_chunk(0, kc, TT - 1, 6)
                last.then_inc(y_mm, 1)

            def y_tile(t, p, j, chunks, final=False):
                pe.wait_ge(y_biased, t - 1)
                for kc in range(KC):
                    if j == 0:
                        pe.wait_ge(x_lo, chunks + kc + 1)
                    last = y_chunk(p, kc, j, 2 * (j % 2))
                    if final:
                        last.then_inc(w2_used, 1)
                if not final:
                    last.then_inc(y_mm, 1)

            def score_rows(k):
                pe.wait_ge(y_score, 2 * TT * (k + 1))
                after(pe, top_mask, k)
                for j in range(TT):
                    last = nc.tensor.transpose(psum[0:2, 4, j * P:(j + 1) * P],
                                               sc[:, j, :], ident)
                last.then_inc(score_T, 1)

            def spread_ranks(k):
                pe.wait_ge(top_rank, k + 1)
                nc.tensor.matmul(bank(5), consts[0:2, Z_PAIR:Z_PAIR + P], rank_b[0:2, :],
                                 start=True, stop=True, skip_group_check=True).then_inc(rank_bc, 1)

            def routed_T(k, ang_bank):
                pe.wait_ge(d_ang[k], 16)
                after(pe, ang_sb, k)
                for q in range(2):
                    last = nc.tensor.transpose(psum[:, ang_bank, q * P:(q + 1) * P],
                                               ang[:, q * P:(q + 1) * P], ident)
                last.then_inc(ang_T, 1)
                pe.wait_ge(h_norm, k + 1)
                after(pe, h_full, k)
                for kc in range(KC):
                    last = nc.tensor.transpose(psum[:, 4 + kc // 4, (kc % 4) * P:(kc % 4 + 1) * P],
                                               hs[:, kc * P:(kc + 1) * P], ident)
                last.then_inc(h_T, 1)

            def windows(i):
                first, end = isinstance(i, int) and i == 0, isinstance(i, int) and i == ST - 1
                if first:
                    first_batch()
                for p in range(1 if first else 0, 2):
                    for j in range(TT):
                        t = i * 2 * TT + p * TT + j
                        y_tile(t, p, j, (i * 2 + p) * KC, final=end and p == 1 and j == TT - 1)
                        if not first and p == 0 and j == 0:
                            score_rows(i - 1)
                        if not first and p == 1 and j == 0:
                            spread_ranks(i - 1)
                        if end and p == 1 and j > 0:
                            routed_T(j - 1, 6)

            windows(0)
            pe.wait_ge(d_consts, 16)
            with pe.Fori(1, ST - 1) as i:
                windows(i)
            windows(ST - 1)

            def v_part(i, kc, banks):
                for half in range(2):
                    cut = slice(half * 512, half * 512 + 512)
                    last = three(bank(banks + half),
                                 (hT[:, kc, 0, i * P:(i + 1) * P], hT[:, kc, 1, i * P:(i + 1) * P]),
                                 (w8[:, kc, 0, cut], w8[:, kc, 1, cut]), kc == 0, kc == KC - 1)
                return last

            pe.wait_ge(h_lo, 2)
            for kc in range(KC):
                pe.wait_ge(w_lo, W_V + kc + 1)
                for i in range(2):
                    if kc == 0:
                        pe.wait_ge(y_biased, BATCH * TT - 1 + i)
                    last = v_part(i, kc, 2 * i)
                    if kc == KC - 1:
                        last.then_inc(v_mm, 1)
                if kc == 1:
                    pe.wait_ge(h_full, ST - 1)
                    score_rows(ST - 1)
            pe.wait_ge(h_lo, 3)
            pe.wait_ge(ang_sb, 3)
            for kc in range(KC):
                if kc == 1:
                    spread_ranks(ST - 1)
                last = v_part(2, kc, 6)
            last.then_inc(v_mm, 1)
            pe.wait_ge(v_sb, 2)
            routed_T(ST - 1, 3)

            def project(slot, b, kcs, cols=slice(0, S)):
                for kc in kcs:
                    wt = [w4[:, slot, q, kc * P:(kc + 1) * P] for q in range(2)]
                    last = three(psum[:, b, cols], wt, (hT[:, kc, 0, cols], hT[:, kc, 1, cols]), kc == 0, kc == KC - 1)
                return last

            def scores(h):
                pe.wait_ge(q_lo, h + 1)
                for i in TILE_ORDER:
                    n = (i + 1) * P
                    qt = [q_hl[:, q, i * P:(i + 1) * P] for q in range(2)]
                    three(score_ps_of(i), qt, (k_hl[:, 0, 0:n], k_hl[:, 1, 0:n]), True, False)
                    last = nc.tensor.matmul(score_ps_of(i, n - P, n), ident_r[:], mask_r[:], start=False, stop=True,
                                            skip_group_check=True)
                    if i > 0:
                        last.then_inc(s_mm, 1)

            def flip(h, j):
                if j == 0:
                    pe.wait_ge(s_prob, (h + 1) * ST)
                after(pe, p_lo, h * ST + j - 1)
                for i in range(j, ST):
                    last = nc.tensor.transpose(psum[:, 4 + j % 2, i * P:(i + 1) * P],
                                               prob(i, j * P, (j + 1) * P), ident)
                last.then_inc(p_T, 1)

            def weigh(h, j):
                pe.wait_ge(p_lo, h * ST + j + 1)
                vt = [v_hl[:, q, j, :] for q in range(2)]
                last = three(psum[:, 6, j * P:], vt, (pT[:, j, 0, j * P:], pT[:, j, 1, j * P:]),
                             j == 0, j == ST - 1)
                last.then_inc(pv_mm, 1)

            def wo_part(h, b, slot, first=False, final=False):
                i, cut = b // 2, slice((b % 2) * 512, (b % 2) * 512 + 512)
                at = [attn_hl[:, slot, q, i * P:(i + 1) * P] for q in range(2)]
                return three(bank(b), at, (w4[:, slot % 4, 0, cut], w4[:, slot % 4, 1, cut]), first, final)

            def next_keys(g, side, part):
                if side == 1 and part == 0:
                    pe.wait_ge(w_lo, W_QK + 3 * g + 6)
                    pe.wait_ge(rope_s, 2 * (3 * g + 4))
                kc = (4 if side == 0 else 0) + 2 * part
                last = project(2, 3, (kc, kc + 1))
                if side == 0 and part == 1:
                    last.then_inc(k_mm, 1)

            def half(g, side, keys=True, query=True, score=True, fill=None):
                h = g * 2 + side
                flip(h, 0)
                flip(h, 1)
                if keys:
                    next_keys(g, side, 0)
                if fill:
                    fill(0)
                if side == 0:
                    pe.wait_ge(v_lo, g + 1)
                after(pe, o_sb, h)
                weigh(h, 0)
                flip(h, 2)
                if keys:
                    next_keys(g, side, 1)
                if fill:
                    fill(1)
                weigh(h, 1)
                flip(h, 3)
                if query:
                    u, slot = (3 * g + 4, 1) if side == 0 else (3 * g + 6, 0)
                    if side == 1 and not keys:
                        u, slot = 3 * g + 5, 2
                    pe.wait_ge(w_lo, W_QK + u + 1)
                    pe.wait_ge(rope_s, 2 * (3 * g + 3 + 2 * side))
                    project(slot, 7, range(3))
                if score:
                    if side == 1:
                        pe.wait_ge(k_lo, g + 2)
                    scores(h + 1)
                if fill:
                    fill(2)
                weigh(h, 2)
                weigh(h, 3)
                if query:
                    project(slot, 7, range(3, KC)).then_inc(q_mm, 1)

            ready = slice(0, (ST - 1) * P)
            pe.wait_ge(ang_sb, ST)
            pe.wait_ge(w_lo, W_QK + 1)
            project(0, 3, range(KC), ready)
            pe.wait_ge(h_lo, ST)
            for kc in range(KC):
                last = v_part(3, kc, 0)
                last.then_inc(wv_used, 1)
            project(0, 3, range(KC), slice((ST - 1) * P, S)).then_inc(k_mm, 1)
            pe.wait_ge(v_sb, 3)
            pe.wait_ge(w_lo, W_QK + 2)
            project(1, 7, range(KC)).then_inc(q_mm, 1)
            pe.wait_ge(w_lo, W_QK + 3)
            pe.wait_ge(rope_s, 2)
            project(2, 3, range(4))
            pe.wait_ge(v_sb, ST)
            pe.wait_ge(const_r, 2)
            pe.wait_ge(k_lo, 1)
            pe.wait_ge(w_lo, W_QK + 4)
            pe.wait_ge(rope_s, 4)
            project(0, 7, range(3))
            scores(0)
            project(0, 7, range(3, KC)).then_inc(q_mm, 1)
            half(0, 0)
            half(0, 1)
            with pe.Fori(1, KV_HEADS - 2) as g:
                half(g, 0)
                half(g, 1)
            half(KV_HEADS - 2, 0)

            def wo_ahead(parts):
                for h, b in parts:
                    pe.wait_ge(w_lo, W_O + h + 1)
                    pe.wait_ge(a_lo, h + 1)
                    if (h, b) == (0, 7):
                        pe.wait_ge(rope_s, 2 * (HEADS + KV_HEADS))
                    wo_part(h, b, h, first=(h == 0))

            half(KV_HEADS - 2, 1, keys=False, fill=lambda c: wo_ahead(((), (), ((0, 3),))[c]))

            half(KV_HEADS - 1, 0, keys=False, query=False,
                 fill=lambda c: wo_ahead(((), ((1, 3), (0, 7), (1, 7)), ())[c]))
            wo_ahead(((2, 3), (2, 7), (3, 3), (3, 7)))

            def fill_banks(b):
                for h in range(4):
                    wo_part(h, b, h, first=(h == 0))

            half(KV_HEADS - 1, 1, keys=False, query=False, score=False, fill=fill_banks)
            for h in range(4):
                for b in (4, 5, 6):
                    if h == 0 and b == 6:
                        pe.wait_ge(o_sb, HEADS)
                    last = wo_part(h, b, h, first=(h == 0))
                last.then_inc(w_used, 1)

            def wo_head(h, slot):
                pe.wait_ge(w_lo, W_O + h + 1)
                pe.wait_ge(a_lo, h + 1)
                for b in range(8):
                    last = wo_part(h, b, slot)
                last.then_inc(w_used, 1)

            for h in range(4, 12):
                wo_head(h, h % 8)

            def norm_T(i):
                pe.wait_ge(n_norm, i + 1)
                for kc in range(KC):
                    last = nc.tensor.transpose(psum[:, 2 * i + kc // 4, (kc % 4) * P:(kc % 4 + 1) * P],
                                               h2s[:, kc * P:(kc + 1) * P], ident)
                last.then_inc(n_T, 1)

            for i in range(ST):
                for h in range(12, HEADS):
                    if i == 0:
                        pe.wait_ge(w_lo, W_O + h + 1)
                        pe.wait_ge(a_lo, h + 1)
                    for b in (2 * i, 2 * i + 1):
                        last = wo_part(h, b, h % 8, final=(h == HEADS - 1))
                    if i == ST - 1:
                        last.then_inc(w_used, 1)
                if i < ST - 1:
                    last.then_inc(wo_mm, 1)
                if i > 0:
                    norm_T(i - 1)

            def ffn_part(s, cols=slice(0, S)):
                for kc in range(KC):
                    wt = [w4[:, s, q, kc * P:(kc + 1) * P] for q in range(2)]
                    last = three(psum[:, s, cols], wt, (hT[:, kc, 0, cols], hT[:, kc, 1, cols]),
                                 kc == 0, kc == KC - 1)
                return last

            def ffn_tile(f, odd):
                for gu in range(2):
                    pe.wait_ge(w_lo, W_GU + f * 2 + gu + 1)
                    pe.wait_ge(m_sb, f - 1)
                    ffn_part(2 * odd + gu).then_inc(w_used, 1)

            pe.wait_ge(n_full, 2)
            pe.wait_ge(n_lo, 2)
            for s in range(4):
                pe.wait_ge(w_lo, W_GU + s + 1)
                ffn_part(s, slice(0, S // 2))
                if s == 1:
                    norm_T(ST - 1)
            pe.wait_ge(n_lo, ST)
            for s in range(4):
                ffn_part(s, slice(S // 2, S)).then_inc(w_used, 1)
            with pe.Fori(1, FT // 2) as k:
                ffn_tile(k * 2, 0)
                ffn_tile(k * 2 + 1, 1)

            def down_tile(f, s, first=False, final=False):
                pe.wait_ge(w_lo, W_DOWN + f + 1)
                pe.wait_ge(m_lo, f + 1)
                order = (2, 3, 0, 1) if first else range(ST)
                for i in order:
                    if first and i == 0:
                        pe.wait_ge(m_sb, FT)
                    mt = [m_hl[:, s, q, i * P:(i + 1) * P] for q in range(2)]
                    for half in range(2):
                        cut = slice(half * 512, half * 512 + 512)
                        last = three(bank(2 * i + half), mt, (w4[:, s, 0, cut], w4[:, s, 1, cut]),
                                     first, final)
                    if final and i < ST - 1:
                        last.then_inc(dn_mm, 1)
                last.then_inc(w_used, 1)

            for s in range(4):
                down_tile(s, s, first=(s == 0))
            with pe.Fori(1, FT // 4 - 1) as k:
                for s in range(4):
                    down_tile(k * 4 + s, s)
            for s in range(4):
                down_tile(FT - 4 + s, s, final=(s == 3))

        @block.scalar
        def _(act):
            act.preload_act_table(ACT.Sqrt)

            def w_part(src, landed, count, dst, free=None, used=0):
                act.wait_ge(landed, count)
                if free is not None:
                    act.wait_ge(free, used)
                nc.scalar.activation(dst, src, ACT.Copy).then_inc(w_hi, 1)

            def x_sums(b, p, kcs):
                for kc in kcs:
                    c = b * KC + kc
                    act.wait_ge(d_xT[kc % 4], 16 * (2 * b + kc // 4) + 16)
                    after(act, x_sum, c)
                    nc.scalar.activation(junk_sum[:, 0:SEQ], xT[:, kc % 4, :], ACT.Identity,
                                         scale=1.0 / SEQ, accum_out=vs[:, p, kc:kc + 1]).then_inc(x_sum, 1)

            def x_parts(b, p, kcs, gemm_done):
                for kc in kcs:
                    c = b * KC + kc
                    act.wait_ge(x_mod, c + 1)
                    after(act, y_mm, gemm_done)
                    nc.scalar.activation(xx[:, p, kc, 0, :], xT[:, kc % 4, :], ACT.Copy).then_inc(x_hi, 1)

            def y_out(t, j, dst, row):
                act.wait_ge(y_biased, t + 1)
                nc.scalar.activation(y[:, j % 2, :], y[:, j % 2, :], ACT.Relu).then_inc(y_relu, 1)
                act.wait_ge(y_relu, t + 1)
                act.dma_start(dst[bass.ds(row, P), :], y[:, j % 2, :]).then_inc(d_y[j % 2], 16)

            def routed(k):
                act.wait_ge(d_ysel[k], 16)
                if k == 0:
                    act.wait_ge(rank_bc, ST - 1)
                after(act, h_T, k)
                nc.scalar.activation(hs, ysel[:, k % 2, :], ACT.Square, accum_out=ssq[:, k:k + 1]).then_inc(h_sq, 1)
                act.wait_ge(h_ms, k + 1)
                nc.scalar.activation(rt[:, k:k + 1], ms[:, k:k + 1], ACT.Sqrt).then_inc(h_rt, 1)

            def routed_split(k):
                act.wait_ge(ang_T, k + 1)
                b = 3 if k == ST - 1 else 6
                nc.scalar.activation(cosT[:, k * P:(k + 1) * P], psum[:, b, 0:P], ACT.Copy)
                nc.scalar.activation(sinT[:, k * P:(k + 1) * P], psum[:, b, P:2 * P], ACT.Copy).then_inc(ang_sb, 1)
                act.wait_ge(h_full, k + 1)
                nc.scalar.activation(hT[:, :, 0, k * P:(k + 1) * P], hfull, ACT.Copy).then_inc(h_hi, 1)

            for kc in range(KC):
                x_sums(0, 0, (kc,))
                w_part(raw_w2[kc], d_w8[kc], 16, w8[:, kc, 0, :])
                x_parts(0, 0, (kc,), 0)
            act.wait_ge(d_consts, 16)
            nc.scalar.activation(ident_r[:], ident, ACT.Copy).then_inc(const_r, 1)
            nc.scalar.activation(mask_r[:], consts[:, Z_MASK:Z_MASK + P], ACT.Copy).then_inc(const_r, 1)

            def wv_part(kc):
                w_part(raw_wv[kc % 5], d_w8[kc], 32, w8[:, kc, 0, :], w2_used, kc + 1)

            def windows(i):
                end = isinstance(i, int) and i == ST - 1
                for p in range(2):
                    b = i * 2 + p
                    for j in range(TT):
                        if end and p == 1 and j == TT - 1:
                            for kc in range(4):
                                wv_part(kc)
                        if not (end and p == 1):
                            x_sums(b + 1, 1 - p, (2 * j, 2 * j + 1))
                            x_parts(b + 1, 1 - p, (2 * j, 2 * j + 1), b * TT)
                        elif j == 0:
                            act.wait_ge(y_mm, b * TT)
                        row = (p * TT + j) * P
                        if end:
                            y_out(b * TT + j, j, y_last, row)
                        elif isinstance(i, int):
                            y_out(b * TT + j, j, y_first, row)
                        else:
                            y_out(b * TT + j, j, y_middle, (i - 1) * PAIR + row)
                        if end and p == 1:
                            if j > 0:
                                routed_split(j - 1)
                            if j < TT - 1:
                                routed(j)

            windows(0)
            with act.Fori(1, ST - 1) as i:
                windows(i)
            windows(ST - 1)

            for kc in range(4, KC):
                wv_part(kc)
            for u in range(3):
                w_part(raw[:, u, :], d_raw3[u], 16, w4[:, u, 0, :], w2_used, KC)
            routed(3)
            routed_split(3)

            act.preload_act_table(ACT.Exp)

            def exponentials(h):
                after(act, p_T, h * ST)
                for c, i in enumerate(TILE_ORDER):
                    if c % 2 == 0:
                        act.wait_ge(s_nmax, 2 * h + c // 2 + 1)
                    nc.scalar.activation(prob(i), score_ps_of(i), ACT.Exp, bias=nmx[:, c:c + 1],
                                         scale=SCALE, accum_out=lsum[:, c:c + 1]).then_inc(s_exp, 1)

            def qk_weights(slot, landed, free, used):
                w_part(raw[:, slot, :], d_raw3[slot], landed, w4[:, slot, 0, :], free, used)

            def key_hi(g):
                act.wait_ge(k_sum, g + 1)
                after(act, s_mm, 3 * 2 * g)
                nc.scalar.activation(k_hl[:, 0, :], k_rope, ACT.Copy).then_inc(k_hi, 1)

            def query_hi(h):
                act.wait_ge(q_sum, h + 1)
                after(act, s_mm, 3 * h)
                nc.scalar.activation(q_hl[:, 0, :], q_rope, ACT.Copy).then_inc(q_hi, 1)

            def value_hi(g):
                after(act, pv_mm, g * 2 * ST)
                nc.scalar.activation(v_hl[:, 0, :, :], V[:, :, bass.ds(g * HD, HD)], ACT.Copy).then_inc(v_hi, 1)

            def prob_hi(h, j):
                act.wait_ge(p_T, h * ST + j + 1)
                after(act, pv_mm, h * ST)
                nc.scalar.activation(pT[:, j, 0, j * P:], psum[:, 4 + j % 2, j * P:], ACT.Copy).then_inc(p_hi, 1)

            def rest_part(n, s, first=None):
                k = n - W_O
                act.wait_ge(d_raw[s % 2], 8 * (k - s % 2) + 16)
                if first is None:
                    act.wait_ge(w_used, k - 3)
                else:
                    act.wait_ge(q_mm, first)
                nc.scalar.activation(w4[:, s, 0, :], raw[:, s % 2, :], ACT.Copy).then_inc(w_hi, 1)

            def attn_part(h, slot):
                act.wait_ge(o_sb, h + 1)
                if h >= 8:
                    act.wait_ge(w_used, h - 7)
                nc.scalar.activation(attn_hl[:, slot, 0, :], attn[:, h, :], ACT.Copy).then_inc(a_hi, 1)

            def half(g, side, before=None, behind=None, key=True, score=True, value=True):
                h = g * 2 + side
                prob_hi(h, 0)
                prob_hi(h, 1)
                if side == 1 and key:
                    key_hi(g + 1)
                if score:
                    query_hi(h + 1)
                prob_hi(h, 2)
                prob_hi(h, 3)
                if before:
                    before(g)
                if score:
                    exponentials(h + 1)
                act.wait_ge(pv_mm, (h + 1) * ST)
                nc.scalar.activation(row(attn, h), bank(6), ACT.Copy).then_inc(o_sb, 1)
                if side == 1 and value:
                    value_hi(g + 1)
                if behind:
                    behind(g)

            def weights_k(g):
                qk_weights(2, 16 * g + 32, k_mm, g + 2)

            def weights_qb(g):
                qk_weights(0, 16 * g + 48, q_mm, 2 * g + 2)

            def weights_qa(g):
                qk_weights(1, 16 * g + 48, q_mm, 2 * g + 3)

            act.wait_ge(wv_used, KC)
            qk_weights(0, 32, k_mm, 1)
            key_hi(0)
            query_hi(0)
            act.wait_ge(v_sb, ST)
            value_hi(0)
            exponentials(0)
            qk_weights(1, 32, q_mm, 1)
            half(0, 0, weights_k, weights_qb)
            half(0, 1, None, weights_qa)
            with act.Fori(1, KV_HEADS - 2) as g:
                half(g, 0, weights_k, weights_qb)
                half(g, 1, None, weights_qa)

            def first_wo(g):
                rest_part(W_O, 0, first=HEADS - 2)
                attn_part(0, 0)

            def second_wo(g):
                rest_part(W_O + 1, 1, first=HEADS - 1)

            def second_attn(g):
                attn_part(1, 1)

            def last_two(g):
                for h in (2, 3):
                    attn_part(h, h)
                for h in (2, 3):
                    rest_part(W_O + h, h, first=HEADS)

            half(KV_HEADS - 2, 0, weights_k, first_wo)
            half(KV_HEADS - 2, 1, second_wo, second_attn)
            half(KV_HEADS - 1, 0, last_two)
            half(KV_HEADS - 1, 1, key=False, score=False, value=False)

            for h in range(4, HEADS):
                rest_part(W_O + h, h % 4)
                attn_part(h, h % 8)
            act.preload_act_table(ACT.Sigmoid)
            nc.scalar.activation(gate, sels, ACT.Sigmoid).then_inc(g_sig, 1)
            act.preload_act_table(ACT.Sqrt)

            def squares(i):
                act.wait_ge(x1_sb, i + 1)
                after(act, n_sq, i)
                nc.scalar.activation(junk[:, 0:D], x1[:, i, :], ACT.Square, accum_out=ssq[:, i:i + 1]).then_inc(n_sq, 1)

            def root(i):
                act.wait_ge(n_ms, i + 1)
                nc.scalar.activation(rt[:, i:i + 1], ms[:, i:i + 1], ACT.Sqrt).then_inc(n_rt, 1)

            def norm_hi(i):
                act.wait_ge(n_full, i + 1)
                nc.scalar.activation(hT[:, :, 0, i * P:(i + 1) * P], h2full, ACT.Copy).then_inc(n_hi, 1)

            squares(0)
            root(0)
            squares(1)
            root(1)
            norm_hi(0)
            squares(2)
            rest_part(W_GU, 0)
            root(2)
            norm_hi(1)
            rest_part(W_GU + 1, 1)
            squares(3)
            root(3)
            rest_part(W_GU + 2, 2)
            norm_hi(2)
            rest_part(W_GU + 3, 3)
            norm_hi(3)

            act.preload_act_table(ACT.Silu)

            def ffn(f, odd):
                act.wait_ge(w_used, HEADS + f * 2 + 1)
                after(act, m_sb, f - 1)
                nc.scalar.activation(silu_g[:, odd, :], bank(2 * odd), ACT.Silu).then_inc(g_silu, 1)
                rest_part(W_GU + f * 2 + 4, 2 * odd)
                rest_part(W_GU + f * 2 + 5, 2 * odd + 1)

            ffn(0, 0)
            ffn(1, 1)
            act.wait_ge(g_base, ST)
            act.dma_start(base_rows.rearrange("(i p) n -> p i n", p=P), xsel).then_inc(d_base, 16)
            with act.Fori(1, FT // 2 - 1) as k:
                ffn(k * 2, 0)
                ffn(k * 2 + 1, 1)

            def m_part(f, s):
                if not isinstance(f, int):
                    act.wait_ge(w_used, W_DOWN - W_O + f - 3)
                nc.scalar.activation(m_hl[:, s, 0, :], row(m, f), ACT.Copy).then_inc(m_hi, 1)

            for f in range(4):
                m_part(f, f)
            ffn(FT - 2, 0)
            ffn(FT - 1, 1)

            def down_parts(k):
                for s in range(4):
                    rest_part(W_DOWN + k * 4 + s, s)
                    m_part(k * 4 + s, s)

            with act.Fori(1, 3) as k:
                down_parts(k)
            act.wait_ge(m_lo, 8)
            act.wait_ge(m_hi, 8)
            for i in range(ST):
                act.dma_start(base[:, i, :], base_rows[i * P:(i + 1) * P, :]).then_inc(d_baseld[i], 16)
            with act.Fori(3, FT // 4) as k:
                down_parts(k)

        @block.gpsimd
        def _(pool):
            def w_part(n, src, dst_slot):
                pool.wait_ge(w_hi, n + 1)
                nc.gpsimd.tensor_tensor(dst_slot[:, 1, :], src, as_f32(dst_slot[:, 0, :]),
                                        ALU.subtract).then_inc(w_lo, 1)

            def x_plus_y(b, j):
                t = b * TT + j
                pool.wait_ge(y_relu, t + 1)
                pool.wait_ge(d_x[j], 16 * b + 16)
                nc.gpsimd.tensor_tensor(xrow[:, j, :], xrow[:, j, :], y[:, j % 2, :], ALU.add).then_inc(out_row, 1)

            def gather_angles(k):
                pool.wait_ge(idx_u, 3 * (k + 1))
                after(pool, ang_T, k)
                pool.indirect_dma_start(ang, None, angles,
                                        bass.IndirectOffsetOnAxis(ap=idx[:, ST + k:ST + k + 1], axis=0)).then_inc(d_ang[k], 16)

            def gather(k):
                pool.wait_ge(idx_u, 3 * (k + 1))
                for s in range(2):
                    pool.wait_ge(d_y[s], 16 * TT * (k + 1))
                after(pool, h_norm, k - 1)
                after(pool, h_sel, k - 1)
                pool.indirect_dma_start(ysel[:, k % 2, :], None, y_of[k],
                                        bass.IndirectOffsetOnAxis(ap=idx[:, 2 * ST + k:2 * ST + k + 1], axis=0)).then_inc(d_ysel[k], 16)

            for n in range(KC):
                w_part(n, raw_w2[n], w8[:, n])
            with pool.Fori(0, ST - 1) as i:
                for p in range(2):
                    for j in range(TT):
                        x_plus_y(i * 2 + p, j)
            b = BATCH - 2
            for p in range(2):
                for j in range(TT):
                    if p == 1 and j == TT - 1:
                        for kc in range(3):
                            w_part(W_V + kc, raw_wv[kc], w8[:, kc])
                    x_plus_y(b + p, j)
                    if p == 0 and j == 0:
                        gather_angles(0)
                        gather(0)
                        gather(1)
                    if p == 1 and j == 0:
                        gather(2)
                    if p == 1 and j in (1, 2):
                        gather_angles(j)
            for kc in range(3, KC):
                w_part(W_V + kc, raw_wv[kc % 5], w8[:, kc])
            w_part(W_QK, raw[:, 0, :], w4[:, 0])
            gather(3)
            gather_angles(3)
            for u in (1, 2):
                w_part(W_QK + u, raw[:, u, :], w4[:, u])

            def key_sum(g):
                pool.wait_ge(rope_s, 6 * g + 2)
                nc.gpsimd.tensor_tensor(k_rope, k_rope, sin_term, ALU.add).then_inc(k_sum, 1)

            def key_lo(g):
                pool.wait_ge(k_hi, g + 1)
                nc.gpsimd.tensor_tensor(k_hl[:, 1, :], k_rope, as_f32(k_hl[:, 0, :]), ALU.subtract).then_inc(k_lo, 1)

            def value_lo(g):
                pool.wait_ge(v_hi, g + 1)
                nc.gpsimd.tensor_tensor(v_hl[:, 1, :, :], V[:, :, bass.ds(g * HD, HD)], as_f32(v_hl[:, 0, :, :]),
                                        ALU.subtract).then_inc(v_lo, 1)

            def group(g, last=False):
                w_part(W_QK + 3 * g + 5, raw[:, 2, :], w4[:, 2])
                key_sum(g + 1)
                w_part(W_O if last else W_QK + 3 * g + 6, raw[:, 0, :], w4[:, 0])
                key_lo(g + 1)
                value_lo(g + 1)
                w_part(W_O + 1 if last else W_QK + 3 * g + 7, raw[:, 1, :], w4[:, 1])

            key_sum(0)
            w_part(W_QK + 3, raw[:, 0, :], w4[:, 0])
            key_lo(0)
            value_lo(0)
            w_part(W_QK + 4, raw[:, 1, :], w4[:, 1])
            group(0)
            with pool.Fori(1, KV_HEADS - 2) as g:
                group(g)
            group(KV_HEADS - 2, last=True)

            def gather_rows(dst, src, c, landed):
                pool.indirect_dma_start(dst, None, src,
                                        bass.IndirectOffsetOnAxis(ap=idx[:, c:c + 1], axis=0)).then_inc(landed, 16)

            for s in range(2, 4):
                w_part(W_O + s, raw[:, s % 2, :], w4[:, s])
            pool.wait_ge(p_T, HEADS * ST)
            for k in range(2):
                gather_rows(ysel4[k], y_of[k], 2 * ST + k, d_ysel[k])
            with pool.Fori(1, HEADS // 4) as k:
                for s in range(4):
                    w_part(W_O + k * 4 + s, raw[:, s % 2, :], w4[:, s])
            pool.wait_ge(a_lo, HEADS)
            for k in (2, 3):
                gather_rows(ysel4[k], y_of[k], 2 * ST + k, d_ysel[k])
            for k in range(ST):
                gather_rows(xsel[:, k, :], x_rows, k, d_xsel[k])
            with pool.Fori(0, (W_END - W_GU) // 4) as k:
                for s in range(4):
                    w_part(W_GU + k * 4 + s, raw[:, s % 2, :], w4[:, s])
            for j in range(TT):
                pool.wait_ge(d_out[j], 16 * BATCH)
            for i in range(ST):
                pool.wait_ge(fin, i + 1)
                pool.indirect_dma_start(out, bass.IndirectOffsetOnAxis(ap=idx[:, i:i + 1], axis=0),
                                        base[:, i, :], None).then_inc(d_fin, 16)

        @block.vector
        def _(dve):
            def modulation(mo):
                dve.wait_ge(qe_mm, mo + 1)
                nc.vector.tensor_scalar(qe[:, mo, :], psum[:, 6 + mo % 2, 0:BATCH], col[:, C_B3 + mo:C_B3 + mo + 1], 0.0,
                                        ALU.add, ALU.max).then_inc(qe_b, 1)
                dve.wait_ge(qe_b, mo + 1)
                nc.vector.tensor_scalar(qe[:, mo, :], qe[:, mo, :], float(SEQ), None, ALU.mult).then_inc(qe_done, 1)
                dve.wait_ge(qe_done, mo + 1)

            def x_chunks(b, p, kcs):
                for kc in kcs:
                    c = b * KC + kc
                    dve.wait_ge(x_sum, c + 1)
                    nc.vector.tensor_scalar(xT[:, kc % 4, :], xT[:, kc % 4, :], vs[:, p, kc:kc + 1],
                                            qe[:, kc, bass.ds(b, 1)], ALU.add, ALU.mult).then_inc(x_mod, 1)
                for kc in kcs:
                    c = b * KC + kc
                    dve.wait_ge(x_hi, c + 1)
                    nc.vector.tensor_tensor(xx[:, p, kc, 1, :], xT[:, kc % 4, :], as_f32(xx[:, p, kc, 0, :]),
                                            ALU.subtract).then_inc(x_lo, 1)

            def y_tile(i, p, j, final=False):
                b = i * 2 + p
                t, half = b * TT + j, 2 * b + j // 2
                if final:
                    dve.wait_ge(w2_used, KC)
                else:
                    dve.wait_ge(y_mm, t + 1)
                after(dve, d_y[j % 2], 16 * half)
                after(dve, y_score, t - 1)
                after(dve, out_row, t - 1)
                banks = 2 * j if isinstance(t, int) and t < TT else 2 * (j % 2)
                nc.vector.tensor_tensor(y[:, j % 2, :], pair(banks), bias_row, ALU.add).then_inc(y_biased, 1)
                dve.wait_ge(y_relu, t + 1)
                after(dve, y_score, t)
                if p == 0 and j == 0:
                    after(dve, score_T, i)
                nc.vector.scalar_tensor_tensor(junk[:, 0:D], y[:, j % 2, :], 1.0, wr_row, ALU.mult, ALU.mult,
                                               accum_out=sc[:, j, p:p + 1]).then_inc(y_score, 1)

            score_ps = psum[0:2, 4, :]
            def top_rounds(k, rounds):
                for r in rounds:
                    src = score_ps if r == 0 else (rank_a, rank_b)[(r - 1) % 2][0:2, :]
                    dst = (rank_a, rank_b)[r % 2][0:2, :]
                    if r == 0:
                        after(dve, top_cut, k * 8)
                        apart(dve, score_T, k + 1, dve_passed)
                    else:
                        apart(dve, top_cut, k * 8 + r, dve_passed)
                    nc.vector.max(top8[0:2, :], src).then_inc(top_max, 1)
                    apart(dve, top_max, k * 8 + r + 1, dve_passed)
                    nc.vector.match_replace(dst, top8[0:2, :], src, LOWEST).then_inc(top_cut, 1)

            def top_ranks(k):
                dve.wait_ge(top_cut, k * 8 + 8)
                nc.vector.tensor_tensor(rank_a[0:2, :], rank_b[0:2, :], score_ps, ALU.not_equal).then_inc(top_mask, 1)
                dve.wait_ge(top_mask, k + 1)
                nc.vector.tensor_tensor_scan(rank_b[0:2, :], rank_a[0:2, :], rank_a[0:2, :], 0.0,
                                             ALU.add, ALU.max).then_inc(top_rank, 1)

            def top_index(k, scored):
                dve.wait_ge(rank_bc, k + 1)
                dve.wait_ge(y_score, scored)
                nc.vector.tensor_scalar(junk[:, 0:SEQ], bank(5), consts[:, Z_RANK:Z_RANK + 1], 0.0, ALU.is_le,
                                        ALU.add, accum_out=idxf[:, bass.ds(k, 1)]).then_inc(idx_f, 1)
                dve.wait_ge(idx_f, k + 1)
                nc.vector.tensor_scalar(idx[:, bass.ds(k, 1)], idxf[:, bass.ds(k, 1)],
                                        consts[:, bass.ds(Z_BASE + k, 1)], None, ALU.add).then_inc(idx_u, 1)
                nc.vector.tensor_copy(idx[:, bass.ds(ST + k, 1)], idxf[:, bass.ds(k, 1)]).then_inc(idx_u, 1)
                nc.vector.tensor_scalar(idx[:, bass.ds(2 * ST + k, 1)], idxf[:, bass.ds(k, 1)],
                                        consts[:, bass.ds(Z_YBASE + k, 1)], None, ALU.add).then_inc(idx_u, 1)

            def inverse_root(k, sq_sem, ms_sem, rt_sem, chain, done):
                a, r, q = ms[:, k:k + 1], rs[:, k:k + 1], na[:, k:k + 1]
                dve.wait_ge(sq_sem, k + 1)
                nc.vector.tensor_scalar(a, ssq[:, k:k + 1], 1.0 / D, EPS, ALU.mult, ALU.add).then_inc(ms_sem, 1)
                dve.wait_ge(rt_sem, k + 1)
                nc.vector.reciprocal(r, rt[:, k:k + 1]).then_inc(chain, 1)
                dve.wait_ge(chain, 3 * k + 1)
                nc.vector.scalar_tensor_tensor(q, r, a, r, ALU.mult, ALU.mult).then_inc(chain, 1)
                dve.wait_ge(chain, 3 * k + 2)
                nc.vector.tensor_scalar(q, q, -0.5, 1.5, ALU.mult, ALU.add).then_inc(chain, 1)
                dve.wait_ge(chain, 3 * k + 3)
                nc.vector.tensor_tensor(r, r, q, ALU.mult).then_inc(done, 1)

            def routed(k, scored):
                inverse_root(k, h_sq, h_ms, h_rt, h_chain, h_rs)
                dve.wait_ge(h_rs, k + 1)
                dve.wait_ge(d_ysel[k], 16)
                nc.vector.tensor_scalar(hs, ysel[:, k % 2, :], rs[:, k:k + 1], None, ALU.mult).then_inc(h_norm, 1)
                dve.wait_ge(y_score, scored)
                after(dve, h_sel, k)
                nc.vector.scalar_tensor_tensor(junk[:, 0:D], ysel[:, k % 2, :], 1.0, wr_row, ALU.mult, ALU.mult,
                                               accum_out=sels[:, k:k + 1]).then_inc(h_sel, 1)

            def routed_split(k):
                dve.wait_ge(h_T, k + 1)
                after(dve, h_lo, k)
                ln = col[:, C_LN1:C_LN1 + KC].rearrange("p (k a) -> p k a", a=1).broadcast_to([P, KC, P])
                h_ps = psum[:, 4:6, :].rearrange("p b (k n) -> p (b k) n", k=4)
                nc.vector.tensor_tensor(hfull, h_ps, ln, ALU.mult).then_inc(h_full, 1)
                dve.wait_ge(h_hi, k + 1)
                nc.vector.tensor_tensor(hT[:, :, 1, k * P:(k + 1) * P], hfull, as_f32(hT[:, :, 0, k * P:(k + 1) * P]),
                                        ALU.subtract).then_inc(h_lo, 1)

            dve.wait_ge(d_cols, 16)
            for kc in range(KC):
                modulation(kc)
                x_chunks(0, 0, (kc,))
            dve.wait_ge(d_b2, 16)
            dve.wait_ge(d_wr, 16)
            dve.wait_ge(d_consts, 16)

            def windows(i):
                first, end = isinstance(i, int) and i == 0, isinstance(i, int) and i == ST - 1
                for p in range(2):
                    b = i * 2 + p
                    for j in range(TT):
                        if not (end and p == 1):
                            x_chunks(b + 1, 1 - p, (2 * j, 2 * j + 1))
                        if not first and p == 0 and j > 0:
                            top_rounds(i - 1, ((), (0, 1, 2), (3, 4, 5), (6, 7))[j])
                        if not first and p == 0 and j == TT - 1:
                            top_ranks(i - 1)
                        y_tile(i, p, j, final=end and p == 1 and j == TT - 1)
                        if not first and p == 1 and j == 0:
                            top_index(i - 1, b * TT + 1)
                        if end and p == 1:
                            if j > 0:
                                routed_split(j - 1)
                            if j < TT - 1:
                                routed(j, b * TT + j + 1)

            windows(0)
            with dve.Fori(1, ST - 1) as i:
                windows(i)
            windows(ST - 1)

            def v_out(i, banks):
                dve.wait_ge(d_bv, 16)
                for j in range(TT):
                    dve.wait_ge(d_out[j], 16 * BATCH)
                nc.vector.tensor_tensor(V[:, i, :], pair(banks), bias_row, ALU.add).then_inc(v_sb, 1)

            top_rounds(ST - 1, range(8))
            top_ranks(ST - 1)
            top_index(ST - 1, BATCH * TT)
            dve.wait_ge(v_mm, 1)
            v_out(0, 0)
            dve.wait_ge(v_mm, 2)
            v_out(1, 2)
            routed(3, BATCH * TT)
            routed_split(3)
            dve.wait_ge(v_mm, 3)
            v_out(2, 6)

            def rope_cos(r, dst, b):
                nc.vector.scalar_tensor_tensor(dst, bank(b), col[:, bass.ds(C_BQK + r, 1)], cosT,
                                               ALU.add, ALU.mult).then_inc(rope_c, 1)

            def rope_sin(r, b, lo):
                nc.vector.scalar_tensor_tensor(sin_term[lo:lo + 64, :], psum[64 - lo:128 - lo, b, :],
                                               col[lo:lo + 64, bass.ds(C_BQKS + r, 1)], sinT[lo:lo + 64, :],
                                               ALU.add, ALU.mult).then_inc(rope_s, 1)

            def query_cos(h, r):
                dve.wait_ge(q_mm, h + 1)
                after(dve, q_lo, h)
                rope_cos(r, q_rope, 7)

            def query_sum(h, r):
                dve.wait_ge(rope_c, r + 1)
                dve.wait_ge(rope_s, 2 * r + 2)
                nc.vector.tensor_tensor(q_rope, q_rope, sin_term, ALU.add).then_inc(q_sum, 1)

            def query_lo(h):
                dve.wait_ge(q_hi, h + 1)
                nc.vector.tensor_tensor(q_hl[:, 1, :], q_rope, as_f32(q_hl[:, 0, :]), ALU.subtract).then_inc(q_lo, 1)

            def key_terms(g, r):
                dve.wait_ge(k_mm, g + 1)
                after(dve, k_lo, g)
                rope_cos(r, k_rope, 3)
                after(dve, q_sum, 2 * g)
                rope_sin(r, 3, 0)

            def prob_lo(h, j):
                dve.wait_ge(p_hi, h * ST + j + 1)
                nc.vector.tensor_tensor(pT[:, j, 1, j * P:], psum[:, 4 + j % 2, j * P:], as_f32(pT[:, j, 0, j * P:]),
                                        ALU.subtract).then_inc(p_lo, 1)

            def maxima(h):
                def largest(c):
                    if c != 1:
                        dve.wait_ge(s_mm, 3 * h + (1, 1, 2, 3)[c])
                    nc.vector.reduce_max(mx[:, c:c + 1], score_ps_of(TILE_ORDER[c]), AX).then_inc(s_max, 1)

                def negate(c, cs):
                    dve.wait_ge(s_max, h * ST + c)
                    nc.vector.tensor_scalar(nmx[:, cs], mx[:, cs], -SCALE, None, ALU.mult).then_inc(s_nmax, 1)

                after(dve, s_nmax, 2 * h)
                after(dve, s_exp, h * ST)
                largest(0)
                largest(1)
                largest(2)
                negate(2, slice(0, 2))
                largest(3)
                negate(4, slice(2, 4))

            def normalize(h):
                after(dve, s_prob, h * ST)
                for c, i in enumerate(TILE_ORDER):
                    dve.wait_ge(s_exp, h * ST + c + 1)
                    nc.vector.reciprocal(rl[:, c:c + 1], lsum[:, c:c + 1]).then_inc(s_rl, 1)
                    dve.wait_ge(s_rl, h * ST + c + 1)
                    nc.vector.tensor_scalar(prob(i), prob(i), rl[:, c:c + 1], None,
                                            ALU.mult).then_inc(s_prob, 1)

            def half(g, side, key=True, score=True, between=None):
                h = g * 2 + side
                r = 3 * g + 2 + 2 * side
                if score:
                    query_cos(h + 1, r)
                prob_lo(h, 0)
                if score:
                    if side == 1 and key:
                        dve.wait_ge(k_sum, g + 2)
                    rope_sin(r, 7, 0)
                prob_lo(h, 1)
                if score:
                    rope_sin(r, 7, 64)
                    query_sum(h + 1, r)
                prob_lo(h, 2)
                if score:
                    query_lo(h + 1)
                prob_lo(h, 3)
                if between:
                    between()
                if side == 0 and key:
                    key_terms(g + 1, r + 1)
                if score:
                    maxima(h + 1)
                    normalize(h + 1)
                if side == 0 and key:
                    rope_sin(r + 1, 3, 64)

            dve.wait_ge(ang_sb, ST)
            key_terms(0, 0)
            rope_sin(0, 3, 64)
            dve.wait_ge(wv_used, KC)
            v_out(3, 0)
            query_cos(0, 1)
            dve.wait_ge(k_sum, 1)
            rope_sin(1, 7, 0)
            rope_sin(1, 7, 64)
            query_sum(0, 1)
            query_lo(0)
            maxima(0)
            normalize(0)
            half(0, 0)
            half(0, 1)
            with dve.Fori(1, KV_HEADS - 2) as g:
                half(g, 0)
                half(g, 1)

            def attn_part(h, slot):
                dve.wait_ge(a_hi, h + 1)
                nc.vector.tensor_tensor(attn_hl[:, slot, 1, :], attn[:, h, :], as_f32(attn_hl[:, slot, 0, :]),
                                        ALU.subtract).then_inc(a_lo, 1)

            def attn_parts(heads):
                for h in heads:
                    attn_part(h, h)

            half(KV_HEADS - 2, 0)
            half(KV_HEADS - 2, 1, between=lambda: attn_parts((0,)))
            attn_part(1, 1)
            half(KV_HEADS - 1, 0, key=False, between=lambda: attn_parts((2, 3)))
            half(KV_HEADS - 1, 1, score=False)
            for h in range(4, HEADS):
                attn_part(h, h % 8)
            dve.wait_ge(g_sig, 1)
            nc.vector.tensor_scalar(ungate, gate, -1.0, 1.0, ALU.mult, ALU.add).then_inc(g_un, 1)

            def add_rows(i):
                if i < ST - 1:
                    dve.wait_ge(wo_mm, i + 1)
                else:
                    dve.wait_ge(w_used, HEADS)
                dve.wait_ge(d_ysel[i], 32)
                nc.vector.tensor_tensor(x1[:, i, :], pair(2 * i), ysel4[i], ALU.add).then_inc(x1_sb, 1)

            def norm(i):
                inverse_root(i, n_sq, n_ms, n_rt, n_chain, n_rs)
                dve.wait_ge(n_rs, i + 1)
                after(dve, n_T, i)
                nc.vector.tensor_scalar(h2s, x1[:, i, :], rs[:, i:i + 1], None, ALU.mult).then_inc(n_norm, 1)

            def norm_full(i):
                dve.wait_ge(n_T, i + 1)
                after(dve, n_lo, i)
                ln = col[:, C_LN2:C_LN2 + KC].rearrange("p (k a) -> p k a", a=1).broadcast_to([P, KC, P])
                n_ps = psum[:, 2 * i:2 * i + 2, :].rearrange("p b (k n) -> p (b k) n", k=4)
                nc.vector.tensor_tensor(h2full, n_ps, ln, ALU.mult).then_inc(n_full, 1)

            def norm_lo(i):
                dve.wait_ge(n_hi, i + 1)
                nc.vector.tensor_tensor(hT[:, :, 1, i * P:(i + 1) * P], h2full, as_f32(hT[:, :, 0, i * P:(i + 1) * P]),
                                        ALU.subtract).then_inc(n_lo, 1)

            for i in range(ST):
                if i > 1:
                    norm_lo(i - 2)
                add_rows(i)
                if i > 0:
                    norm_full(i - 1)
                norm(i)
            norm_lo(ST - 2)
            norm_full(ST - 1)
            norm_lo(ST - 1)
            dve.wait_ge(g_un, 1)
            for i in range(ST):
                dve.wait_ge(d_xsel[i], 16)
                nc.vector.scalar_tensor_tensor(xsel[:, i, :], x1[:, i, :], gate[:, i:i + 1], xsel[:, i, :],
                                               ALU.mult, ALU.add).then_inc(g_mix, 1)
                dve.wait_ge(g_mix, i + 1)
                nc.vector.scalar_tensor_tensor(xsel[:, i, :], ysel4[i], ungate[:, i:i + 1], xsel[:, i, :],
                                               ALU.mult, ALU.add).then_inc(g_base, 1)
                dve.wait_ge(g_base, i + 1)

            def ffn(f, odd):
                dve.wait_ge(w_used, HEADS + f * 2 + 2)
                dve.wait_ge(g_silu, f + 1)
                nc.vector.tensor_tensor(m[:, bass.ds(f, 1), :].rearrange("p a n -> p (a n)"), silu_g[:, odd, :],
                                        bank(2 * odd + 1), ALU.mult).then_inc(m_sb, 1)

            for f in range(12):
                ffn(f, f % 2)
            dve.wait_ge(d_base, 16)
            with dve.Fori(6, FT // 2 - 1) as k:
                ffn(k * 2, 0)
                ffn(k * 2 + 1, 1)

            def m_part(f, s):
                dve.wait_ge(m_hi, f + 1)
                nc.vector.tensor_tensor(m_hl[:, s, 1, :], row(m, f), as_f32(m_hl[:, s, 0, :]), ALU.subtract).then_inc(m_lo, 1)

            for f in range(4):
                m_part(f, f)
            ffn(FT - 2, 0)
            ffn(FT - 1, 1)
            with dve.Fori(1, FT // 4) as k:
                for s in range(4):
                    m_part(k * 4 + s, s)
            for i in range(ST):
                if i < ST - 1:
                    dve.wait_ge(dn_mm, i + 1)
                else:
                    dve.wait_ge(w_used, W_END - W_O)
                dve.wait_ge(d_baseld[i], 16)
                nc.vector.scalar_tensor_tensor(base[:, i, :], pair(2 * i), gate[:, i:i + 1], base[:, i, :],
                                               ALU.mult, ALU.add).then_inc(fin, 1)


_OUTS = [((BATCH, SEQ, D), "float32")]


def kernel(**inputs):
    import concourse.bacc as _bacc
    from concourse.bass_utils import run_bass_kernel_spmd as _run

    a = {k: np.asarray(v) for k, v in inputs.items()}
    x = a["x"]

    def columns(v):
        return v.reshape(-1, P).T

    x_t = np.ascontiguousarray(x.reshape(BATCH, SEQ, KC, P).transpose(0, 2, 3, 1)).reshape(BATCH * KC, P, SEQ)
    heads = lambda w: w.reshape(KC, P, -1, P).transpose(2, 1, 0, 3).reshape(-1, P, D)
    wq, wk = heads(a["L0_ffn_wq"]), heads(a["L0_ffn_wk"])
    qk = [wk[0]] + [t for g in range(KV_HEADS) for t in (wq[2 * g], *wk[g + 1:g + 2], wq[2 * g + 1])]
    wg, wu = heads(a["L0_ffn_w_gate"]), heads(a["L0_ffn_w_up"])
    gu = [t for f in range(FT) for t in (wg[f], wu[f])]
    rows_of = lambda w: w.reshape(-1, P, D)
    wstream = np.concatenate([rows_of(a["L0_cond_W2"]), rows_of(a["L0_ffn_wv"]), np.stack(qk),
                              rows_of(a["L0_ffn_wo"]), np.stack(gu), rows_of(a["L0_ffn_w_down"])])
    bq, bk = a["L0_ffn_bq"].reshape(HEADS, HD), a["L0_ffn_bk"].reshape(KV_HEADS, HD)
    bqk = np.stack([bk[0], bq[0]] + [t for g in range(KV_HEADS) for t in (bq[2 * g + 1], *bk[g + 1:g + 2], *bq[2 * g + 2:2 * g + 3])])
    swapped = np.concatenate([bqk[:, HD // 2:], bqk[:, :HD // 2]], axis=1)
    cols = np.concatenate([columns(a["L0_cond_b3"]), columns(a["L0_ffn_ln1_w"]), columns(a["L0_ffn_ln2_w"]),
                           bqk.T, swapped.T], axis=1)
    rows = np.stack([a["L0_cond_b2"], a["L0_ffn_w_router"], a["L0_ffn_bv"]])

    part = np.arange(P)
    shape_consts = np.zeros((P, N_CONSTS), np.float32)
    shape_consts[:, Z_IDENT:Z_IDENT + P] = np.eye(P)
    shape_consts[:, Z_MASK:Z_MASK + P] = np.where(part[None, :] > part[:, None], LOWEST, 0.0)
    for half in range(2):
        shape_consts[half, Z_PAIR + half * PICK:Z_PAIR + (half + 1) * PICK] = 1.0
    shape_consts[:, Z_RANK] = part % PICK
    for k in range(ST):
        shape_consts[:, Z_BASE + k] = (2 * k + part // PICK) * SEQ
        shape_consts[:, Z_YBASE + k] = (2 * (k == 2) + part // PICK) * SEQ
    inv_freq = (np.float32(1.0) / np.float32(10000.0) ** (np.arange(0, HD, 2, dtype=np.float32) / np.float32(HD)))
    phase = (np.arange(SEQ, dtype=np.float32)[:, None] * inv_freq.astype(np.float32)).astype(np.float32)
    cos, sin = np.cos(phase), np.sin(phase)
    angles = np.concatenate([cos, cos, -sin, sin], axis=1).astype(np.float32)

    arrays = {
        "x_t": x_t, "x_rows": x.reshape(BATCH * SEQ, D),
        "cond_t": a["cond_1024"].T.reshape(COND // P, P, BATCH).transpose(1, 0, 2),
        "w3": a["L0_cond_W3"].reshape(COND // P, P, KC, P).transpose(2, 1, 0, 3), "wstream": wstream, "cols": cols, "rows": rows,
        "shape_consts": shape_consts, "angles": angles,
    }
    arrays = {k: np.ascontiguousarray(v) for k, v in arrays.items()}
    nc = _bacc.Bacc("TRN2", target_bir_lowering=False, num_devices=1)
    args = {k: nc.dram_tensor(k, v.shape, mybir.dt.from_np(v.dtype), kind="ExternalInput").ap()
            for k, v in arrays.items()}
    out = nc.dram_tensor("out", (BATCH * SEQ, D), mybir.dt.float32, kind="ExternalOutput").ap()
    build(nc, out=out, **args)
    r = _run(nc, [arrays], core_ids=[0])
    return r.results[0]["out"].reshape(BATCH, SEQ, D)
```
